# Optimizing a Trainium2 kernel written in Bass

```python
import numpy as np
import jax
import jax.numpy as jnp

def _softmax(x, axis=-1):
    return jax.nn.softmax(x, axis=axis)

def _gelu(x):
    return jax.nn.gelu(x, approximate=True)

def _silu(x):
    return jax.nn.silu(x)

def _sigmoid(x):
    return jax.nn.sigmoid(x)

def _layernorm(x, axis=-1, eps=1e-05):
    m = jnp.mean(x, axis=axis, keepdims=True)
    v = jnp.var(x, axis=axis, keepdims=True)
    return (x - m) / jnp.sqrt(v + eps)

def _scatter_add(tgt, idx, src, axis=0):
    return tgt.at[idx].add(src)

def _segment_sum(src, seg, n):
    return jax.ops.segment_sum(src, seg, n)
kernel_name = 'mk_adaln_d2_jaxref_r8_707311'

def setup_inputs(seed: int=0):
    np.random.seed(seed)
    _w = jnp.asarray

    def _L0_attn_setup():
        import jax, jax.numpy as jnp
        import numpy as np
        B, N, D = (8, 128, 512)
        H = 8
        HEAD_DIM = D // H
        E = HEAD_DIM // H
        key = jax.random.key(seed)
        ks = jax.random.split(key, 7)
        s = 0.02
        return {'x': jax.random.normal(ks[0], (B, N, D), dtype=jnp.float32), 'Wqk_w': jax.random.normal(ks[1], (2 * HEAD_DIM, D), dtype=jnp.float32) * s, 'Wqk_b': jnp.zeros((2 * HEAD_DIM,), dtype=jnp.float32), 'Wv_w': jax.random.normal(ks[2], (HEAD_DIM, D), dtype=jnp.float32) * s, 'Wv_b': jnp.zeros((HEAD_DIM,), dtype=jnp.float32), 'Wo_w': jax.random.normal(ks[3], (D, HEAD_DIM), dtype=jnp.float32) * s, 'Wo_b': jnp.zeros((D,), dtype=jnp.float32)}
    _L0_attn_in = _L0_attn_setup()

    def _L0_ffn_setup():
        import jax, jax.numpy as jnp
        import numpy as np
        SCALING = 32.0 / 16.0
        key = jax.random.key(seed)
        ks = jax.random.split(key, 7)
        B, T, D, O, R, E = (4, 256, 512, 512, 16, 8)
        x = jax.random.normal(ks[0], (B, T, D), dtype=jnp.float32)
        base_W = jax.random.normal(ks[1], (O, D), dtype=jnp.float32) * D ** (-0.5)
        base_b = jax.random.normal(ks[2], (O,), dtype=jnp.float32) * 0.01
        router_W = jax.random.normal(ks[3], (2 * E - 1, D), dtype=jnp.float32) * D ** (-0.5)
        router_b = jax.random.normal(ks[4], (2 * E - 1,), dtype=jnp.float32) * 0.01
        A = jax.random.normal(ks[5], (E, R, D), dtype=jnp.float32) * D ** (-0.5)
        Bm = jax.random.normal(ks[6], (E, O, R), dtype=jnp.float32) * R ** (-0.5)
        assigned_idx = 0
        others = [i for i in range(E) if i != assigned_idx]
        expert_map = jnp.array([assigned_idx] * E + others, dtype=jnp.int32)
        return {'x': x, 'base_W': base_W, 'base_b': base_b, 'router_W': router_W, 'router_b': router_b, 'A': A, 'B': Bm, 'expert_map': expert_map}
    _L0_ffn_in = _L0_ffn_setup()
    _L0_c = _w((lambda *s: np.random.randn(*s).astype(np.float32) * 0.05)(4, 512))
    _L0_wmod = _w((lambda *s: np.random.randn(*s).astype(np.float32) * 0.05)(512, 6 * 512) * 512 ** (-0.5))

    def _L1_attn_setup():
        import jax, jax.numpy as jnp
        import numpy as np
        B, S, D = (2, 256, 512)
        NH, NKV = (32, 8)
        HD = D // NH
        NREP = NH // NKV
        SCALE = HD ** (-0.5)
        key = jax.random.key(seed)
        kx, kq, kk, kv, ko = jax.random.split(key, 5)
        s = 0.02
        return {'x': jax.random.normal(kx, (B, S, D), dtype=jnp.float32), 'wq': jax.random.normal(kq, (D, NH * HD), dtype=jnp.float32) * s, 'wk': jax.random.normal(kk, (D, NKV * HD), dtype=jnp.float32) * s, 'wv': jax.random.normal(kv, (D, NKV * HD), dtype=jnp.float32) * s, 'wo': jax.random.normal(ko, (NH * HD, D), dtype=jnp.float32) * s}
    _L1_attn_in = _L1_attn_setup()

    def _L1_ffn_setup():
        import jax, jax.numpy as jnp
        import numpy as np
        import math
        E, DK, R = (8, 32, 16)
        SCALING = 16.0 / 16.0
        key = jax.random.key(seed)
        ks = jax.random.split(key, 7)
        Bt, S, Din, Dout = (4, 256, 512, 512)
        x = jax.random.normal(ks[0], (Bt, S, Din), jnp.float32)
        W = jax.random.normal(ks[1], (Dout, Din), jnp.float32) * 0.02
        b = jnp.zeros((Dout,), jnp.float32)
        Wq = jax.random.normal(ks[2], (E * DK, Din), jnp.float32) * 0.02
        Wk = jax.random.normal(ks[3], (E * DK, Din), jnp.float32) * 0.02
        A = jax.random.normal(ks[4], (E, R, Din), jnp.float32) * 0.02
        Bm = jax.random.normal(ks[5], (E, Dout, R), jnp.float32) * 0.02
        return {'x': x, 'W': W, 'b': b, 'Wq': Wq, 'Wk': Wk, 'A': A, 'Bm': Bm}
    _L1_ffn_in = _L1_ffn_setup()
    _L1_c = _w((lambda *s: np.random.randn(*s).astype(np.float32) * 0.05)(4, 512))
    _L1_wmod = _w((lambda *s: np.random.randn(*s).astype(np.float32) * 0.05)(512, 6 * 512) * 512 ** (-0.5))
    _d = {'L0_attn_x': _L0_attn_in['x'], 'L0_attn_Wqk_w': _L0_attn_in['Wqk_w'], 'L0_attn_Wqk_b': _L0_attn_in['Wqk_b'], 'L0_attn_Wv_w': _L0_attn_in['Wv_w'], 'L0_attn_Wv_b': _L0_attn_in['Wv_b'], 'L0_attn_Wo_w': _L0_attn_in['Wo_w'], 'L0_attn_Wo_b': _L0_attn_in['Wo_b'], 'L0_ffn_base_W': _L0_ffn_in['base_W'], 'L0_ffn_base_b': _L0_ffn_in['base_b'], 'L0_ffn_router_W': _L0_ffn_in['router_W'], 'L0_ffn_router_b': _L0_ffn_in['router_b'], 'L0_ffn_A': _L0_ffn_in['A'], 'L0_ffn_B': _L0_ffn_in['B'], 'L0_ffn_expert_map': _L0_ffn_in['expert_map'], 'L0_c': _L0_c, 'L0_wmod': _L0_wmod, 'L1_attn_wq': _L1_attn_in['wq'], 'L1_attn_wk': _L1_attn_in['wk'], 'L1_attn_wv': _L1_attn_in['wv'], 'L1_attn_wo': _L1_attn_in['wo'], 'L1_ffn_W': _L1_ffn_in['W'], 'L1_ffn_b': _L1_ffn_in['b'], 'L1_ffn_Wq': _L1_ffn_in['Wq'], 'L1_ffn_Wk': _L1_ffn_in['Wk'], 'L1_ffn_A': _L1_ffn_in['A'], 'L1_ffn_Bm': _L1_ffn_in['Bm'], 'L1_c': _L1_c, 'L1_wmod': _L1_wmod}
    _x0 = _d['L0_attn_x']
    _d['L0_attn_x'] = jax.random.normal(jax.random.fold_in(jax.random.key(seed), 1), (4, 512, 512), dtype=_x0.dtype)
    del _x0
    return _d

def reference(L0_attn_x, L0_attn_Wqk_w, L0_attn_Wqk_b, L0_attn_Wv_w, L0_attn_Wv_b, L0_attn_Wo_w, L0_attn_Wo_b, L0_ffn_base_W, L0_ffn_base_b, L0_ffn_router_W, L0_ffn_router_b, L0_ffn_A, L0_ffn_B, L0_ffn_expert_map, L0_c, L0_wmod, L1_attn_wq, L1_attn_wk, L1_attn_wv, L1_attn_wo, L1_ffn_W, L1_ffn_b, L1_ffn_Wq, L1_ffn_Wk, L1_ffn_A, L1_ffn_Bm, L1_c, L1_wmod):

    def _L0_attn_ref(x, Wqk_w, Wqk_b, Wv_w, Wv_b, Wo_w, Wo_b):
        import jax, jax.numpy as jnp
        import numpy as np
        B, N, D = (8, 128, 512)
        H = 8
        HEAD_DIM = D // H
        E = HEAD_DIM // H
        b, n, _ = x.shape
        qk = (x @ Wqk_w.T + Wqk_b).reshape(b, n, H, E, 2)
        q = jnp.transpose(qk[..., 0], (0, 2, 1, 3))
        k = jnp.transpose(qk[..., 1], (0, 2, 1, 3))
        v = (x @ Wv_w.T + Wv_b).reshape(b, n, H, E)
        v = jnp.transpose(v, (0, 2, 1, 3))
        scores = jnp.einsum('bhqd,bhkd->bhqk', q, k)
        attn = jax.nn.softmax(scores, axis=-1) / jnp.asarray(HEAD_DIM ** 0.5, x.dtype)
        out = jnp.einsum('bhsl,bhlv->bhsv', attn, v)
        out = jnp.transpose(out, (0, 2, 1, 3)).reshape(b, n, H * E)
        return out @ Wo_w.T + Wo_b

    def _L0_ffn_ref(x, base_W, base_b, router_W, router_b, A, B, expert_map):
        import jax, jax.numpy as jnp
        import numpy as np
        SCALING = 32.0 / 16.0
        E = A.shape[0]
        base_out = jnp.einsum('btd,od->bto', x, base_W) + base_b
        logits = jnp.einsum('btd,nd->btn', x, router_W) + router_b
        probs = jax.nn.softmax(logits, axis=-1)
        topk_p, topk_i = jax.lax.top_k(probs, E)
        mapped = expert_map[topk_i]
        onehot = (mapped[..., None] == jnp.arange(E)).astype(x.dtype)
        w = jnp.einsum('btk,btke->bte', topk_p, onehot)
        h = jnp.einsum('btd,erd->bter', x, A)
        lora = jnp.einsum('bter,eor->bto', h * w[..., None], B) * SCALING
        return base_out + lora

    def _L1_attn_ref(x, wq, wk, wv, wo):
        import jax, jax.numpy as jnp
        import numpy as np
        B, S, D = (2, 256, 512)
        NH, NKV = (32, 8)
        HD = D // NH
        NREP = NH // NKV
        SCALE = HD ** (-0.5)
        b, s, _ = x.shape
        q = (x @ wq).reshape(b, s, NH, HD)
        k = (x @ wk).reshape(b, s, NKV, HD)
        v = (x @ wv).reshape(b, s, NKV, HD)
        k = jnp.repeat(k, NREP, axis=2)
        v = jnp.repeat(v, NREP, axis=2)
        scores = jnp.einsum('bihd,bjhd->bhij', q, k) * SCALE
        causal = jnp.tril(jnp.ones((s, s), dtype=bool))
        scores = jnp.where(causal, scores, jnp.finfo(scores.dtype).min)
        attn = jax.nn.softmax(scores, axis=-1)
        out = jnp.einsum('bhij,bjhd->bihd', attn, v)
        out = out.reshape(b, s, NH * HD)
        return out @ wo

    def _L1_ffn_ref(x, W, b, Wq, Wk, A, Bm):
        import jax, jax.numpy as jnp
        import numpy as np
        import math
        E, DK, R = (8, 32, 16)
        SCALING = 16.0 / 16.0
        Bt, S, Din = x.shape
        result = jnp.einsum('bsi,oi->bso', x, W) + b
        q = jnp.einsum('bsi,ni->bsn', x, Wq).reshape(Bt, S, E, DK)
        k = jnp.einsum('bsi,ni->bsn', x, Wk).reshape(Bt, S, E, DK)
        scores = jnp.einsum('bsed,bsed->bse', q, k) / math.sqrt(DK)
        w = jax.nn.softmax(scores, axis=-1)
        h = jnp.einsum('bsi,eri->bser', x, A)
        combined = jnp.einsum('bse,bser,eor->bso', w, h, Bm) * SCALING
        return result + combined
    x = L0_attn_x
    mod = (_silu(L0_c) @ L0_wmod).reshape(L0_c.shape[0], 6, 1, -1)
    sa, ca, ga, sb, cb, gb = (mod[:, 0], mod[:, 1], mod[:, 2], mod[:, 3], mod[:, 4], mod[:, 5])
    ga = (2 * (ga >= 0) - 1) * jnp.maximum(jnp.abs(ga), 0.25)
    gb = (2 * (gb >= 0) - 1) * jnp.maximum(jnp.abs(gb), 0.25)
    h = _layernorm(x, axis=-1) * (1 + ca) + sa
    x = x + ga * _L0_attn_ref(h, L0_attn_Wqk_w, L0_attn_Wqk_b, L0_attn_Wv_w, L0_attn_Wv_b, L0_attn_Wo_w, L0_attn_Wo_b)
    h = _layernorm(x, axis=-1) * (1 + cb) + sb
    x = x + gb * _L0_ffn_ref(h, L0_ffn_base_W, L0_ffn_base_b, L0_ffn_router_W, L0_ffn_router_b, L0_ffn_A, L0_ffn_B, L0_ffn_expert_map)
    mod = (_silu(L1_c) @ L1_wmod).reshape(L1_c.shape[0], 6, 1, -1)
    sa, ca, ga, sb, cb, gb = (mod[:, 0], mod[:, 1], mod[:, 2], mod[:, 3], mod[:, 4], mod[:, 5])
    ga = (2 * (ga >= 0) - 1) * jnp.maximum(jnp.abs(ga), 0.25)
    gb = (2 * (gb >= 0) - 1) * jnp.maximum(jnp.abs(gb), 0.25)
    h = _layernorm(x, axis=-1) * (1 + ca) + sa
    x = x + ga * _L1_attn_ref(h, L1_attn_wq, L1_attn_wk, L1_attn_wv, L1_attn_wo)
    h = _layernorm(x, axis=-1) * (1 + cb) + sb
    x = x + gb * _L1_ffn_ref(h, L1_ffn_W, L1_ffn_b, L1_ffn_Wq, L1_ffn_Wk, L1_ffn_A, L1_ffn_Bm)
    return x

_drawn_inputs = setup_inputs


def setup_inputs(seed=0):
    import zlib

    import numpy as np

    out = dict(_drawn_inputs(seed))
    spreads = {'L0_attn_Wqk_b': (0.0, 0.8),
     'L0_attn_Wv_b': (0.0, 0.8),
     'L0_attn_Wo_b': (0.0, 0.308),
     'L1_ffn_b': (0.0, 1.022)}
    factors = {'L0_attn_Wqk_w': 8.0,
     'L0_attn_Wv_w': 8.0,
     'L0_attn_Wo_w': 8.0,
     'L0_ffn_base_b': 8.0,
     'L0_ffn_router_b': 8.0,
     'L1_attn_wq': 8.0,
     'L1_attn_wk': 8.0,
     'L1_attn_wv': 8.0,
     'L1_attn_wo': 8.0,
     'L1_ffn_Wq': 8.0,
     'L1_ffn_Wk': 8.0,
     'L1_ffn_A': 8.0,
     'L1_ffn_Bm': 8.0}
    for name, (base, spread) in spreads.items():
        noise = np.random.default_rng([zlib.crc32(name.encode()), seed]).standard_normal(out[name].shape)
        drawn = base * np.exp(spread * noise) if base else spread * noise
        out[name] = jnp.asarray(drawn.astype(out[name].dtype))
    for name, factor in factors.items():
        out[name] = (out[name] * factor).astype(out[name].dtype)
    return out
```

```python
import concourse.bass as bass
from concourse import mybir
from contextlib import ExitStack

F32 = mybir.dt.float32
F32R = mybir.dt.float32r
BF16 = mybir.dt.bfloat16
I32 = mybir.dt.int32
ALU = mybir.AluOpType
ACT = mybir.ActivationFunctionType
AX = mybir.AxisListType

P = 128
D = 512
NB = 4
N = 512
TT = N // P
CH = D // P
EPS = 1e-5
GATE_MIN = 0.25
NEG = -1e30
NMAP = 15
E = 8
R = 16
DK = 32
LORA_SCALE0 = 32.0 / 16.0
MROW = 96
SEED = 1
MIN_R = 256


class Attn:

    def __init__(self, name, hd, kv, rep, steps, causal, scale, ones):
        self.name, self.hd, self.kv, self.rep, self.steps = name, hd, kv, rep, steps
        self.causal, self.scale, self.ones = causal, scale, ones
        self.khs = kv // steps
        self.heads = self.khs * rep
        if rep == 1:
            self.quads = [[(0, k) for k in range(self.khs)]]
        else:
            self.quads = [[(r, k) for r in range(rep)] for k in range(self.khs)]
        self.nq = len(self.quads)
        self.jobs = self.heads * TT
        self.groups = steps * self.nq * TT
        self.vch = kv * hd
        self.och = kv * rep * hd
        self.oc = max(1, self.och // P)
        self.orows = min(P, self.och)
        self.kdma = 16 * 3 * kv
        self.qdma = 16 * 3 * rep
        self.mdma = 16 * 2 * (1 if rep == 1 else self.khs)
        g = [f"t{c}" for c in range(CH)]
        g += ["q0", "v"] if rep == 1 else ["k", "v", "q0", "q1"]
        for s in range(steps):
            g += [f"m{s}"]
            if rep > 1 and s + 2 < steps:
                g += [f"q{s + 2}"]
            if s:
                g += [f"o{n}" for n in range((s - 1) * self.nq, s * self.nq)]
        g += [f"o{n}" for n in range((steps - 1) * self.nq, steps * self.nq)]
        g += [f"c{c}" for c in range(self.oc)] + [f"y{q}" for q in range(TT)]
        self.gjobs = g


A0 = Attn("a0", 8, 8, 1, 2, False, 1.0, 8.0)
A1 = Attn("a1", 16, 8, 4, 4, True, 16.0 ** -0.5, 1.0)

XB = ["M0", "M1", "E0", "E1"]
BANKS = XB + ["V0", "V1", "G0", "G1"]
PHASES = ["mod0", "a0", "f0", "mod1", "a1", "f1"]
TURNS = {"mod0": 1, "mod1": 1, "a0": NB, "a1": NB, "f0": NB, "f1": NB}


def job_tables():
    uses = {p: {k: [] for k in BANKS} for p in PHASES}
    for m in ("mod0", "mod1"):
        for n in range(6):
            uses[m][f"G{n % 2}"].append(f"n{n}")
        for n in (0, 1, 3, 4):
            uses[m]["M0"].append(f"col{n}")
    for a in (A0, A1):
        for i, j in enumerate(a.gjobs):
            uses[a.name][f"G{i % 2}"].append(j)
        for i in range(a.steps * a.jobs):
            uses[a.name][f"M{i % 2}"].append(i)
            uses[a.name][f"E{i % 2}"].append(i)
        for i in range(a.steps * a.nq):
            uses[a.name][f"V{i % 2}"].append(i)
    for f in ("f0", "f1"):
        tiles = [f"s{q}" for q in range(TT)] if f == "f1" else []
        for i, j in enumerate([f"t{c}" for c in range(CH)] + tiles + ["w"]):
            uses[f][f"G{i % 2}"].append(j)
        for q in range(TT):
            uses[f][XB[q]].append("y")
        uses[f]["V0"].append("ar")
    return uses


USES = job_tables()


def start(phase, bank, b):
    base = SEED + sum(TURNS[p] * len(USES[p][bank]) for p in PHASES[:PHASES.index(phase)])
    return b * len(USES[phase][bank]) + base


def before(phase, bank, job, b):
    return start(phase, bank, b) + USES[phase][bank].index(job)


def g_bank(phase, job):
    return "G0" if job in USES[phase]["G0"] else "G1"


def output_bank(phase, q):
    return (g_bank(phase, f"y{q}"), f"y{q}") if phase[0] == "a" else (XB[q], "y")


def build(nc, t):
    with ExitStack() as ctx:
        def sb(name, shape, dt=F32):
            return ctx.enter_context(nc.sbuf_tensor(name, shape, dt))

        def sem(name):
            return ctx.enter_context(nc.semaphore(name))

        x = sb("x", [P, NB * TT, D])
        xn = sb("xn", [P, TT, D])
        hT = sb("hT", [P, CH, N])
        QS = sb("QS", [P, 16, N], F32R)
        KS = sb("KS", [P, 8, N], F32R)
        V = sb("V", [P, TT, 8, 32])
        PR = sb("PR", [P, 2, 4, N])
        partR = sb("partR", [P, 2, N], F32R)
        partL = sb("partL", [P, 2, N], F32R)
        kR = sb("kR", [P, N], F32R)
        kL = sb("kL", [P, N], F32R)
        tile2 = sb("tile2", [P, 2, D])
        oT = sb("oT", [P, CH, N])
        gate = sb("gate", [P, D])

        wqk0 = sb("wqk0", [P, CH, P])
        wv0 = sb("wv0", [P, CH, A0.vch])
        wo0 = sb("wo0", [A0.och, D])
        wbase = sb("wbase", [P, CH, D])
        war = sb("war", [P, CH, E * R + NMAP])
        wB = sb("wB", [E * R, D])
        wq1 = sb("wq1", [P, CH, D])
        wk1 = sb("wk1", [P, CH, P])
        wv1 = sb("wv1", [P, CH, P])
        wo1 = sb("wo1", [P, CH, D])
        wQK = sb("wQK", [P, CH, 2 * E * DK])
        wA1 = sb("wA1", [P, CH, E * R])
        bqk = sb("bqk", [P, 1])
        bv = sb("bv", [P, A0.vch])
        bo = sb("bo", [P, D])
        bbase = sb("bbase", [P, D])
        brout = sb("brout", [P, NMAP])
        emap = sb("emap", [P, NMAP], I32)
        emapf = sb("emapf", [P, NMAP])
        onehot = sb("onehot", [P, E, NMAP])

        ident = sb("ident", [P, P])
        identb = sb("identb", [P, P], BF16)
        maskf = sb("maskf", [P, P])
        maskb = sb("maskb", [P, P], BF16)
        padc = sb("padc", [P, 2, 8])
        half = sb("half", [P, TT])
        cT = sb("cT", [P, 2, CH, NB])
        cE = sb("cE", [P, 2, CH, NB])
        cols = sb("cols", [P, 2, 4 * CH, NB])
        st = sb("st", [P, TT, 6])
        mv = sb("mv", [P, TT, 2])
        vareps = sb("vareps", [P, TT])
        rstd = sb("rstd", [P, TT])
        mcol = sb("mcol", [P, 2, TT, 8])
        mh = sb("mh", [8, N], F32R)
        ml = sb("ml", [8, N], F32R)
        rs = sb("rs", [P, 2, TT, 4])
        lg = sb("lg", [P, TT, 16])
        lmax = sb("lmax", [P, TT])
        top = sb("top", [P, TT, 8])
        rest = sb("rest", [P, TT, 16])
        sel = sb("sel", [P, TT, 16])
        lsum = sb("lsum", [P, TT])
        lrec = sb("lrec", [P, TT])
        wsel = sb("wsel", [P, TT, E, NMAP])
        wexp = sb("wexp", [P, TT, E])
        modrow = oT[0:NB, 0:2, :]
        gabs = oT[0:NB, 2, :]
        gsign = oT[0:NB, 3, :]
        hw = oT[:, 0, :].rearrange("p (t n) -> p t n", t=TT)
        hwT = oT[:, 1, :].rearrange("p (t n) -> p t n", t=TT)
        qs = oT[:, 2, :].rearrange("p (a n) -> p a n", a=2)
        qk = oT[:, 3, :].rearrange("p (a n) -> p a n", a=2)

        gates_dram = nc.dram_tensor("gates_scratch", (2, 2, NB, D), F32).ap()

        ps = {k: ctx.enter_context(nc.psum_tensor(k, [P, 512], F32)) for k in XB + ["G0", "G1"]}
        VV = ctx.enter_context(nc.psum_tensor("VV", [P, 2, 512], F32))
        ps["V0"], ps["V1"] = VV[:, 0, :], VV[:, 1, :]

        full = {k: sem(f"full_{k}") for k in BANKS if k[0] != "V"}
        read = {k: sem(f"read_{k}") for k in BANKS}
        ld = {k: sem(f"ld_{k}") for k in ("c", "x", "l0", "l0f", "l1", "l1f", "wm0", "wm1", "gates", "gate", "out")}
        s_const = sem("s_const")
        s_constd = sem("s_constd")
        s_pad = sem("s_pad")
        s_apart = sem("s_apart")
        s_silu = sem("s_silu")
        s_silu_e = sem("s_silu_e")
        s_gate = sem("s_gate")
        s_vfill = sem("s_vfill")
        ph = {}
        for p in ("a0", "f0", "a1", "f1"):
            names = ["bn", "stats", "vareps", "rstd", "xn", "gated", "xadd"]
            if p[0] == "a":
                names += ["high", "kstack", "mstack", "rs", "on", "pd0", "pd1", "pv0", "pv1"]
                names += [f"qstack{i}" for i in range(4)]
            else:
                names += ["step", "lg", "ex", "qs", "ar"]
            ph[p] = {n: sem(f"{p}_{n}") for n in names}
        gate_turn = {"a0": 0, "f0": NB, "a1": 2 * NB, "f1": 3 * NB}

        block = ctx.enter_context(nc.Block())

        def xt(b, q, k=1):
            return x[:, bass.ds(b * TT + q, k), :]

        def wait_alone(eng, s, value):
            eng.wait_ge(s, value)
            eng.sem_inc(s_apart, 1)

        @block.sync
        def _(sp):
            def chunks(w):
                return w.rearrange("(c p) n -> p c n", p=P)

            def row_to_all(dst, v, s):
                sp.dma_start(dst, v.rearrange("(a n) -> a n", a=1).to_broadcast([P, v.shape[0]])).then_inc(s, 16)

            def load_wmod(layer, n):
                if n >= 2:
                    bank = f"G{n % 2}"
                    sp.wait_ge(full[bank], before(f"mod{layer}", bank, f"n{n - 2}", 0) + 1)
                sp.dma_start(PR[:, n % 2, :, :], chunks(t[f"wmod{layer}"])[:, :, n * D:(n + 1) * D])\
                    .then_inc(ld[f"wm{n % 2}"], 16)

            def store_gate(layer, which):
                sp.wait_ge(s_gate, (2 * layer + which) * 5 + 5)
                sp.dma_start(gates_dram[layer, which], gabs).then_inc(ld["gates"], 16)

            def load_gate(layer, which, b, phase):
                wait_alone(sp, ph[phase]["gated"], SEED + b * TT)
                sp.dma_start(gate[:, :], gates_dram[layer, which, bass.ds(b, 1), :].to_broadcast([P, D]))\
                    .then_inc(ld["gate"], 16)

            def move(dst, src, s):
                sp.dma_start(dst.bitcast(F32), src.bitcast(F32)).then_inc(s, 16)

            def stack_maxima(a, step, b):
                bank = g_bank(a.name, f"m{step}")
                sp.wait_ge(read[bank], before(a.name, bank, f"m{step}", b) + 1)
                for row, part in ((MROW, mh), (MROW + a.khs, ml)):
                    if a.rep == 1:
                        move(QS[row:row + a.khs, step, :], part[0:a.khs, :], ph[a.name]["mstack"])
                    else:
                        for k in range(a.khs):
                            move(QS[row + k:row + k + 1, step * 4:step * 4 + 4, :], part[4 * k:4 * k + 4, :], ph[a.name]["mstack"])

            def attention0():
                a, s = A0, ph["a0"]
                with sp.Fori(0, NB) as b:
                    load_gate(0, 0, b, "a0")
                    bank = g_bank("a0", "q0")
                    wait_alone(sp, read[bank], before("a0", bank, "q0", b) + 1)
                    sp.wait_ge(full["E1"], start("a0", "E1", b))
                    for step in range(a.steps):
                        for rows, part in ((0, partR), (32, partR), (64, partL)):
                            move(QS[rows:rows + 32, step, :], part[32 * step:32 * step + 32, 0, :], s[f"qstack{step}"])
                        for h in range(a.khs * step, a.khs * step + a.khs):
                            for rows, part in ((0, partR), (32, partL), (64, partR)):
                                row = rows + a.hd * (h % a.khs)
                                move(KS[row:row + a.hd, h, :], part[64 + a.hd * h:64 + a.hd * (h + 1), 0, :], s["kstack"])
                    for step in range(a.steps):
                        stack_maxima(a, step, b)

            def attention1():
                a, s = A1, ph["a1"]
                with sp.Fori(0, NB) as b:
                    load_gate(1, 0, b, "a1")
                    bank = g_bank("a1", "k")
                    wait_alone(sp, read[bank], before("a1", bank, "k", b) + 1)
                    sp.wait_ge(full["E1"], start("a1", "E1", b))
                    for h in range(a.kv):
                        for rows, part in ((0, kR), (32, kL), (64, kR)):
                            row = rows + a.hd * (h % a.khs)
                            move(KS[row:row + a.hd, h, :], part[a.hd * h:a.hd * (h + 1), :], s["kstack"])

                    def stack_queries(step):
                        bank = g_bank("a1", f"q{step}")
                        sp.wait_ge(read[bank], before("a1", bank, f"q{step}", b) + 1)
                        for rows, part in ((0, partR), (32, partR), (64, partL)):
                            for r in range(a.rep):
                                move(QS[rows:rows + 32, step * 4 + r, :], part[32 * r:32 * r + 32, step % 2, :], s[f"qstack{step}"])

                    stack_queries(0)
                    stack_queries(1)
                    for step in range(a.steps):
                        stack_maxima(a, step, b)
                        if step + 2 < a.steps:
                            stack_queries(step + 2)

            seeded = [*full.values(), *read.values()]
            for p in ("a0", "f0", "a1", "f1"):
                seeded += [ph[p][n] for n in ph[p] if n in ("gated", "xadd", "kstack", "mstack", "pv0", "pv1") or n[:6] == "qstack"]
            for s_ in seeded:
                sp.sem_inc(s_, SEED)
            for layer in (0, 1):
                sp.dma_start(cT[:, layer, :, :], t[f"c{layer}"].rearrange("(c p) b -> p c b", p=P)).then_inc(ld["c"], 16)
            load_wmod(0, 0)
            load_wmod(0, 1)
            for b in range(NB):
                sp.dma_start(x[:, b * TT:(b + 1) * TT, :], t["x"][b].rearrange("(t p) d -> p t d", p=P)).then_inc(ld["x"], 16)
            for dst, src in ((wqk0, "wqk0"), (wv0, "wv0")):
                sp.dma_start(dst[:, :, :], chunks(t[src])).then_inc(ld["l0"], 16)
            sp.dma_start(wo0[:, :], t["wo0"]).then_inc(ld["l0"], 16)
            sp.dma_start(bqk[:, :], t["bqk0"].rearrange("(p a) -> p a", a=1)).then_inc(ld["l0"], 16)
            row_to_all(bv[:, :], t["bv0"], ld["l0"])
            row_to_all(bo[:, :], t["bo0"], ld["l0"])
            for n in range(2, 4):
                load_wmod(0, n)
            store_gate(0, 0)
            for n in range(4, 6):
                load_wmod(0, n)
            sp.dma_start(wbase[:, :, :], chunks(t["wbase"])).then_inc(ld["l0f"], 16)
            sp.dma_start(war[:, :, :], chunks(t["war"])).then_inc(ld["l0f"], 16)
            sp.dma_start(wB[:, :], t["wB0"]).then_inc(ld["l0f"], 16)
            row_to_all(bbase[:, :], t["bbase"], ld["l0f"])
            row_to_all(brout[:, :], t["brout"], ld["l0f"])
            row_to_all(emap[:, :], t["emap"], ld["l0f"])
            for dst, src in ((wq1, "wq1"), (wk1, "wk1"), (wv1, "wv1"), (wo1, "wo1")):
                sp.dma_start(dst[:, :, :], chunks(t[src])).then_inc(ld["l1"], 16)
            for dst, src in ((wQK, "wQK1"), (wA1, "wA1")):
                sp.dma_start(dst[:, :, :], chunks(t[src])).then_inc(ld["l1f"], 16)
            store_gate(0, 1)
            sp.wait_ge(ld["gates"], 32)
            sp.wait_ge(s_pad, 2)
            attention0()
            sp.wait_ge(ph["a0"]["gated"], SEED + NB * TT)
            for parity in range(2):
                sp.wait_ge(ph["a0"][f"pv{parity}"], SEED + NB * A0.groups // 2)
            load_wmod(1, 0)
            load_wmod(1, 1)
            with sp.Fori(0, NB) as b:
                load_gate(0, 1, b, "f0")
            sp.wait_ge(ph["f0"]["xadd"], SEED + NB * TT)
            sp.dma_start(wbase[:, :, :], chunks(t["wW1"])).then_inc(ld["l1f"], 16)
            sp.dma_start(wB[:, :], t["wB1"]).then_inc(ld["l1f"], 16)
            row_to_all(bo[:, :], t["b1"], ld["l1f"])
            sp.wait_ge(ph["f0"]["gated"], SEED + NB * TT)
            for n in range(2, 4):
                load_wmod(1, n)
            store_gate(1, 0)
            for n in range(4, 6):
                load_wmod(1, n)
            store_gate(1, 1)
            sp.wait_ge(ld["gates"], 64)
            sp.wait_ge(s_pad, 4)
            attention1()
            sp.wait_ge(ph["a1"]["gated"], SEED + NB * TT)
            with sp.Fori(0, NB) as b:
                load_gate(1, 1, b, "f1")
                wait_alone(sp, ph["f1"]["xadd"], SEED + b * TT + TT)
                sp.dma_start(t["out"][bass.ds(b, 1), :, :].rearrange("a (t p) d -> p (a t) d", p=P),
                             xt(b, 0, TT)).then_inc(ld["out"], 16)
            sp.wait_ge(ld["out"], 16 * NB)

        @block.gpsimd
        def _(gp):
            for dst, value in ((ident[:, :], 0.0), (maskf[:, :], 0.0), (padc[:, :, :], 0.0), (half[:, :], -0.5)):
                gp.memset(dst, value).then_inc(s_const, 1)
            gp.wait_ge(s_const, 4)
            gp.affine_select(out=ident[:, :], in_=ident[:, :], compare_op=ALU.not_equal, fill=1.0, base=0,
                             pattern=[[-1, P]], channel_multiplier=1).then_inc(s_const, 1)
            gp.affine_select(out=maskf[:, :], in_=maskf[:, :], compare_op=ALU.is_ge, fill=NEG, base=0,
                             pattern=[[-1, P]], channel_multiplier=1).then_inc(s_const, 1)
            made = 6
            for layer, a in ((0, A0), (1, A1)):
                for row in (MROW, MROW + a.khs):
                    v = padc[:, layer, :].rearrange("p (g k) -> p g k", k=a.khs)
                    gp.affine_select(out=v, in_=v, compare_op=ALU.not_equal, fill=1.0, base=-row,
                                     pattern=[[0, a.steps], [-1, a.khs]], channel_multiplier=1).then_inc(s_const, 1)
                    made += 1
                    gp.wait_ge(s_const, made)

            def pads(layer):
                gp.memset(QS[MROW:P, :, :].bitcast(F32), 0.0).then_inc(s_const, 1)
                gp.wait_ge(s_const, made + 1 + layer)
                gp.memset(KS[:, :, :].bitcast(F32), 0.0).then_inc(s_pad, 1)
                gp.wait_ge(s_pad, 2 * layer + 1)
                gp.tensor_copy(KS[MROW:P, :, :], padc[MROW:P, layer, :, None].to_broadcast([P - MROW, 8, N]))\
                    .then_inc(s_pad, 1)
                gp.wait_ge(s_pad, 2 * layer + 2)

            def reciprocal_deviation(s, b):
                wait_alone(gp, s["stats"], b * TT + TT)
                gp.tensor_scalar(vareps[:, :], mv[:, :, 1], EPS, None, ALU.add).then_inc(s["vareps"], 1)
                gp.wait_ge(s["vareps"], b + 1)
                gp.tensor_tensor(rstd[:, :], vareps[:, :], half[:, :], ALU.pow).then_inc(s["rstd"], 1)

            def residual(phase, b):
                s = ph[phase]
                gp.wait_ge(ld["gate"], b * 16 + 16 * (gate_turn[phase] + 1))
                for q in range(TT):
                    bank, job = output_bank(phase, q)
                    gp.wait_ge(read[bank], before(phase, bank, job, b) + 1)
                    gp.tensor_tensor(tile2[:, q % 2, :], tile2[:, q % 2, :], gate[:, :], ALU.mult).then_inc(s["gated"], 1)
                    gp.wait_ge(s["gated"], SEED + b * TT + (q + 1))
                    gp.tensor_tensor(xt(b, q), xt(b, q), tile2[:, q % 2, None, :], ALU.add).then_inc(s["xadd"], 1)

            pads(0)
            with gp.Fori(0, NB) as b:
                reciprocal_deviation(ph["a0"], b)
                residual("a0", b)
            gp.wait_ge(full["E1"], start("f0", "E1", 0))
            gp.wait_ge(ph["a0"]["xadd"], SEED + NB * TT)
            pads(1)
            with gp.Fori(0, NB) as b:
                reciprocal_deviation(ph["f0"], b)
                residual("f0", b)
            with gp.Fori(0, NB) as b:
                s = ph["a1"]
                reciprocal_deviation(s, b)
                for g in range(A1.groups):
                    kt = g % TT
                    for n in (4 * g + 2, 4 * g + 3):
                        wait_alone(gp, read[f"E{n % 2}"], before("a1", f"E{n % 2}", n, b) + 1)
                    v = PR[:, g % 2, :, kt * P:(kt + 1) * P]
                    gp.affine_select(out=v, in_=v, compare_op=ALU.is_ge, fill=0.0, base=0,
                                     pattern=[[0, 4], [1, P]], channel_multiplier=-1).then_inc(s[f"pd{g % 2}"], 1)
                residual("a1", b)
            with gp.Fori(0, NB) as b:
                reciprocal_deviation(ph["f1"], b)
                residual("f1", b)

        @block.scalar
        def _(act):
            def modulated(phase, layer, kind, b):
                for c in range(CH):
                    bank = g_bank(phase, f"t{c}")
                    act.wait_ge(full[bank], before(phase, bank, f"t{c}", b) + 1)
                    act.activation(hT[:, c, :], ps[bank][:, :], ACT.Identity,
                                   scale=cols[:, layer, (kind + 1) * CH + c, bass.ds(b, 1)],
                                   bias=cols[:, layer, kind * CH + c, bass.ds(b, 1)]).then_inc(read[bank], 1)

            def high_part(phase, job, dst, b, bias):
                bank = g_bank(phase, job)
                act.wait_ge(full[bank], before(phase, bank, job, b) + 1)
                act.activation(dst, ps[bank][:, :], ACT.Identity, bias=bias).then_inc(ph[phase]["high"], 1)

            def max_high(a, step, b):
                bank = g_bank(a.name, f"m{step}")
                act.wait_ge(full[bank], before(a.name, bank, f"m{step}", b) + 1)
                act.wait_ge(ph[a.name]["mstack"], SEED + (b * a.steps + step) * a.mdma)
                act.activation(mh[0:a.heads, :], ps[bank][0:a.heads, :], ACT.Copy).then_inc(ph[a.name]["high"], 1)

            def copy_out(a, n, b):
                act.wait_ge(ph[a.name]["pv1"], SEED + b * (a.groups // 2) + (n + 1) * TT // 2)
                if n >= 2:
                    bank = g_bank(a.name, f"o{n - 2}")
                    act.wait_ge(full[bank], before(a.name, bank, f"o{n - 2}", b) + 1)
                else:
                    act.wait_ge(ph[a.name]["xadd"], SEED + b * TT)
                act.activation(tile2[:, n % 2, :], ps[f"V{n % 2}"], ACT.Copy).then_inc(read[f"V{n % 2}"], 1)

            def exp_step(a, step, b):
                for i in range(a.jobs):
                    n = step * a.jobs + i
                    g = n // 4
                    q0 = (g % TT) * P if a.causal else 0
                    bank = f"E{n % 2}"
                    if n % 4 == 0:
                        act.wait_ge(ph[a.name][f"pv{g % 2}"], SEED + b * (a.groups // 2) + g // 2)
                    if i > 4 * TT and i % (4 * TT) == 4:
                        copy_out(a, step * a.nq + i // (4 * TT) - 1, b)
                    act.wait_ge(full[bank], before(a.name, bank, n, b) + 1)
                    act.activation(PR[:, g % 2, n % 4, q0:N], ps[bank][:, q0:N], ACT.Exp, scale=a.scale)\
                        .then_inc(read[bank], 1)
                copy_out(a, step * a.nq + a.nq - 1, b)

            def finish(a, b):
                for c in range(a.oc):
                    bank = g_bank(a.name, f"c{c}")
                    act.wait_ge(full[bank], before(a.name, bank, f"c{c}", b) + 1)
                    act.activation(oT[0:a.orows, c, :], ps[bank][0:a.orows, :], ACT.Copy).then_inc(read[bank], 1)

            def lora_turned(phase, b):
                bank = g_bank(phase, "w")
                act.wait_ge(full[bank], before(phase, bank, "w", b) + 1)
                act.activation(oT[:, 1, :], ps[bank][:, :], ACT.Copy).then_inc(read[bank], 1)

            act.wait_ge(ld["c"], 32)
            act.activation(cE[:, :, :, :], cT[:, :, :, :], ACT.Exp, scale=-1.0).then_inc(s_silu_e, 1)
            act.wait_ge(ld["l0"], 16 * 6)
            act.wait_ge(read["M0"], start("a0", "M0", 0))
            with act.Fori(0, NB) as b:
                modulated("a0", 0, 0, b)
                act.wait_ge(ph["a0"]["kstack"], SEED + b * A0.kdma)
                for step in range(A0.steps):
                    act.wait_ge(ph["a0"][f"qstack{step}"], SEED + b * A0.qdma)
                high_part("a0", "q0", partR[:, 0, :], b, bqk[:, 0:1])
                max_high(A0, 0, b)
                for step in range(A0.steps):
                    exp_step(A0, step, b)
                    if step + 1 < A0.steps:
                        max_high(A0, step + 1, b)
                finish(A0, b)
            with act.Fori(0, NB) as b:
                modulated("f0", 0, 2, b)
                act.wait_ge(ph["f0"]["lg"], b + 1)
                act.activation(lg[:, :, 0:NMAP], lg[:, :, 0:NMAP], ACT.Exp).then_inc(ph["f0"]["ex"], 1)
                lora_turned("f0", b)
            act.wait_ge(read["M0"], start("a1", "M0", 0))
            with act.Fori(0, NB) as b:
                s = ph["a1"]
                modulated("a1", 1, 0, b)
                act.wait_ge(s["kstack"], SEED + b * A1.kdma)
                high_part("a1", "k", kR[:, :], b, 0.0)
                for i in range(2):
                    act.wait_ge(s[f"qstack{i + 2}"], SEED + b * A1.qdma)
                    high_part("a1", f"q{i}", partR[:, i, :], b, 0.0)
                max_high(A1, 0, b)
                for step in range(A1.steps):
                    if step + 2 < A1.steps:
                        act.wait_ge(s[f"qstack{step}"], SEED + b * A1.qdma + A1.qdma)
                        high_part("a1", f"q{step + 2}", partR[:, step % 2, :], b, 0.0)
                    exp_step(A1, step, b)
                    if step + 1 < A1.steps:
                        max_high(A1, step + 1, b)
                finish(A1, b)
            with act.Fori(0, NB) as b:
                s = ph["f1"]
                modulated("f1", 1, 2, b)
                for q in range(TT):
                    bank = g_bank("f1", f"s{q}")
                    act.wait_ge(full[bank], before("f1", bank, f"s{q}", b) + 1)
                    act.wait_ge(read[bank], before("f1", bank, f"s{q}", b))
                    act.activation(qs[:, q % 2, :], ps[bank][:, 0:E * DK], ACT.Copy).then_inc(s["qs"], 1)
                act.wait_ge(s["lg"], b + 1)
                act.activation(lg[:, :, 0:E], lg[:, :, 0:E], ACT.Exp, scale=float(DK) ** -0.5).then_inc(s["ex"], 1)
                lora_turned("f1", b)

        @block.vector
        def _(dve):
            def modulation(layer):
                m = f"mod{layer}"
                for n in range(6):
                    bank = f"G{n % 2}"
                    dve.wait_ge(full[bank], before(m, bank, f"n{n}", 0) + 1)
                    if n >= 2 and n - 2 in (0, 1, 3, 4):
                        dve.wait_ge(full["M0"], before(m, "M0", f"col{n - 2}", 0) + 1)
                    row = modrow[:, n % 2, :]
                    if n in (2, 5):
                        done = (2 * layer + n // 3) * 5
                        if done:
                            dve.wait_ge(ld["gates"], 16 * (done // 5))
                        dve.tensor_copy(row, ps[bank][0:NB, :]).then_inc(read[bank], 1)
                        dve.wait_ge(read[bank], before(m, bank, f"n{n}", 0) + 1)
                        dve.tensor_scalar(gabs, row, -1.0, None, ALU.mult).then_inc(s_gate, 1)
                        dve.tensor_scalar(gsign, row, 0.0, 2.0, ALU.is_ge, ALU.mult).then_inc(s_gate, 1)
                        dve.wait_ge(s_gate, done + 2)
                        dve.tensor_tensor(gabs, gabs, row, ALU.max).then_inc(s_gate, 1)
                        dve.wait_ge(s_gate, done + 3)
                        dve.tensor_scalar(gabs, gabs, GATE_MIN, None, ALU.max).then_inc(s_gate, 1)
                        dve.wait_ge(s_gate, done + 4)
                        dve.scalar_tensor_tensor(out=gabs, in0=gsign, scalar=-1.0, in1=gabs,
                                                 op0=ALU.add, op1=ALU.mult).then_inc(s_gate, 1)
                        continue
                    dve.tensor_scalar(row, ps[bank][0:NB, :], 1.0 if n in (1, 4) else 0.0, None, ALU.add)\
                        .then_inc(read[bank], 1)
                    kind = {0: 0, 1: 1, 3: 2, 4: 3}[n]
                    dve.wait_ge(full["M0"], before(m, "M0", f"col{n}", 0) + 1)
                    dve.tensor_copy(cols[:, layer, kind * CH:(kind + 1) * CH, :],
                                    ps["M0"][:, 0:CH * NB].rearrange("p (c b) -> p c b", c=CH)).then_inc(read["M0"], 1)

            def normalise(phase, b):
                s = ph[phase]
                for q in range(TT):
                    dve.bn_stats(st[:, q, :], xt(b, q)).then_inc(s["bn"], 1)
                wait_alone(dve, s["bn"], b * TT + TT)
                for q in range(TT):
                    dve.bn_aggr(mv[:, q, :], st[:, q, :]).then_inc(s["stats"], 1)
                dve.wait_ge(s["rstd"], b + 1)
                for q in range(TT):
                    dve.tensor_scalar(xn[:, q, None, :], xt(b, q), mv[:, q, 0:1], rstd[:, q:q + 1],
                                      ALU.subtract, ALU.mult).then_inc(s["xn"], 1)

            def low_part(a, job, dst, high, b, nth, bias=None):
                highs = 1 + a.steps if a.rep == 1 else 1 + 2 * a.steps
                bank = g_bank(a.name, job)
                dve.wait_ge(ph[a.name]["high"], b * highs + nth)
                rows = dst.shape[0]
                if bias is None:
                    dve.tensor_tensor(dst, ps[bank][0:rows, :], high.bitcast(F32), ALU.subtract).then_inc(read[bank], 1)
                else:
                    dve.scalar_tensor_tensor(out=dst, in0=ps[bank][0:rows, :], scalar=bias, in1=high.bitcast(F32),
                                             op0=ALU.add, op1=ALU.subtract).then_inc(read[bank], 1)

            def values(a, b):
                bank = g_bank(a.name, "v")
                dve.wait_ge(full[bank], before(a.name, bank, "v", b) + 1)
                src = ps[bank][:, 0:TT * a.vch].rearrange("p (t h d) -> p t h d", t=TT, d=a.hd)
                dst = V[:, :, :, 0:a.hd]
                if a is A0:
                    dve.tensor_tensor(dst, src, bv[:, None, :].rearrange("p a (h d) -> p a h d", d=a.hd)
                                      .to_broadcast([P, TT, a.kv, a.hd]), ALU.add).then_inc(read[bank], 1)
                else:
                    dve.tensor_copy(dst, src).then_inc(read[bank], 1)

            def maxima(a, step, b):
                if step >= 2:
                    bank = g_bank(a.name, f"m{step - 2}")
                    dve.wait_ge(full[bank], before(a.name, bank, f"m{step - 2}", b) + 1)
                for i in range(a.jobs):
                    n = step * a.jobs + i
                    h, qt = i // TT, i % TT
                    bank = f"M{n % 2}"
                    dve.wait_ge(full[bank], before(a.name, bank, n, b) + 1)
                    dve.tensor_reduce(mcol[:, step % 2, qt, h:h + 1], ps[bank][:, 0:(qt + 1) * P if a.causal else N],
                                      AX.X, ALU.max, negate=True).then_inc(read[bank], 1)

            def heads_normalised(a, n, b):
                s = ph[a.name]
                bank = g_bank(a.name, f"o{n}")
                dve.wait_ge(full[bank], before(a.name, bank, f"o{n}", b) + 1)
                v = ps[bank][:, :].rearrange("p (t i w) -> p t i w", t=TT, i=4)
                dve.reciprocal(rs[:, n % 2, :, :], v[:, :, :, a.hd]).then_inc(s["rs"], 1)
                dve.wait_ge(s["rs"], b * (a.steps * a.nq) + (n + 1))
                dst = xn[:, :, n * 4 * a.hd:(n + 1) * 4 * a.hd].rearrange("p t (i w) -> p t i w", i=4)
                dve.tensor_tensor(dst, v[:, :, :, 0:a.hd], rs[:, n % 2, :, :, None].to_broadcast([P, TT, 4, a.hd]), ALU.mult)\
                    .then_inc(read[bank], 1)

            def output_tiles(phase, bias, b):
                s = ph[phase]
                for q in range(TT):
                    bank, job = output_bank(phase, q)
                    dve.wait_ge(full[bank], before(phase, bank, job, b) + 1)
                    if q >= 2:
                        dve.wait_ge(s["xadd"], SEED + b * TT + (q - 1))
                    else:
                        dve.wait_ge(s["xadd"], SEED + b * TT)
                    if bias is None:
                        dve.tensor_copy(tile2[:, q % 2, :], ps[bank][:, :]).then_inc(read[bank], 1)
                    else:
                        dve.tensor_tensor(tile2[:, q % 2, :], ps[bank][:, :], bias, ALU.add).then_inc(read[bank], 1)

            def attention(a, prev, bias):
                s = ph[a.name]
                done = 2 * (a is A1)
                dve.memset(V[:, :, :, :], 0.0).then_inc(s_vfill, 1)
                dve.wait_ge(s_vfill, done + 1)
                dve.memset(V[:, :, :, a.hd], a.ones).then_inc(s_vfill, 1)
                dve.wait_ge(s_vfill, done + 2)
                with dve.Fori(0, NB) as b:
                    if prev:
                        dve.wait_ge(ph[prev]["xadd"], SEED + b * TT + TT)
                    for c in range(a.oc):
                        bank = g_bank(a.name, f"c{c}")
                        dve.wait_ge(full[bank], start(a.name, bank, b))
                    normalise(a.name, b)
                    if a.rep == 1:
                        low_part(a, "q0", partL[:, 0, :], partR[:, 0, :], b, 1, bqk[:, 0:1])
                        values(a, b)
                        nth = 1
                    else:
                        low_part(a, "k", kL[:, :], kR[:, :], b, 1)
                        values(a, b)
                        low_part(a, "q0", partL[:, 0, :], partR[:, 0, :], b, 2)
                        low_part(a, "q1", partL[:, 1, :], partR[:, 1, :], b, 3)
                        nth = 3
                    for step in range(a.steps):
                        maxima(a, step, b)
                        nth += 1
                        low_part(a, f"m{step}", ml[0:a.heads, :], mh[0:a.heads, :], b, nth)
                        if a.rep > 1 and step + 2 < a.steps:
                            nth += 1
                            low_part(a, f"q{step + 2}", partL[:, step % 2, :], partR[:, step % 2, :], b, nth)
                        if step:
                            for n in range((step - 1) * a.nq, step * a.nq):
                                heads_normalised(a, n, b)
                    for n in range((a.steps - 1) * a.nq, a.steps * a.nq):
                        heads_normalised(a, n, b)
                    output_tiles(a.name, bias, b)

            def feed0():
                s = ph["f0"]
                S = 9
                with dve.Fori(0, NB) as b:
                    dve.wait_ge(ph["a0"]["xadd"], SEED + b * TT + TT)
                    normalise("f0", b)
                    dve.wait_ge(s["ar"], b + 1)
                    ar = VV[:, :, 0:2 * (E * R + NMAP)].rearrange("p k (j n) -> p k j n", j=2)
                    dve.tensor_tensor(lg[:, :, 0:NMAP].rearrange("p (k j) n -> p k j n", k=2), ar[:, :, :, E * R:],
                                      brout[:, None, None, :].to_broadcast([P, 2, 2, NMAP]), ALU.add).then_inc(s["step"], 1)
                    dve.wait_ge(s["step"], b * S + 1)
                    dve.tensor_reduce(lmax[:, :], lg[:, :, 0:NMAP], AX.X, ALU.max).then_inc(s["step"], 1)
                    dve.wait_ge(s["step"], b * S + 2)
                    dve.tensor_tensor(lg[:, :, 0:NMAP], lg[:, :, 0:NMAP], lmax[:, :, None].to_broadcast([P, TT, NMAP]),
                                      ALU.subtract).then_inc(s["lg"], 1)
                    dve.wait_ge(s["ex"], b + 1)
                    dve.tensor_reduce(lsum[:, :], lg[:, :, 0:NMAP], AX.X, ALU.add).then_inc(s["step"], 1)
                    for q in range(TT):
                        ins = dve.max(top[:, q, :], lg[:, q, 0:NMAP])
                    ins.then_inc(s["step"], 1)
                    dve.wait_ge(s["step"], b * S + 4)
                    dve.reciprocal(lrec[:, :], lsum[:, :]).then_inc(s["step"], 1)
                    for q in range(TT):
                        ins = dve.match_replace(out=rest[:, q, 0:NMAP], in_to_replace=top[:, q, :],
                                                in_values=lg[:, q, 0:NMAP], imm_value=0.0)
                    ins.then_inc(s["step"], 1)
                    dve.wait_ge(s["step"], b * S + 6)
                    dve.tensor_tensor(sel[:, :, 0:NMAP], lg[:, :, 0:NMAP], rest[:, :, 0:NMAP], ALU.subtract)\
                        .then_inc(s["step"], 1)
                    dve.wait_ge(s["step"], b * S + 7)
                    dve.tensor_tensor(wsel[:, :, :, :], sel[:, :, None, 0:NMAP].to_broadcast([P, TT, E, NMAP]),
                                      onehot[:, None, :, :].to_broadcast([P, TT, E, NMAP]), ALU.mult).then_inc(s["step"], 1)
                    dve.wait_ge(s["step"], b * S + 8)
                    dve.tensor_reduce(wexp[:, :, :], wsel[:, :, :, :], AX.X, ALU.add).then_inc(s["step"], 1)
                    dve.wait_ge(s["step"], b * S + 9)
                    for q in range(TT):
                        h = ar[:, q // 2, q % 2, 0:E * R].rearrange("p (e r) -> p e r", e=E)
                        ins = dve.scalar_tensor_tensor(out=hw[:, q, :].rearrange("p (e r) -> p e r", e=E), in0=h,
                                                       scalar=lrec[:, q:q + 1],
                                                       in1=wexp[:, q, :, None].to_broadcast([P, E, R]),
                                                       op0=ALU.mult, op1=ALU.mult)
                    ins.then_inc(read["V0"], 1)
                    output_tiles("f0", bbase[:, :], b)

            def feed1():
                s = ph["f1"]
                S = 11
                with dve.Fori(0, NB) as b:
                    dve.wait_ge(ph["a1"]["xadd"], SEED + b * TT + TT)
                    normalise("f1", b)
                    for q in range(TT):
                        bank = g_bank("f1", f"s{q}")
                        dve.wait_ge(s["qs"], b * TT + (q + 1))
                        dve.tensor_tensor(qk[:, q % 2, :], ps[bank][:, E * DK:2 * E * DK], qs[:, q % 2, :], ALU.mult)\
                            .then_inc(read[bank], 1)
                        dve.wait_ge(read[bank], before("f1", bank, f"s{q}", b) + 1)
                        dve.tensor_reduce(lg[:, q, 0:E], qk[:, q % 2, :].rearrange("p (e d) -> p e d", e=E), AX.X, ALU.add)\
                            .then_inc(s["step"], 1)
                        dve.wait_ge(s["step"], b * 8 + (q + 1))
                    dve.tensor_reduce(lmax[:, :], lg[:, :, 0:E], AX.X, ALU.max).then_inc(s["step"], 1)
                    dve.wait_ge(s["step"], b * 8 + 5)
                    dve.tensor_tensor(lg[:, :, 0:E], lg[:, :, 0:E], lmax[:, :, None].to_broadcast([P, TT, E]),
                                      ALU.subtract).then_inc(s["lg"], 1)
                    dve.wait_ge(s["ex"], b + 1)
                    dve.tensor_reduce(lsum[:, :], lg[:, :, 0:E], AX.X, ALU.add).then_inc(s["step"], 1)
                    dve.wait_ge(s["step"], b * 8 + 6)
                    dve.reciprocal(lrec[:, :], lsum[:, :]).then_inc(s["step"], 1)
                    dve.wait_ge(s["step"], b * 8 + 7)
                    dve.tensor_tensor(wexp[:, :, :], lg[:, :, 0:E], lrec[:, :, None].to_broadcast([P, TT, E]), ALU.mult)\
                        .then_inc(s["step"], 1)
                    dve.wait_ge(s["step"], b * 8 + 8)
                    dve.wait_ge(s["ar"], b + 1)
                    dve.tensor_tensor(hw[:, :, :].rearrange("p t (e r) -> p (t e) r", e=E),
                                      ps["V0"].rearrange("p (u r) -> p u r", r=R),
                                      wexp[:, :, :].rearrange("p t e -> p (t e)")[:, :, None].to_broadcast([P, TT * E, R]),
                                      ALU.mult).then_inc(read["V0"], 1)
                    output_tiles("f1", bo[:, :], b)

            dve.wait_ge(s_silu_e, 1)
            dve.tensor_scalar(cE[:, :, :, :], cE[:, :, :, :], 1.0, None, ALU.add).then_inc(s_silu, 1)
            dve.wait_ge(s_silu, 1)
            dve.reciprocal(cE[:, :, :, :], cE[:, :, :, :]).then_inc(s_silu, 1)
            dve.wait_ge(s_silu, 2)
            dve.tensor_tensor(cT[:, :, :, :], cT[:, :, :, :], cE[:, :, :, :], ALU.mult).then_inc(s_silu, 1)
            dve.wait_ge(s_const, 6)
            dve.tensor_copy(identb[:, :], ident[:, :]).then_inc(s_constd, 1)
            dve.tensor_copy(maskb[:, :], maskf[:, :]).then_inc(s_constd, 1)
            modulation(0)
            dve.wait_ge(ld["l0f"], 16 * 6)
            dve.tensor_copy(emapf[:, :], emap[:, :]).then_inc(s_constd, 1)
            dve.wait_ge(s_constd, 3)
            for e in range(E):
                dve.tensor_scalar(onehot[:, e, :], emapf[:, :], float(e), LORA_SCALE0, ALU.is_equal, ALU.mult)\
                    .then_inc(s_constd, 1)
            dve.wait_ge(s_constd, 3 + E)
            dve.wait_ge(ld["l0"], 16 * 6)
            dve.wait_ge(ld["x"], 16 * NB)
            attention(A0, None, bo[:, :])
            feed0()
            modulation(1)
            attention(A1, "f0", None)
            dve.wait_ge(ld["l1f"], 16 * 5)
            feed1()

        @block.tensor
        def _(pe):
            def modulation(layer):
                m = f"mod{layer}"
                for n in range(6):
                    bank = f"G{n % 2}"
                    pe.wait_ge(ld[f"wm{n % 2}"], 16 * (3 * layer + n // 2 + 1))
                    pe.wait_ge(read[bank], before(m, bank, f"n{n}", 0))
                    for c in range(CH):
                        mm = pe.matmul(ps[bank][0:NB, :], cT[:, layer, c, :], PR[:, n % 2, c, :],
                                       start=(c == 0), stop=(c == CH - 1))
                    mm.then_inc(full[bank], 1)
                    if n in (2, 5):
                        continue
                    pe.wait_ge(read[bank], before(m, bank, f"n{n}", 0) + 1)
                    pe.wait_ge(read["M0"], before(m, "M0", f"col{n}", 0))
                    for c in range(CH):
                        mm = pe.transpose(ps["M0"][:, c * NB:(c + 1) * NB], modrow[:, n % 2, c * P:(c + 1) * P],
                                          ident[0:NB, 0:NB])
                    mm.then_inc(full["M0"], 1)

            def turned(phase, b):
                pe.wait_ge(ph[phase]["xn"], b * TT + TT)
                for c in range(CH):
                    bank = g_bank(phase, f"t{c}")
                    pe.wait_ge(read[bank], before(phase, bank, f"t{c}", b))
                    for q in range(TT):
                        mm = pe.transpose(ps[bank][:, q * P:(q + 1) * P], xn[:, q, c * P:(c + 1) * P], ident[:, :])
                    mm.then_inc(full[bank], 1)

            def hT_ready(phase, b):
                for c in range(CH):
                    bank = g_bank(phase, f"t{c}")
                    pe.wait_ge(read[bank], before(phase, bank, f"t{c}", b) + 1)

            def project(phase, job, w, b):
                bank = g_bank(phase, job)
                pe.wait_ge(read[bank], before(phase, bank, job, b))
                for c in range(CH):
                    mm = pe.matmul(ps[bank][:, :], w[:, c, :], hT[:, c, :], start=(c == 0), stop=(c == CH - 1))
                mm.then_inc(full[bank], 1)

            def project_values(a, w, b):
                bank = g_bank(a.name, "v")
                pe.wait_ge(read[bank], before(a.name, bank, "v", b))
                for q in range(TT):
                    for c in range(CH):
                        mm = pe.matmul(ps[bank][:, q * a.vch:(q + 1) * a.vch], hT[:, c, q * P:(q + 1) * P], w[:, c, :],
                                       start=(c == 0), stop=(c == CH - 1))
                mm.then_inc(full[bank], 1)

            def query_major(a, step, i, b):
                n = step * a.jobs + i
                h, qt = i // TT, i % TT
                kh = step * a.khs + h // a.rep
                slot = step if a.rep == 1 else step * 4 + h % a.rep
                bank = f"M{n % 2}"
                if i == 0:
                    pe.wait_ge(ph[a.name][f"qstack{step}"], SEED + b * a.qdma + a.qdma)
                    if step == 0:
                        pe.wait_ge(ph[a.name]["kstack"], SEED + b * a.kdma + a.kdma)
                pe.wait_ge(read[bank], before(a.name, bank, n, b))
                cols_ = max(MIN_R, (qt + 1) * P) if a.causal else N
                mm = pe.matmul(ps[bank][:, 0:cols_], QS[0:MROW, slot, qt * P:(qt + 1) * P], KS[0:MROW, kh, 0:cols_],
                               start=True, stop=not a.causal)
                if a.causal:
                    mm = pe.matmul(ps[bank][:, qt * P:(qt + 1) * P], identb[:, :], maskb[:, :], start=False, stop=True)
                mm.then_inc(full[bank], 1)

            def maxima_turned(a, step, b):
                for n in (step * a.jobs + a.jobs - 2, step * a.jobs + a.jobs - 1):
                    pe.wait_ge(read[f"M{n % 2}"], before(a.name, f"M{n % 2}", n, b) + 1)
                bank = g_bank(a.name, f"m{step}")
                pe.wait_ge(read[bank], before(a.name, bank, f"m{step}", b))
                for q in range(TT):
                    mm = pe.transpose(ps[bank][0:a.heads, q * P:(q + 1) * P], mcol[:, step % 2, q, 0:a.heads], ident[:, :])
                mm.then_inc(full[bank], 1)

            def key_major(a, step, i, b):
                n = step * a.jobs + i
                g = i // 4
                r, k = a.quads[g // TT][i % 4]
                kt = g % TT
                kh = step * a.khs + k
                slot = step if a.rep == 1 else step * 4 + r
                q0 = min(kt * P, N - MIN_R) if a.causal else 0
                bank = f"E{n % 2}"
                if i == 0:
                    pe.wait_ge(ph[a.name]["mstack"], SEED + (b * a.steps + (step + 1)) * a.mdma)
                pe.wait_ge(read[bank], before(a.name, bank, n, b))
                pe.matmul(ps[bank][:, q0:N], KS[:, kh, kt * P:(kt + 1) * P], QS[:, slot, q0:N],
                          start=True, stop=True).then_inc(full[bank], 1)

            def value_product(a, step, gi, b):
                g = step * a.nq * TT + gi
                kt = gi % TT
                quad = step * a.nq + gi // TT
                q0 = kt * P if a.causal else 0
                bank = f"V{quad % 2}"
                for n in (4 * g + 2, 4 * g + 3):
                    pe.wait_ge(read[f"E{n % 2}"], before(a.name, f"E{n % 2}", n, b) + 1)
                if a.causal:
                    pe.wait_ge(ph[a.name][f"pd{g % 2}"], b * (a.groups // 2) + (g // 2 + 1))
                if kt == 0:
                    pe.wait_ge(read[bank], before(a.name, bank, quad, b))
                for i, (_, k) in enumerate(a.quads[gi // TT]):
                    mm = pe.matmul(ps[bank][32 * i:32 * i + 32, q0:N], V[:, kt, step * a.khs + k, :],
                                   PR[:, g % 2, i, q0:N], start=(kt == 0), stop=(kt == TT - 1))
                mm.then_inc(ph[a.name][f"pv{g % 2}"], 1)

            def heads_turned(a, n, b):
                bank = g_bank(a.name, f"o{n}")
                pe.wait_ge(read[f"V{n % 2}"], before(a.name, f"V{n % 2}", n, b) + 1)
                pe.wait_ge(read[bank], before(a.name, bank, f"o{n}", b))
                for q in range(TT):
                    mm = pe.transpose(ps[bank][:, q * P:(q + 1) * P], tile2[:, n % 2, q * P:(q + 1) * P], ident[:, :])
                mm.then_inc(full[bank], 1)

            def output(a, w, b):
                for n in (a.steps * a.nq - 2, a.steps * a.nq - 1):
                    bank = g_bank(a.name, f"o{n}")
                    wait_alone(pe, read[bank], before(a.name, bank, f"o{n}", b) + 1)
                for c in range(a.oc):
                    bank = g_bank(a.name, f"c{c}")
                    wait_alone(pe, read[bank], before(a.name, bank, f"c{c}", b))
                    for q in range(TT):
                        mm = pe.transpose(ps[bank][0:a.orows, q * P:(q + 1) * P], xn[:, q, c * P:c * P + a.orows], ident[:, :])
                    mm.then_inc(full[bank], 1)
                for c in range(a.oc):
                    bank = g_bank(a.name, f"c{c}")
                    pe.wait_ge(read[bank], before(a.name, bank, f"c{c}", b) + 1)
                for q in range(TT):
                    bank = g_bank(a.name, f"y{q}")
                    pe.wait_ge(read[bank], before(a.name, bank, f"y{q}", b))
                    for c in range(a.oc):
                        rhs = w[:, :] if a.oc == 1 else w[:, c, :]
                        mm = pe.matmul(ps[bank][:, :], oT[0:a.orows, c, q * P:(q + 1) * P], rhs,
                                       start=(c == 0), stop=(c == a.oc - 1))
                    mm.then_inc(full[bank], 1)

            def attention(a, w, b):
                turned(a.name, b)
                hT_ready(a.name, b)
                if a.rep == 1:
                    project(a.name, "q0", w["qk"], b)
                    project_values(a, w["v"], b)
                else:
                    project(a.name, "k", w["k"], b)
                    project_values(a, w["v"], b)
                    project(a.name, "q0", w["q"][:, :, 0:P], b)
                    project(a.name, "q1", w["q"][:, :, P:2 * P], b)
                for i in range(a.jobs):
                    query_major(a, 0, i, b)
                for step in range(a.steps):
                    maxima_turned(a, step, b)
                    if a.rep > 1 and step + 2 < a.steps:
                        project(a.name, f"q{step + 2}", w["q"][:, :, (step + 2) * P:(step + 3) * P], b)
                    if step:
                        for n in range((step - 1) * a.nq, step * a.nq):
                            heads_turned(a, n, b)
                    for i in range(a.jobs):
                        key_major(a, step, i, b)
                        if step + 1 < a.steps:
                            query_major(a, step + 1, i, b)
                        if i % 4 == 3 and i > 4:
                            value_product(a, step, i // 4 - 1, b)
                    value_product(a, step, a.jobs // 4 - 1, b)
                for n in range((a.steps - 1) * a.nq, a.steps * a.nq):
                    heads_turned(a, n, b)
                output(a, w["o"], b)

            def feed(phase, b):
                turned(phase, b)
                hT_ready(phase, b)
                pe.wait_ge(read["V0"], before(phase, "V0", "ar", b))
                for q in range(TT):
                    if phase == "f0":
                        dst, w = VV[:, q // 2, (q % 2) * (E * R + NMAP):(q % 2 + 1) * (E * R + NMAP)], war
                    else:
                        dst, w = VV[:, 0, q * E * R:(q + 1) * E * R], wA1
                    for c in range(CH):
                        mm = pe.matmul(dst, hT[:, c, q * P:(q + 1) * P], w[:, c, :], start=(c == 0), stop=(c == CH - 1))
                mm.then_inc(ph[phase]["ar"], 1)
                if phase == "f1":
                    for q in range(TT):
                        bank = g_bank(phase, f"s{q}")
                        pe.wait_ge(read[bank], before(phase, bank, f"s{q}", b))
                        for c in range(CH):
                            mm = pe.matmul(ps[bank][:, :], hT[:, c, q * P:(q + 1) * P], wQK[:, c, :],
                                           start=(c == 0), stop=(c == CH - 1))
                        mm.then_inc(full[bank], 1)
                for q in range(TT):
                    pe.wait_ge(read[XB[q]], before(phase, XB[q], "y", b))
                    for c in range(CH):
                        pe.matmul(ps[XB[q]][:, :], hT[:, c, q * P:(q + 1) * P], wbase[:, c, :], start=(c == 0), stop=False)
                bank = g_bank(phase, "w")
                pe.wait_ge(read["V0"], before(phase, "V0", "ar", b) + 1)
                pe.wait_ge(read[bank], before(phase, bank, "w", b))
                for q in range(TT):
                    mm = pe.transpose(ps[bank][:, q * P:(q + 1) * P], hw[:, q, :], ident[:, :])
                mm.then_inc(full[bank], 1)
                pe.wait_ge(read[bank], before(phase, bank, "w", b) + 1)
                for q in range(TT):
                    pe.matmul(ps[XB[q]][:, :], hwT[:, q, :], wB[:, :], start=False, stop=True).then_inc(full[XB[q]], 1)

            pe.wait_ge(s_silu, 3)
            pe.wait_ge(s_const, 5)
            pe.wait_ge(s_constd, 2)
            modulation(0)
            pe.wait_ge(ld["l0"], 16 * 6)
            pe.wait_ge(s_vfill, 2)
            with pe.Fori(0, NB) as b:
                attention(A0, {"qk": wqk0, "v": wv0, "o": wo0}, b)
            pe.wait_ge(ld["l0f"], 16 * 6)
            with pe.Fori(0, NB) as b:
                feed("f0", b)
            modulation(1)
            pe.wait_ge(ld["l1"], 16 * 4)
            pe.wait_ge(s_vfill, 4)
            with pe.Fori(0, NB) as b:
                attention(A1, {"k": wk1, "v": wv1, "q": wq1, "o": wo1}, b)
            pe.wait_ge(ld["l1f"], 16 * 5)
            with pe.Fori(0, NB) as b:
                feed("f1", b)


def kernel(**inputs):
    import numpy as np
    import concourse.bacc as bacc
    from concourse import mybir as mb
    from concourse.bass_utils import run_bass_kernel_spmd

    g = {k: np.asarray(v) for k, v in inputs.items()}
    kv, rep, hd = A1.kv, A1.rep, A1.hd
    wqk = g["L0_attn_Wqk_w"].reshape(64, 2, D).transpose(1, 0, 2).reshape(128, D)
    bqk = g["L0_attn_Wqk_b"].reshape(64, 2).T.reshape(128)
    wq = g["L1_attn_wq"].reshape(D, A1.steps, A1.khs, rep, hd).transpose(0, 1, 3, 2, 4).reshape(D, kv * rep * hd)
    data = {
        "x": g["L0_attn_x"],
        "c0": g["L0_c"].T, "c1": g["L1_c"].T, "wmod0": g["L0_wmod"], "wmod1": g["L1_wmod"],
        "wqk0": wqk.T, "bqk0": bqk, "wv0": g["L0_attn_Wv_w"].T, "bv0": g["L0_attn_Wv_b"],
        "wo0": g["L0_attn_Wo_w"].T, "bo0": g["L0_attn_Wo_b"],
        "wbase": g["L0_ffn_base_W"].T, "bbase": g["L0_ffn_base_b"],
        "war": np.concatenate([g["L0_ffn_A"].reshape(E * R, D).T, g["L0_ffn_router_W"].T], axis=1),
        "brout": g["L0_ffn_router_b"],
        "wB0": g["L0_ffn_B"].transpose(0, 2, 1).reshape(E * R, D),
        "emap": g["L0_ffn_expert_map"],
        "wq1": wq, "wk1": g["L1_attn_wk"], "wv1": g["L1_attn_wv"], "wo1": g["L1_attn_wo"],
        "wW1": g["L1_ffn_W"].T, "b1": g["L1_ffn_b"],
        "wQK1": np.concatenate([g["L1_ffn_Wq"].T, g["L1_ffn_Wk"].T], axis=1),
        "wA1": g["L1_ffn_A"].reshape(E * R, D).T,
        "wB1": g["L1_ffn_Bm"].transpose(0, 2, 1).reshape(E * R, D),
    }
    nc = bacc.Bacc("TRN2", target_bir_lowering=False, num_devices=1)
    arrays, t = {}, {}
    for name, a in data.items():
        a = np.ascontiguousarray(a)
        arrays[f"in_{name}"] = a
        t[name] = nc.dram_tensor(f"in_{name}", a.shape, mb.dt.from_np(a.dtype), kind="ExternalInput").ap()
    t["out"] = nc.dram_tensor("out", (NB, N, D), F32, kind="ExternalOutput").ap()
    build(nc, t)
    r = run_bass_kernel_spmd(nc, [arrays], core_ids=[0])
    return r.results[0]["out"]
```

```python
import concourse.bass as bass
from concourse import mybir
from contextlib import ExitStack

F32 = mybir.dt.float32
F32R = mybir.dt.float32r
BF16 = mybir.dt.bfloat16
I32 = mybir.dt.int32
ALU = mybir.AluOpType
ACT = mybir.ActivationFunctionType
AX = mybir.AxisListType

P = 128
D = 512
NB = 4
N = 512
TT = N // P
CH = D // P
EPS = 1e-5
GATE_MIN = 0.25
NEG = -1e30
NMAP = 15
E = 8
R = 16
DK = 32
LORA_SCALE0 = 32.0 / 16.0
MROW = 96
SEED = 1
MIN_R = 256


class Attn:

    def __init__(self, name, hd, kv, rep, steps, causal, scale, ones):
        self.name, self.hd, self.kv, self.rep, self.steps = name, hd, kv, rep, steps
        self.causal, self.scale, self.ones = causal, scale, ones
        self.khs = kv // steps
        self.heads = self.khs * rep
        if rep == 1:
            self.quads = [[(0, k) for k in range(self.khs)]]
        else:
            self.quads = [[(r, k) for r in range(rep)] for k in range(self.khs)]
        self.nq = len(self.quads)
        self.jobs = self.heads * TT
        self.groups = steps * self.nq * TT
        self.vch = kv * hd
        self.och = kv * rep * hd
        self.oc = max(1, self.och // P)
        self.orows = min(P, self.och)
        self.kgroups = kv if rep == 1 else 2
        self.kdma = 16 * 3 * (1 if rep == 1 else self.khs)
        self.qdma = 16 * 3
        self.mdma = 16 * 2
        turned = [f"t{c}'" for c in range(CH)]
        last = [f"c{c}" for c in range(self.oc)] + [f"y{q}" for q in range(TT)]
        if rep == 1:
            self.after = [["m1"] + turned + ["q0'", "o0"], ["m0'", "o1", "v'"] + last]
            self.lag = 8
        else:
            self.after = [["m1", "q3", "o0", "o1"], ["m2"] + turned + ["k'", "o2", "o3"],
                          ["m3", "q0'", "q1'", "o4", "o5"], ["m0'", "o6", "o7", "v'", "q2'"] + last]
            self.lag = 0
        self.ahead = [j[:-1] for jobs in self.after for j in jobs if j[-1] == "'"]
        first = self.ahead.index("m0")
        self.first, self.second = self.ahead[:first], self.ahead[first:]
        self.turn_step = 0 if rep == 1 else 1


A0 = Attn("a0", 8, 8, 1, 2, False, 1.0, 8.0)
A1 = Attn("a1", 16, 8, 4, 4, True, 16.0 ** -0.5, 1.0)

XB = ["M0", "M1", "E0", "E1"]
BANKS = XB + ["V0", "V1", "G0", "G1"]
PHASES = ["mod0", "a0", "mod1a", "f0", "mod1b", "a1", "f1"]
TURNS = {"mod0": 1, "mod1a": 1, "mod1b": 1, "a0": NB, "a1": NB, "f0": NB, "f1": NB}


def mod_phase(layer, n):
    return "mod0" if layer == 0 else "mod1a" if n < 2 else "mod1b"


def job_tables():
    uses = {p: {k: [] for k in BANKS + ["high"]} for p in PHASES}
    for layer in (0, 1):
        for n in (0, 1, 3, 4):
            uses[mod_phase(layer, n)]["M0"].append(f"col{n}")
        for n in (2, 5):
            uses[mod_phase(layer, n)]["M1"].append(f"gate{n}")
    for a in (A0, A1):
        jobs = [j for step in a.after for j in step]
        for i, j in enumerate(jobs):
            uses[a.name][f"G{i % 2}"].append(j)
        uses[a.name]["high"] += [j for j in jobs if j[0] in "kqm"]
        for i in range(a.steps * a.jobs):
            uses[a.name][f"M{i % 2}"].append(i)
            uses[a.name][f"E{i % 2}"].append(i)
        for i in range(a.steps * a.nq):
            uses[a.name][f"V{i % 2}"].append(i)
    for f in ("f0", "f1"):
        tiles = [f"s{q}" for q in range(TT)] if f == "f1" else []
        for i, j in enumerate(tiles + [f"t{c}'" for c in range(CH)] + ["w"]):
            uses[f][f"G{i % 2}"].append(j)
        for q in range(TT):
            uses[f][XB[q]].append("y")
        uses[f]["V0"].append("ar")
    return uses


USES = job_tables()


class Sample:

    def __init__(self, turn, ahead=0):
        self.turn, self.ahead = turn, ahead

    def count(self, per, more):
        if isinstance(self.turn, int):
            return (self.turn + self.ahead) * per + more
        return self.turn * per + (self.ahead * per + more)


def loop(eng, turn):
    with eng.Fori(0, NB - 1) as b:
        turn(Sample(b), Sample(b, 1))
    turn(Sample(NB - 1), None)


ONCE = Sample(0)


def start(phase, bank):
    return SEED + sum(TURNS[p] * len(USES[p][bank]) for p in PHASES[:PHASES.index(phase)])


def before(phase, bank, job, smp):
    jobs = USES[phase][bank]
    base = 0 if bank == "high" else start(phase, bank)
    ahead = [j for j in jobs if str(j)[-1] == "'"]
    if not ahead:
        return smp.count(len(jobs), base + jobs.index(job))
    if isinstance(smp.turn, int) and smp.turn < 0:
        return base + ahead.index(job + "'")
    if smp.ahead:
        job += "'"
    if isinstance(smp.turn, int):
        jobs_here = [j for j in jobs if j not in ahead]
        return base + len(ahead) + smp.turn * len(jobs) + jobs_here.index(job)
    return smp.turn * len(jobs) + (base + len(ahead) + jobs.index(job))


def turn_start(phase, bank, smp):
    jobs = USES[phase][bank]
    return smp.count(len(jobs), start(phase, bank) + len([j for j in jobs if j[-1] == "'"]))


def g_bank(phase, job):
    here = USES[phase]["G0"]
    return "G0" if job in here or job + "'" in here else "G1"


def output_bank(phase, q):
    return (g_bank(phase, f"y{q}"), f"y{q}") if phase[0] == "a" else (XB[q], "y")


def build(nc, t):
    with ExitStack() as ctx:
        def sb(name, shape, dt=F32):
            return ctx.enter_context(nc.sbuf_tensor(name, shape, dt))

        def sem(name):
            return ctx.enter_context(nc.semaphore(name))

        x = sb("x", [P, NB * TT, D])
        xn = sb("xn", [P, TT, D])
        on = sb("on", [P, TT, D])
        hT = sb("hT", [P, CH, N])
        QS = sb("QS", [P, 16, N], F32R)
        KS = sb("KS", [P, 8, N], F32R)
        V = sb("V", [P, TT, 8, 32])
        PR = sb("PR", [P, 2, 4, N])
        partR = sb("partR", [P, 2, N], F32R)
        partL = sb("partL", [P, 2, N], F32R)
        kR = sb("kR", [P, N], F32R)
        kL = sb("kL", [P, N], F32R)
        tile2 = sb("tile2", [P, 2, D])
        oT = sb("oT", [P, CH, N])
        gate = sb("gate", [P, D])

        wqk0 = sb("wqk0", [P, CH, P])
        wv0 = sb("wv0", [P, CH, A0.vch])
        wo0 = sb("wo0", [A0.och, D])
        wbase = sb("wbase", [P, CH, D])
        war = sb("war", [P, CH, E * R + NMAP])
        wB = sb("wB", [E * R, D])
        wq1 = sb("wq1", [P, CH, D])
        wk1 = sb("wk1", [P, CH, P])
        wv1 = sb("wv1", [P, CH, P])
        wo1 = sb("wo1", [P, CH, D])
        wQK, wA1 = wq1, wk1
        bqk = sb("bqk", [P, 1])
        bv = sb("bv", [P, A0.vch])
        bo = sb("bo", [P, D])
        bbase = sb("bbase", [P, D])
        brout = sb("brout", [P, NMAP])
        emap = sb("emap", [P, NMAP], I32)
        emapf = sb("emapf", [P, NMAP])
        onehot = sb("onehot", [P, E, NMAP])

        ident = sb("ident", [P, P])
        identb = sb("identb", [P, P], BF16)
        maskf = sb("maskf", [P, P])
        maskb = sb("maskb", [P, P], BF16)
        padc = sb("padc", [P, 2, 8])
        half = sb("half", [P, TT])
        cT = sb("cT", [P, 2, CH, NB])
        cE = sb("cE", [P, 2, CH, NB])
        cols = sb("cols", [P, 2, 4 * CH, NB])
        st = sb("st", [P, TT, 6])
        mv = sb("mv", [P, TT, 2])
        vareps = sb("vareps", [P, TT])
        rstd = sb("rstd", [P, TT])
        mcol = sb("mcol", [P, 2, TT, 8])
        mh = sb("mh", [8, N], F32R)
        ml = sb("ml", [8, N], F32R)
        rs = sb("rs", [P, 2, TT, 4])
        lg = sb("lg", [P, TT, 16])
        lmax = sb("lmax", [P, TT])
        top = sb("top", [P, TT, 8])
        rest = sb("rest", [P, TT, 16])
        sel = sb("sel", [P, TT, 16])
        lsum = sb("lsum", [P, TT])
        lrec = sb("lrec", [P, TT])
        wsel = sb("wsel", [P, TT, E, NMAP])
        wexp = sb("wexp", [P, TT, E])
        grow = oT[0:NB, 0, :]
        gabs = oT[0:NB, 2, :]
        gsign = oT[0:NB, 3, :]
        hw = oT[:, 0, :].rearrange("p (t n) -> p t n", t=TT)
        hwT = oT[:, 1, :].rearrange("p (t n) -> p t n", t=TT)
        qs = oT[:, 2, :].rearrange("p (a n) -> p a n", a=2)
        qk = oT[:, 3, :].rearrange("p (a n) -> p a n", a=2)

        gates_dram = nc.dram_tensor("gates_scratch", (2, 2, NB, D), F32).ap()

        ps = {k: ctx.enter_context(nc.psum_tensor(k, [P, 512], F32)) for k in XB + ["G0", "G1"]}
        VV = ctx.enter_context(nc.psum_tensor("VV", [P, 2, 512], F32))
        ps["V0"], ps["V1"] = VV[:, 0, :], VV[:, 1, :]

        full = {k: sem(f"full_{k}") for k in BANKS if k[0] != "V"}
        read = {k: sem(f"read_{k}") for k in BANKS}
        ld = {k: sem(f"ld_{k}") for k in ("c", "x0", "x", "l0", "l0f", "l1", "l1f", "gates", "gate", "out")}
        ld_wmod = [sem(f"ld_wmod{n}") for n in range(6)]
        s_const = sem("s_const")
        s_constd = sem("s_constd")
        s_pad = sem("s_pad")
        s_apart = sem("s_apart")
        s_silu = sem("s_silu")
        s_silu_e = sem("s_silu_e")
        s_gate = sem("s_gate")
        s_vfill = sem("s_vfill")
        ph = {}
        for p in ("a0", "f0", "a1", "f1"):
            names = ["bn", "stats", "vareps", "rstd", "xn", "gated", "xadd"]
            if p[0] == "a":
                names += ["high", "mstack", "rs", "pd0", "pd1", "pv0", "pv1"]
                a = A0 if p == "a0" else A1
                names += [f"qstack{n}" for n in range(a.steps)] + [f"kstack{n}" for n in range(a.kgroups)]
            else:
                names += ["step", "lg", "ex", "qs", "ar"]
            ph[p] = {n: sem(f"{p}_{n}") for n in names}
        gate_turn = {"a0": 0, "f0": NB, "a1": 2 * NB, "f1": 3 * NB}

        block = ctx.enter_context(nc.Block())

        wmod_at = [[PR[:, 0, :, :], PR[:, 1, :, :], wq1[:, :, :], wo1[:, :, :], wbase[:, :, :], on[:, :, :]],
                   [wq1[:, :, :], wo1[:, :, :], on[:, :, :], PR[:, 0, :, :], PR[:, 1, :, :], wo1[:, :, :]]]

        def xt(smp, q, k=1):
            return x[:, bass.ds(smp.count(TT, q), k), :]

        def wait_alone(eng, s, value):
            eng.wait_ge(s, value)
            eng.sem_inc(s_apart, 1)

        @block.sync
        def _(sp):
            def chunks(w):
                return w.rearrange("(c p) n -> p c n", p=P)

            def row_to_all(dst, v, s):
                sp.dma_start(dst, v.rearrange("(a n) -> a n", a=1).to_broadcast([P, v.shape[0]])).then_inc(s, 16)

            def load_wmod(layer, n):
                sp.dma_start(wmod_at[layer][n], chunks(t[f"wmod{layer}"])[:, :, n * D:(n + 1) * D]).then_inc(ld_wmod[n], 16)

            def store_gate(layer, which):
                sp.wait_ge(s_gate, (2 * layer + which) * 5 + 5)
                sp.dma_start(gates_dram[layer, which], gabs).then_inc(ld["gates"], 16)

            def load_gate(layer, which, smp, phase):
                wait_alone(sp, ph[phase]["xadd"], smp.count(TT, SEED))
                sp.dma_start(gate[:, :], gates_dram[layer, which, bass.ds(smp.count(1, 0), 1), :].to_broadcast([P, D]))\
                    .then_inc(ld["gate"], 16)

            def move(dst, src, s):
                sp.dma_start(dst.bitcast(F32), src.bitcast(F32)).then_inc(s, 16)

            def stack_maxima(a, step, smp):
                bank = g_bank(a.name, f"m{step}")
                sp.wait_ge(read[bank], before(a.name, bank, f"m{step}", smp) + 1)
                for row, part in ((MROW, mh), (MROW + a.khs, ml)):
                    move(QS[row:row + a.khs, step * a.rep:(step + 1) * a.rep, :], part[0:a.heads, :], ph[a.name]["mstack"])

            def stack_step0(step):
                for rows, part in ((0, partR), (32, partR), (64, partL)):
                    move(QS[rows:rows + 32, step, :], part[32 * step:32 * step + 32, 0, :], ph["a0"][f"qstack{step}"])
                for h in range(A0.khs * step, A0.khs * step + A0.khs):
                    for rows, part in ((0, partR), (32, partL), (64, partR)):
                        row, src = rows + A0.hd * (h % A0.khs), 64 + A0.hd * h
                        move(KS[row:row + A0.hd, h, :], part[src:src + A0.hd, 0, :], ph["a0"][f"kstack{h}"])

            def projection_split(phase, job, smp):
                bank = g_bank(phase, job)
                sp.wait_ge(read[bank], before(phase, bank, job, smp) + 1)

            def first0(nxt):
                projection_split("a0", "q0", nxt)
                stack_step0(0)
                stack_step0(1)
                store_gate(0, 0)
                store_gate(0, 1)
                stack_maxima(A0, 0, nxt)

            def turn0(smp, nxt):
                stack_maxima(A0, 1, smp)
                load_gate(0, 0, smp, "a0")
                if nxt:
                    projection_split("a0", "q0", nxt)
                    stack_step0(0)
                    stack_maxima(A0, 0, nxt)
                    stack_step0(1)

            def stack_queries(step, smp):
                projection_split("a1", f"q{step}", smp)
                for rows, part in ((0, partR), (32, partR), (64, partL)):
                    move(QS[rows:rows + 32, step * A1.rep:(step + 1) * A1.rep, :], part[:, step % 2, :], ph["a1"][f"qstack{step}"])

            def stack_keys(half):
                for parity in range(A1.khs):
                    first = 4 * half + parity
                    src = 64 * half + 32 * parity
                    for rows, part in ((0, kR), (32, kL), (64, kR)):
                        row = rows + A1.hd * parity
                        move(KS[row:row + A1.hd, first:first + 3:2, :], part[src:src + 32, :], ph["a1"][f"kstack{half}"])

            def first1(nxt):
                projection_split("a1", "k", nxt)
                stack_keys(0)
                stack_queries(0, nxt)
                stack_queries(1, nxt)
                stack_keys(1)
                store_gate(1, 0)
                store_gate(1, 1)
                stack_maxima(A1, 0, nxt)
                stack_queries(2, nxt)

            def turn1(smp, nxt):
                stack_maxima(A1, 1, smp)
                stack_queries(3, smp)
                stack_maxima(A1, 2, smp)
                load_gate(1, 0, smp, "a1")
                if nxt:
                    projection_split("a1", "k", nxt)
                    stack_keys(0)
                else:
                    for dst, src in ((wQK, "wQK1"), (wA1, "wA1")):
                        sp.dma_start(dst[:, :, :], chunks(t[src])).then_inc(ld["l1f"], 16)
                stack_maxima(A1, 3, smp)
                if nxt:
                    stack_queries(0, nxt)
                    stack_queries(1, nxt)
                    stack_maxima(A1, 0, nxt)
                    stack_keys(1)
                    stack_queries(2, nxt)

            seeded = [*full.values(), *read.values()]
            for p in ("a0", "f0", "a1", "f1"):
                seeded += [ph[p][n] for n in ph[p] if n in ("xadd", "mstack", "pv0", "pv1") or n[1:6] == "stack"]
            for s_ in seeded:
                sp.sem_inc(s_, SEED)
            for layer in (0, 1):
                sp.dma_start(cT[:, layer, :, :], t[f"c{layer}"].rearrange("(c p) b -> p c b", p=P)).then_inc(ld["c"], 16)
            def load_x(b, s):
                sp.dma_start(x[:, b * TT:(b + 1) * TT, :], t["x"][b].rearrange("(t p) d -> p t d", p=P)).then_inc(ld[s], 16)

            load_x(0, "x0")
            load_wmod(0, 0)
            load_wmod(0, 1)
            sp.dma_start(wqk0[:, :, :], chunks(t["wqk0"])).then_inc(ld["l0"], 16)
            sp.dma_start(bqk[:, :], t["bqk0"].rearrange("(p a) -> p a", a=1)).then_inc(ld["l0"], 16)
            sp.dma_start(wv0[:, :, :], chunks(t["wv0"])).then_inc(ld["l0"], 16)
            sp.dma_start(wo0[:, :], t["wo0"]).then_inc(ld["l0"], 16)
            row_to_all(bv[:, :], t["bv0"], ld["l0"])
            row_to_all(bo[:, :], t["bo0"], ld["l0"])
            for n in range(2, 6):
                load_wmod(0, n)
            for b in range(1, NB):
                load_x(b, "x")
            sp.dma_start(war[:, :, :], chunks(t["war"])).then_inc(ld["l0f"], 16)
            sp.dma_start(wB[:, :], t["wB0"]).then_inc(ld["l0f"], 16)
            row_to_all(bbase[:, :], t["bbase"], ld["l0f"])
            row_to_all(brout[:, :], t["brout"], ld["l0f"])
            row_to_all(emap[:, :], t["emap"], ld["l0f"])
            sp.wait_ge(s_pad, 2)
            first0(Sample(-1, 1))
            sp.dma_start(wbase[:, :, :], chunks(t["wbase"])).then_inc(ld["l0f"], 16)
            for n in (0, 1):
                load_wmod(1, n)
            sp.wait_ge(ld["gates"], 32)
            loop(sp, turn0)
            sp.wait_ge(full["E1"], start("f0", "E1"))
            for parity in range(2):
                sp.wait_ge(ph["a0"][f"pv{parity}"], SEED + NB * A0.groups // 2)
            sp.wait_ge(ph["a0"]["xadd"], SEED + NB * TT)
            with sp.Fori(0, 1) as b:
                load_gate(0, 1, Sample(b), "f0")
            for n in (3, 4, 2):
                load_wmod(1, n)
            sp.wait_ge(full["M0"], start("f0", "M0"))
            for dst, src in ((wk1, "wk1"), (wv1, "wv1"), (wq1, "wq1")):
                sp.dma_start(dst[:, :, :], chunks(t[src])).then_inc(ld["l1"], 16)
            load_wmod(1, 5)
            with sp.Fori(0, NB - 1) as b:
                load_gate(0, 1, Sample(b, 1), "f0")
            sp.wait_ge(ph["f0"]["xadd"], SEED + NB * TT)
            sp.dma_start(wbase[:, :, :], chunks(t["wW1"])).then_inc(ld["l1f"], 16)
            sp.dma_start(wB[:, :], t["wB1"]).then_inc(ld["l1f"], 16)
            row_to_all(bo[:, :], t["b1"], ld["l1f"])
            sp.wait_ge(s_pad, 3)
            first1(Sample(-1, 1))
            sp.dma_start(wo1[:, :, :], chunks(t["wo1"])).then_inc(ld["l1"], 16)
            sp.wait_ge(ld["gates"], 64)
            sp.wait_ge(ph["f0"]["xadd"], SEED + NB * TT)
            loop(sp, turn1)
            sp.wait_ge(ph["a1"]["xadd"], SEED + NB * TT)
            with sp.Fori(0, NB) as b:
                smp = Sample(b)
                load_gate(1, 1, smp, "f1")
                wait_alone(sp, ph["f1"]["xadd"], smp.count(TT, SEED + TT))
                sp.dma_start(t["out"][bass.ds(b, 1), :, :].rearrange("a (t p) d -> p (a t) d", p=P),
                             xt(smp, 0, TT)).then_inc(ld["out"], 16)
            sp.wait_ge(ld["out"], 16 * NB)

        @block.gpsimd
        def _(gp):
            for dst, value in ((ident[:, :], 0.0), (maskf[:, :], 0.0), (padc[:, :, :], 0.0), (half[:, :], -0.5)):
                gp.memset(dst, value).then_inc(s_const, 1)
            gp.wait_ge(s_const, 4)
            gp.affine_select(out=ident[:, :], in_=ident[:, :], compare_op=ALU.not_equal, fill=1.0, base=0,
                             pattern=[[-1, P]], channel_multiplier=1).then_inc(s_const, 1)
            gp.affine_select(out=maskf[:, :], in_=maskf[:, :], compare_op=ALU.is_ge, fill=NEG, base=0,
                             pattern=[[-1, P]], channel_multiplier=1).then_inc(s_const, 1)
            made = 6
            for layer, a in ((0, A0), (1, A1)):
                for row in (MROW, MROW + a.khs):
                    v = padc[:, layer, :].rearrange("p (g k) -> p g k", k=a.khs)
                    gp.affine_select(out=v, in_=v, compare_op=ALU.not_equal, fill=1.0, base=-row,
                                     pattern=[[0, a.steps], [-1, a.khs]], channel_multiplier=1).then_inc(s_const, 1)
                    made += 1
                    gp.wait_ge(s_const, made)

            def clear_keys(layer):
                gp.tensor_copy(KS[:, :, :], padc[:, layer, :, None].to_broadcast([P, 8, N])).then_inc(s_pad, 1)

            def reciprocal_deviation(s, smp):
                wait_alone(gp, s["stats"], smp.count(TT, TT))
                gp.tensor_scalar(vareps[:, :], mv[:, :, 1], EPS, None, ALU.add).then_inc(s["vareps"], 1)
                gp.wait_ge(s["vareps"], smp.count(1, 1))
                gp.tensor_tensor(rstd[:, :], vareps[:, :], half[:, :], ALU.pow).then_inc(s["rstd"], 1)

            def residual(phase, smp):
                s = ph[phase]
                for q in range(TT):
                    bank, job = output_bank(phase, q)
                    if phase == "a1":
                        wait_alone(gp, read[bank], before(phase, bank, job, smp) + 1)
                    else:
                        wait_alone(gp, s["gated"], smp.count(TT, q + 1))
                    gp.tensor_tensor(xt(smp, q), xt(smp, q), tile2[:, q % 2, None, :], ALU.add).then_inc(s["xadd"], 1)

            def mask_group(g, smp):
                kt = g % TT
                for n in (4 * g + 2, 4 * g + 3):
                    wait_alone(gp, read[f"E{n % 2}"], before("a1", f"E{n % 2}", n, smp) + 1)
                v = PR[:, g % 2, :, kt * P:(kt + 1) * P]
                gp.affine_select(out=v, in_=v, compare_op=ALU.is_ge, fill=0.0, base=0,
                                 pattern=[[0, 4], [1, P]], channel_multiplier=-1).then_inc(ph["a1"][f"pd{g % 2}"], 1)

            def turn(phase, onward):
                def one(smp, nxt):
                    if nxt:
                        reciprocal_deviation(ph[phase], nxt)
                    elif onward:
                        reciprocal_deviation(ph[onward], Sample(-1, 1))
                    residual(phase, smp)
                return one

            def turn1(smp, nxt):
                each = A1.nq * TT
                for g in range(A1.groups):
                    if nxt and g == A1.turn_step * each + each // 2 - 1:
                        reciprocal_deviation(ph["a1"], nxt)
                    if not nxt and g == (A1.steps - 1) * each + 1:
                        reciprocal_deviation(ph["f1"], Sample(-1, 1))
                    mask_group(g, smp)
                residual("a1", smp)

            gp.memset(QS[MROW:P, :, :].bitcast(F32), 0.0).then_inc(s_pad, 1)
            gp.wait_ge(s_pad, 1)
            clear_keys(0)
            reciprocal_deviation(ph["a0"], Sample(-1, 1))
            loop(gp, turn("a0", "f0"))
            gp.wait_ge(full["E1"], start("f0", "E1"))
            clear_keys(1)
            loop(gp, turn("f0", "a1"))
            loop(gp, turn1)
            loop(gp, turn("f1", None))

        @block.scalar
        def _(act):
            def modulated(phase, c, smp):
                layer, kind = int(phase[1]), 2 * (phase[0] == "f")
                bank = g_bank(phase, f"t{c}")
                act.wait_ge(full[bank], before(phase, bank, f"t{c}", smp) + 1)
                b = smp.count(1, 0)
                act.activation(hT[:, c, :], ps[bank][:, :], ACT.Identity,
                               scale=cols[:, layer, (kind + 1) * CH + c, bass.ds(b, 1)],
                               bias=cols[:, layer, kind * CH + c, bass.ds(b, 1)]).then_inc(read[bank], 1)

            def high_part(a, job, smp):
                s = ph[a.name]
                if a.rep == 1:
                    for n in range(a.kgroups):
                        act.wait_ge(s[f"kstack{n}"], smp.count(a.kdma, SEED))
                    for n in range(a.steps):
                        act.wait_ge(s[f"qstack{n}"], smp.count(a.qdma, SEED))
                    dst, bias = partR[:, 0, :], bqk[:, 0:1]
                elif job == "k":
                    for n in range(a.kgroups):
                        act.wait_ge(s[f"kstack{n}"], smp.count(a.kdma, SEED))
                    dst, bias = kR[:, :], 0.0
                else:
                    step = int(job[1])
                    if step < 2:
                        act.wait_ge(s[f"qstack{step + 2}"], smp.count(a.qdma, SEED))
                    else:
                        act.wait_ge(s[f"qstack{step - 2}"], smp.count(a.qdma, SEED + a.qdma))
                    dst, bias = partR[:, step % 2, :], 0.0
                bank = g_bank(a.name, job)
                act.wait_ge(full[bank], before(a.name, bank, job, smp) + 1)
                act.activation(dst, ps[bank][:, :], ACT.Identity, bias=bias).then_inc(s["high"], 1)

            def max_high(a, step, smp):
                bank = g_bank(a.name, f"m{step}")
                act.wait_ge(full[bank], before(a.name, bank, f"m{step}", smp) + 1)
                act.wait_ge(ph[a.name]["mstack"], smp.count(a.steps * a.mdma, step * a.mdma + SEED))
                act.activation(mh[0:a.heads, :], ps[bank][0:a.heads, :], ACT.Copy).then_inc(ph[a.name]["high"], 1)

            def copy_out(a, n, smp):
                act.wait_ge(ph[a.name]["pv1"], smp.count(a.groups // 2, (n + 1) * TT // 2 + SEED))
                if n >= 2:
                    bank = g_bank(a.name, f"o{n - 2}")
                    act.wait_ge(full[bank], before(a.name, bank, f"o{n - 2}", smp) + 1)
                else:
                    act.wait_ge(ph[a.name]["xadd"], smp.count(TT, SEED))
                act.activation(tile2[:, n % 2, :], ps[f"V{n % 2}"], ACT.Copy).then_inc(read[f"V{n % 2}"], 1)

            def exp_step(a, step, smp):
                for i in range(a.jobs):
                    n = step * a.jobs + i
                    g = n // 4
                    q0 = (g % TT) * P if a.causal else 0
                    bank = f"E{n % 2}"
                    if n % 4 == 0:
                        act.wait_ge(ph[a.name][f"pv{g % 2}"], smp.count(a.groups // 2, g // 2 + SEED))
                    if i > 4 * TT and i % (4 * TT) == 4:
                        copy_out(a, step * a.nq + i // (4 * TT) - 1, smp)
                    act.wait_ge(full[bank], before(a.name, bank, n, smp) + 1)
                    act.activation(PR[:, g % 2, n % 4, q0:N], ps[bank][:, q0:N], ACT.Exp, scale=a.scale)\
                        .then_inc(read[bank], 1)
                copy_out(a, step * a.nq + a.nq - 1, smp)

            def outputs_turned(a, c, smp):
                bank = g_bank(a.name, f"c{c}")
                act.wait_ge(full[bank], before(a.name, bank, f"c{c}", smp) + 1)
                act.activation(oT[0:a.orows, c, :], ps[bank][0:a.orows, :], ACT.Copy).then_inc(read[bank], 1)

            def job(a, j, smp):
                if j[0] == "t":
                    modulated(a.name, int(j[1]), smp)
                elif j[0] in "kq":
                    high_part(a, j, smp)
                elif j[0] == "m":
                    max_high(a, int(j[1]), smp)
                elif j[0] == "c":
                    outputs_turned(a, int(j[1]), smp)

            def attention_turn(a, smp, nxt):
                for step in range(a.steps):
                    exp_step(a, step, smp)
                    for j in a.after[step]:
                        if j[-1] != "'":
                            job(a, j, smp)
                        elif nxt:
                            job(a, j[:-1], nxt)

            def attention(a):
                for j in a.ahead:
                    job(a, j, Sample(-1, 1))
                act.wait_ge(ld["gates"], 32 * (int(a.name[1]) + 1))
                loop(act, lambda smp, nxt: attention_turn(a, smp, nxt))

            def feed(phase):
                s = ph[phase]

                def first(nxt):
                    for c in range(CH):
                        modulated(phase, c, nxt)

                def turn(smp, nxt):
                    if phase == "f1":
                        for q in range(TT):
                            bank = g_bank("f1", f"s{q}")
                            act.wait_ge(full[bank], before("f1", bank, f"s{q}", smp) + 1)
                            act.wait_ge(read[bank], before("f1", bank, f"s{q}", smp))
                            act.activation(qs[:, q % 2, :], ps[bank][:, 0:E * DK], ACT.Copy).then_inc(s["qs"], 1)
                    logits, scale = (NMAP, 1.0) if phase == "f0" else (E, float(DK) ** -0.5)
                    act.wait_ge(s["lg"], smp.count(1, 1))
                    act.activation(lg[:, :, 0:logits], lg[:, :, 0:logits], ACT.Exp, scale=scale).then_inc(s["ex"], 1)
                    if nxt:
                        first(nxt)
                    bank = g_bank(phase, "w")
                    act.wait_ge(full[bank], before(phase, bank, "w", smp) + 1)
                    act.activation(oT[:, 1, :], ps[bank][:, :], ACT.Copy).then_inc(read[bank], 1)

                first(Sample(-1, 1))
                loop(act, turn)

            act.wait_ge(ld["c"], 32)
            act.activation(cE[:, :, :, :], cT[:, :, :, :], ACT.Exp, scale=-1.0).then_inc(s_silu_e, 1)
            act.wait_ge(ld["l0"], 16 * 6)
            act.wait_ge(read["M0"], SEED + 2)
            attention(A0)
            act.wait_ge(read["M0"], start("a0", "M0"))
            feed("f0")
            act.wait_ge(read["M0"], start("f0", "M0"))
            attention(A1)
            act.wait_ge(read["M0"], start("a1", "M0"))
            feed("f1")

        @block.vector
        def _(dve):
            def modulation_columns(layer, n):
                m, kind = mod_phase(layer, n), {0: 0, 1: 1, 3: 2, 4: 3}[n]
                dve.wait_ge(full["M0"], before(m, "M0", f"col{n}", ONCE) + 1)
                dve.tensor_scalar(cols[:, layer, kind * CH:(kind + 1) * CH, :],
                                  ps["M0"][:, 0:CH * NB].rearrange("p (c b) -> p c b", c=CH), float(kind % 2), None, ALU.add)\
                    .then_inc(read["M0"], 1)

            def bounded_gate(layer, n):
                m, done = mod_phase(layer, n), (2 * layer + n // 3) * 5
                dve.wait_ge(full["M1"], before(m, "M1", f"gate{n}", ONCE) + 1)
                if done:
                    dve.wait_ge(ld["gates"], 16 * (done // 5))
                dve.tensor_copy(grow, ps["M1"][0:NB, :]).then_inc(read["M1"], 1)
                dve.wait_ge(read["M1"], before(m, "M1", f"gate{n}", ONCE) + 1)
                dve.tensor_scalar(gabs, grow, -1.0, None, ALU.mult).then_inc(s_gate, 1)
                dve.tensor_scalar(gsign, grow, 0.0, 2.0, ALU.is_ge, ALU.mult).then_inc(s_gate, 1)
                dve.wait_ge(s_gate, done + 2)
                dve.tensor_tensor(gabs, gabs, grow, ALU.max).then_inc(s_gate, 1)
                dve.wait_ge(s_gate, done + 3)
                dve.tensor_scalar(gabs, gabs, GATE_MIN, None, ALU.max).then_inc(s_gate, 1)
                dve.wait_ge(s_gate, done + 4)
                dve.scalar_tensor_tensor(out=gabs, in0=gsign, scalar=-1.0, in1=gabs,
                                         op0=ALU.add, op1=ALU.mult).then_inc(s_gate, 1)

            def tile_statistics(phase, q, smp):
                dve.bn_stats(st[:, q, :], xt(smp, q)).then_inc(ph[phase]["bn"], 1)

            def sample_statistics(phase, smp):
                wait_alone(dve, ph[phase]["bn"], smp.count(TT, TT))
                for q in range(TT):
                    dve.bn_aggr(mv[:, q, :], st[:, q, :]).then_inc(ph[phase]["stats"], 1)

            def tile_normalised(phase, q, smp):
                dve.wait_ge(ph[phase]["rstd"], smp.count(1, 1))
                dve.tensor_scalar(xn[:, q, None, :], xt(smp, q), mv[:, q, 0:1], rstd[:, q:q + 1],
                                  ALU.subtract, ALU.mult).then_inc(ph[phase]["xn"], 1)

            def normalise(phase, smp):
                for q in range(TT):
                    tile_statistics(phase, q, smp)
                sample_statistics(phase, smp)
                for q in range(TT):
                    tile_normalised(phase, q, smp)

            def low_part(a, job, smp):
                bank = g_bank(a.name, job)
                dve.wait_ge(ph[a.name]["high"], before(a.name, "high", job, smp) + 1)
                if a.rep == 1 and job == "q0":
                    dve.scalar_tensor_tensor(out=partL[:, 0, :], in0=ps[bank][:, :], scalar=bqk[:, 0:1],
                                             in1=partR[:, 0, :].bitcast(F32), op0=ALU.add, op1=ALU.subtract)\
                        .then_inc(read[bank], 1)
                    return
                if job == "k":
                    dst, high = kL[:, :], kR[:, :]
                elif job[0] == "m":
                    dst, high = ml[0:a.heads, :], mh[0:a.heads, :]
                else:
                    dst, high = partL[:, int(job[1]) % 2, :], partR[:, int(job[1]) % 2, :]
                dve.tensor_tensor(dst, ps[bank][0:dst.shape[0], :], high.bitcast(F32), ALU.subtract).then_inc(read[bank], 1)

            def values(a, smp):
                bank = g_bank(a.name, "v")
                dve.wait_ge(full[bank], before(a.name, bank, "v", smp) + 1)
                src = ps[bank][:, 0:TT * a.vch].rearrange("p (t h d) -> p t h d", t=TT, d=a.hd)
                dst = V[:, :, :, 0:a.hd]
                if a is A0:
                    dve.tensor_tensor(dst, src, bv[:, None, :].rearrange("p a (h d) -> p a h d", d=a.hd)
                                      .to_broadcast([P, TT, a.kv, a.hd]), ALU.add).then_inc(read[bank], 1)
                else:
                    dve.tensor_copy(dst, src).then_inc(read[bank], 1)

            def maxima(a, step, smp, nxt=None):
                for i in range(a.jobs):
                    n = step * a.jobs + i
                    h, qt = i // TT, i % TT
                    bank = f"M{n % 2}"
                    dve.wait_ge(full[bank], before(a.name, bank, n, smp) + 1)
                    dve.tensor_reduce(mcol[:, step % 2, qt, h:h + 1], ps[bank][:, 0:(qt + 1) * P if a.causal else N],
                                      AX.X, ALU.max, negate=True).then_inc(read[bank], 1)
                    if nxt:
                        if i < TT:
                            tile_statistics(a.name, i, nxt)
                        elif i == TT:
                            sample_statistics(a.name, nxt)
                        elif i >= a.jobs - TT:
                            tile_normalised(a.name, i - (a.jobs - TT), nxt)

            def heads_normalised(a, n, smp):
                s = ph[a.name]
                bank = g_bank(a.name, f"o{n}")
                dve.wait_ge(full[bank], before(a.name, bank, f"o{n}", smp) + 1)
                v = ps[bank][:, :].rearrange("p (t i w) -> p t i w", t=TT, i=4)
                dve.reciprocal(rs[:, n % 2, :, :], v[:, :, :, a.hd]).then_inc(s["rs"], 1)
                dve.wait_ge(s["rs"], smp.count(a.steps * a.nq, n + 1))
                dst = on[:, :, n * 4 * a.hd:(n + 1) * 4 * a.hd].rearrange("p t (i w) -> p t i w", i=4)
                dve.tensor_tensor(dst, v[:, :, :, 0:a.hd], rs[:, n % 2, :, :, None].to_broadcast([P, TT, 4, a.hd]), ALU.mult)\
                    .then_inc(read[bank], 1)

            def output_tile(phase, q, bias, smp):
                s = ph[phase]
                bank, job = output_bank(phase, q)
                if q == 0:
                    wait_alone(dve, ld["gate"], smp.count(16, 16 * (gate_turn[phase] + 1)))
                dve.wait_ge(full[bank], before(phase, bank, job, smp) + 1)
                dve.wait_ge(s["xadd"], smp.count(TT, SEED + max(q - 1, 0)))
                if bias is None:
                    dve.tensor_tensor(tile2[:, q % 2, :], ps[bank][:, :], gate[:, :], ALU.mult).then_inc(read[bank], 1)
                    return
                dve.tensor_tensor(tile2[:, q % 2, :], ps[bank][:, :], bias, ALU.add).then_inc(read[bank], 1)
                dve.wait_ge(read[bank], before(phase, bank, job, smp) + 1)
                dve.tensor_tensor(tile2[:, q % 2, :], tile2[:, q % 2, :], gate[:, :], ALU.mult).then_inc(s["gated"], 1)

            def fill_values(a):
                done = 2 * (a is A1)
                dve.memset(V[:, :, :, :], 0.0).then_inc(s_vfill, 1)
                dve.wait_ge(s_vfill, done + 1)
                dve.memset(V[:, :, :, a.hd], a.ones).then_inc(s_vfill, 1)
                dve.wait_ge(s_vfill, done + 2)

            def attention_job(a, j, bias, smp):
                if j[0] in "kqm":
                    low_part(a, j, smp)
                elif j[0] == "v":
                    values(a, smp)
                elif j[0] == "o":
                    heads_normalised(a, int(j[1]), smp)
                elif j[0] == "y":
                    output_tile(a.name, int(j[1]), bias, smp)

            def first_normalised(phase, prev):
                dve.wait_ge(ph[prev]["xadd"], SEED + TT)
                normalise(phase, Sample(-1, 1))

            def attention_turn(a, bias, smp, nxt, onward):
                for step in range(a.steps):
                    here = nxt if step == a.turn_step else None
                    if step + 1 < a.steps:
                        maxima(a, step + 1, smp, here)
                    elif nxt:
                        maxima(a, 0, nxt, here)
                    else:
                        first_normalised(onward, a.name)
                    for j in a.after[step]:
                        if j[-1] != "'":
                            attention_job(a, j, bias, smp)
                        elif nxt:
                            attention_job(a, j[:-1], bias, nxt)

            def attention_loop(a, bias, onward):
                loop(dve, lambda smp, nxt: attention_turn(a, bias, smp, nxt, onward))

            def expert_weights0(smp):
                s = ph["f0"]
                S = 9

                def after(n):
                    dve.wait_ge(s["step"], smp.count(S, n))

                dve.wait_ge(s["ar"], smp.count(1, 1))
                ar = VV[:, :, 0:2 * (E * R + NMAP)].rearrange("p k (j n) -> p k j n", j=2)
                dve.tensor_tensor(lg[:, :, 0:NMAP].rearrange("p (k j) n -> p k j n", k=2), ar[:, :, :, E * R:],
                                  brout[:, None, None, :].to_broadcast([P, 2, 2, NMAP]), ALU.add).then_inc(s["step"], 1)
                after(1)
                dve.tensor_reduce(lmax[:, :], lg[:, :, 0:NMAP], AX.X, ALU.max).then_inc(s["step"], 1)
                after(2)
                dve.tensor_tensor(lg[:, :, 0:NMAP], lg[:, :, 0:NMAP], lmax[:, :, None].to_broadcast([P, TT, NMAP]),
                                  ALU.subtract).then_inc(s["lg"], 1)
                dve.wait_ge(s["ex"], smp.count(1, 1))
                dve.tensor_reduce(lsum[:, :], lg[:, :, 0:NMAP], AX.X, ALU.add).then_inc(s["step"], 1)
                for q in range(TT):
                    ins = dve.max(top[:, q, :], lg[:, q, 0:NMAP])
                ins.then_inc(s["step"], 1)
                after(4)
                dve.reciprocal(lrec[:, :], lsum[:, :]).then_inc(s["step"], 1)
                for q in range(TT):
                    ins = dve.match_replace(out=rest[:, q, 0:NMAP], in_to_replace=top[:, q, :],
                                            in_values=lg[:, q, 0:NMAP], imm_value=0.0)
                ins.then_inc(s["step"], 1)
                after(6)
                dve.tensor_tensor(sel[:, :, 0:NMAP], lg[:, :, 0:NMAP], rest[:, :, 0:NMAP], ALU.subtract).then_inc(s["step"], 1)
                after(7)
                dve.tensor_tensor(wsel[:, :, :, :], sel[:, :, None, 0:NMAP].to_broadcast([P, TT, E, NMAP]),
                                  onehot[:, None, :, :].to_broadcast([P, TT, E, NMAP]), ALU.mult).then_inc(s["step"], 1)
                after(8)
                dve.tensor_reduce(wexp[:, :, :], wsel[:, :, :, :], AX.X, ALU.add).then_inc(s["step"], 1)
                after(9)
                for q in range(TT):
                    h = ar[:, q // 2, q % 2, 0:E * R].rearrange("p (e r) -> p e r", e=E)
                    ins = dve.scalar_tensor_tensor(out=hw[:, q, :].rearrange("p (e r) -> p e r", e=E), in0=h,
                                                   scalar=lrec[:, q:q + 1],
                                                   in1=wexp[:, q, :, None].to_broadcast([P, E, R]),
                                                   op0=ALU.mult, op1=ALU.mult)
                ins.then_inc(read["V0"], 1)

            def expert_weights1(smp):
                s = ph["f1"]
                S = 8

                def after(n):
                    dve.wait_ge(s["step"], smp.count(S, n))

                for q in range(TT):
                    bank = g_bank("f1", f"s{q}")
                    dve.wait_ge(s["qs"], smp.count(TT, q + 1))
                    dve.tensor_tensor(qk[:, q % 2, :], ps[bank][:, E * DK:2 * E * DK], qs[:, q % 2, :], ALU.mult)\
                        .then_inc(read[bank], 1)
                    dve.wait_ge(read[bank], before("f1", bank, f"s{q}", smp) + 1)
                    dve.tensor_reduce(lg[:, q, 0:E], qk[:, q % 2, :].rearrange("p (e d) -> p e d", e=E), AX.X, ALU.add)\
                        .then_inc(s["step"], 1)
                    after(q + 1)
                dve.tensor_reduce(lmax[:, :], lg[:, :, 0:E], AX.X, ALU.max).then_inc(s["step"], 1)
                after(5)
                dve.tensor_tensor(lg[:, :, 0:E], lg[:, :, 0:E], lmax[:, :, None].to_broadcast([P, TT, E]),
                                  ALU.subtract).then_inc(s["lg"], 1)
                dve.wait_ge(s["ex"], smp.count(1, 1))
                dve.tensor_reduce(lsum[:, :], lg[:, :, 0:E], AX.X, ALU.add).then_inc(s["step"], 1)
                after(6)
                dve.reciprocal(lrec[:, :], lsum[:, :]).then_inc(s["step"], 1)
                after(7)
                dve.tensor_tensor(wexp[:, :, :], lg[:, :, 0:E], lrec[:, :, None].to_broadcast([P, TT, E]), ALU.mult)\
                    .then_inc(s["step"], 1)
                after(8)
                dve.wait_ge(s["ar"], smp.count(1, 1))
                dve.tensor_tensor(hw[:, :, :].rearrange("p t (e r) -> p (t e) r", e=E),
                                  ps["V0"].rearrange("p (u r) -> p u r", r=R),
                                  wexp[:, :, :].rearrange("p t e -> p (t e)")[:, :, None].to_broadcast([P, TT * E, R]),
                                  ALU.mult).then_inc(read["V0"], 1)

            def feed(phase, prev, weights, bias, onward):
                def turn(smp, nxt):
                    weights(smp)
                    if nxt:
                        dve.wait_ge(ph[prev]["xadd"], nxt.count(TT, SEED + TT))
                        normalise(phase, nxt)
                    elif onward:
                        first_normalised(onward, phase)
                    for q in range(TT):
                        output_tile(phase, q, bias, smp)

                loop(dve, turn)

            dve.wait_ge(s_silu_e, 1)
            dve.tensor_scalar(cE[:, :, :, :], cE[:, :, :, :], 1.0, None, ALU.add).then_inc(s_silu, 1)
            dve.wait_ge(s_silu, 1)
            dve.reciprocal(cE[:, :, :, :], cE[:, :, :, :]).then_inc(s_silu, 1)
            dve.wait_ge(s_silu, 2)
            dve.tensor_tensor(cT[:, :, :, :], cT[:, :, :, :], cE[:, :, :, :], ALU.mult).then_inc(s_silu, 1)
            dve.wait_ge(s_const, 6)
            dve.tensor_copy(identb[:, :], ident[:, :]).then_inc(s_constd, 1)
            dve.tensor_copy(maskb[:, :], maskf[:, :]).then_inc(s_constd, 1)

            def first_sample(a, bias):
                smp = Sample(-1, 1)
                for j in a.first:
                    attention_job(a, j, bias, smp)
                modulation_rest(int(a.name[1]))
                maxima(a, 0, smp)
                for j in a.second:
                    attention_job(a, j, bias, smp)

            def modulation_rest(layer):
                for n in (3, 4):
                    modulation_columns(layer, n)
                for n in (2, 5):
                    bounded_gate(layer, n)

            for n in (0, 1):
                modulation_columns(0, n)
            dve.wait_ge(ld["l0"], 16 * 6)
            dve.wait_ge(ld["x0"], 16)
            fill_values(A0)
            normalise("a0", Sample(-1, 1))
            first_sample(A0, bo[:, :])
            dve.wait_ge(ld["x"], 16 * (NB - 1))
            attention_loop(A0, bo[:, :], "f0")
            for n in (0, 1):
                modulation_columns(1, n)
            dve.wait_ge(ld["l0f"], 16 * 6)
            dve.tensor_copy(emapf[:, :], emap[:, :]).then_inc(s_constd, 1)
            dve.wait_ge(s_constd, 3)
            for e in range(E):
                dve.tensor_scalar(onehot[:, e, :], emapf[:, :], float(e), LORA_SCALE0, ALU.is_equal, ALU.mult)\
                    .then_inc(s_constd, 1)
            dve.wait_ge(s_constd, 3 + E)
            feed("f0", "a0", expert_weights0, bbase[:, :], "a1")
            fill_values(A1)
            first_sample(A1, None)
            dve.wait_ge(ph["f0"]["xadd"], SEED + NB * TT)
            attention_loop(A1, None, "f1")
            dve.wait_ge(ld["l1f"], 16 * 5)
            feed("f1", "a1", expert_weights1, bo[:, :], None)

        @block.tensor
        def _(pe):
            def modulation_columns(layer, n):
                m = mod_phase(layer, n)
                pe.wait_ge(ld_wmod[n], 16 * (layer + 1))
                pe.wait_ge(read["M0"], before(m, "M0", f"col{n}", ONCE))
                w = wmod_at[layer][n]
                for o in range(CH):
                    for c in range(CH):
                        mm = pe.matmul(ps["M0"][:, o * NB:(o + 1) * NB], w[:, c, o * P:(o + 1) * P], cT[:, layer, c, :],
                                       start=(c == 0), stop=(c == CH - 1))
                mm.then_inc(full["M0"], 1)

            def modulation_gate(layer, n):
                m = mod_phase(layer, n)
                pe.wait_ge(ld_wmod[n], 16 * (layer + 1))
                pe.wait_ge(read["M1"], before(m, "M1", f"gate{n}", ONCE))
                for c in range(CH):
                    mm = pe.matmul(ps["M1"][0:NB, :], cT[:, layer, c, :], wmod_at[layer][n][:, c, :],
                                   start=(c == 0), stop=(c == CH - 1))
                mm.then_inc(full["M1"], 1)

            def turned(phase, c, smp):
                if c == 0:
                    pe.wait_ge(ph[phase]["xn"], smp.count(TT, TT))
                bank = g_bank(phase, f"t{c}")
                pe.wait_ge(read[bank], before(phase, bank, f"t{c}", smp))
                for q in range(TT):
                    mm = pe.transpose(ps[bank][:, q * P:(q + 1) * P], xn[:, q, c * P:(c + 1) * P], ident[:, :])
                mm.then_inc(full[bank], 1)

            def hT_ready(phase, smp):
                for c in range(CH - 2, CH):
                    bank = g_bank(phase, f"t{c}")
                    pe.wait_ge(read[bank], before(phase, bank, f"t{c}", smp) + 1)

            def project(a, job, w, smp):
                bank = g_bank(a.name, job)
                pe.wait_ge(read[bank], before(a.name, bank, job, smp))
                for c in range(CH):
                    mm = pe.matmul(ps[bank][:, :], w[:, c, :], hT[:, c, :], start=(c == 0), stop=(c == CH - 1))
                mm.then_inc(full[bank], 1)

            def project_values(a, w, smp):
                bank = g_bank(a.name, "v")
                pe.wait_ge(read[bank], before(a.name, bank, "v", smp))
                for q in range(TT):
                    for c in range(CH):
                        mm = pe.matmul(ps[bank][:, q * a.vch:(q + 1) * a.vch], hT[:, c, q * P:(q + 1) * P], w[:, c, :],
                                       start=(c == 0), stop=(c == CH - 1))
                mm.then_inc(full[bank], 1)

            def query_major(a, step, i, smp):
                n = step * a.jobs + i
                h, qt = i // TT, i % TT
                kh = step * a.khs + h // a.rep
                slot = step if a.rep == 1 else step * 4 + h % a.rep
                bank = f"M{n % 2}"
                if i == 0:
                    pe.wait_ge(ph[a.name][f"qstack{step}"], smp.count(a.qdma, SEED + a.qdma))
                if i == 0 or a.rep == 1 and i % TT == 0:
                    group = kh if a.rep == 1 else step // 2
                    pe.wait_ge(ph[a.name][f"kstack{group}"], smp.count(a.kdma, SEED + a.kdma))
                pe.wait_ge(read[bank], before(a.name, bank, n, smp))
                cols_ = max(MIN_R, (qt + 1) * P) if a.causal else N
                mm = pe.matmul(ps[bank][:, 0:cols_], QS[0:MROW, slot, qt * P:(qt + 1) * P], KS[0:MROW, kh, 0:cols_],
                               start=True, stop=not a.causal)
                if a.causal:
                    mm = pe.matmul(ps[bank][:, qt * P:(qt + 1) * P], identb[:, :], maskb[:, :], start=False, stop=True)
                mm.then_inc(full[bank], 1)

            def maxima_turned(a, step, smp):
                for n in (step * a.jobs + a.jobs - 2, step * a.jobs + a.jobs - 1):
                    pe.wait_ge(read[f"M{n % 2}"], before(a.name, f"M{n % 2}", n, smp) + 1)
                bank = g_bank(a.name, f"m{step}")
                pe.wait_ge(read[bank], before(a.name, bank, f"m{step}", smp))
                for q in range(TT):
                    mm = pe.transpose(ps[bank][0:a.heads, q * P:(q + 1) * P], mcol[:, step % 2, q, 0:a.heads], ident[:, :])
                mm.then_inc(full[bank], 1)

            def key_major(a, step, i, smp):
                n = step * a.jobs + i
                g = i // 4
                r, k = a.quads[g // TT][i % 4]
                kt = g % TT
                kh = step * a.khs + k
                slot = step if a.rep == 1 else step * 4 + r
                q0 = min(kt * P, N - MIN_R) if a.causal else 0
                bank = f"E{n % 2}"
                if i == 0:
                    pe.wait_ge(ph[a.name]["mstack"], smp.count(a.steps * a.mdma, (step + 1) * a.mdma + SEED))
                pe.wait_ge(read[bank], before(a.name, bank, n, smp))
                pe.matmul(ps[bank][:, q0:N], KS[:, kh, kt * P:(kt + 1) * P], QS[:, slot, q0:N],
                          start=True, stop=True).then_inc(full[bank], 1)

            def value_product(a, step, gi, smp):
                g = step * a.nq * TT + gi
                kt = gi % TT
                quad = step * a.nq + gi // TT
                q0 = kt * P if a.causal else 0
                bank = f"V{quad % 2}"
                if g == 0:
                    b_ = g_bank(a.name, "v")
                    pe.wait_ge(read[b_], turn_start(a.name, b_, smp))
                for n in (4 * g + 2, 4 * g + 3):
                    pe.wait_ge(read[f"E{n % 2}"], before(a.name, f"E{n % 2}", n, smp) + 1)
                if a.causal:
                    pe.wait_ge(ph[a.name][f"pd{g % 2}"], smp.count(a.groups // 2, g // 2 + 1))
                if kt == 0:
                    pe.wait_ge(read[bank], before(a.name, bank, quad, smp))
                for i, (_, k) in enumerate(a.quads[gi // TT]):
                    mm = pe.matmul(ps[bank][32 * i:32 * i + 32, q0:N], V[:, kt, step * a.khs + k, :],
                                   PR[:, g % 2, i, q0:N], start=(kt == 0), stop=(kt == TT - 1))
                mm.then_inc(ph[a.name][f"pv{g % 2}"], 1)

            def heads_turned(a, n, smp):
                bank = g_bank(a.name, f"o{n}")
                pe.wait_ge(read[f"V{n % 2}"], before(a.name, f"V{n % 2}", n, smp) + 1)
                pe.wait_ge(read[bank], before(a.name, bank, f"o{n}", smp))
                for q in range(TT):
                    mm = pe.transpose(ps[bank][:, q * P:(q + 1) * P], tile2[:, n % 2, q * P:(q + 1) * P], ident[:, :])
                mm.then_inc(full[bank], 1)

            def outputs_turned(a, c, smp):
                if c == 0:
                    for n in (a.steps * a.nq - 2, a.steps * a.nq - 1):
                        bank = g_bank(a.name, f"o{n}")
                        wait_alone(pe, read[bank], before(a.name, bank, f"o{n}", smp) + 1)
                bank = g_bank(a.name, f"c{c}")
                wait_alone(pe, read[bank], before(a.name, bank, f"c{c}", smp))
                for q in range(TT):
                    mm = pe.transpose(ps[bank][0:a.orows, q * P:(q + 1) * P], on[:, q, c * P:c * P + a.orows], ident[:, :])
                mm.then_inc(full[bank], 1)

            def output(a, q, w, smp):
                if q == 0:
                    for c in range(a.oc):
                        bank = g_bank(a.name, f"c{c}")
                        pe.wait_ge(read[bank], before(a.name, bank, f"c{c}", smp) + 1)
                bank = g_bank(a.name, f"y{q}")
                pe.wait_ge(read[bank], before(a.name, bank, f"y{q}", smp))
                for c in range(a.oc):
                    rhs = w[:, :] if a.oc == 1 else w[:, c, :]
                    mm = pe.matmul(ps[bank][:, :], oT[0:a.orows, c, q * P:(q + 1) * P], rhs,
                                   start=(c == 0), stop=(c == a.oc - 1))
                mm.then_inc(full[bank], 1)

            def job(a, j, w, smp):
                kind, n = j[0], int(j[1:] or 0)
                if kind == "t":
                    turned(a.name, n, smp)
                    if n == CH - 1:
                        hT_ready(a.name, smp)
                elif kind == "k":
                    project(a, j, w["k"], smp)
                elif kind == "q":
                    project(a, j, w["q"][:, :, n * P:(n + 1) * P], smp)
                elif kind == "v":
                    project_values(a, w["v"], smp)
                elif kind == "m":
                    maxima_turned(a, n, smp)
                elif kind == "o":
                    heads_turned(a, n, smp)
                elif kind == "c":
                    outputs_turned(a, n, smp)
                elif kind == "y":
                    output(a, n, w["o"], smp)

            def first_sample(a, w):
                smp = Sample(-1, 1)
                for j in a.first:
                    job(a, j, w, smp)
                modulation_rest(int(a.name[1]))
                for i in range(a.jobs):
                    query_major(a, 0, i, smp)
                for j in a.second:
                    job(a, j, w, smp)

            def attention_turn(a, w, smp, nxt):
                for step in range(a.steps):
                    lag = 0
                    if step + 1 < a.steps:
                        after_step, after_smp = step + 1, smp
                    else:
                        after_step, after_smp, lag = 0, nxt, a.lag
                    for i in range(a.jobs + lag):
                        if i < a.jobs:
                            key_major(a, step, i, smp)
                        if after_smp and i >= lag:
                            query_major(a, after_step, i - lag, after_smp)
                        if i % 4 == 3 and 4 < i < a.jobs:
                            value_product(a, step, i // 4 - 1, smp)
                        if lag and i == a.jobs:
                            value_product(a, step, a.jobs // 4 - 1, smp)
                    if not lag:
                        value_product(a, step, a.jobs // 4 - 1, smp)
                    for j in a.after[step]:
                        if j[-1] != "'":
                            job(a, j, w, smp)
                        elif nxt:
                            job(a, j[:-1], w, nxt)

            def attention_loop(a, w):
                loop(pe, lambda smp, nxt: attention_turn(a, w, smp, nxt))

            def feed(phase):
                def first(nxt):
                    for c in range(CH):
                        turned(phase, c, nxt)

                def turn(smp, nxt):
                    for bank in ("G0", "G1"):
                        pe.wait_ge(read[bank], turn_start(phase, bank, smp))
                    pe.wait_ge(read["V0"], before(phase, "V0", "ar", smp))
                    for q in range(TT):
                        if phase == "f0":
                            dst, w = VV[:, q // 2, (q % 2) * (E * R + NMAP):(q % 2 + 1) * (E * R + NMAP)], war
                        else:
                            dst, w = VV[:, 0, q * E * R:(q + 1) * E * R], wA1
                        for c in range(CH):
                            mm = pe.matmul(dst, hT[:, c, q * P:(q + 1) * P], w[:, c, :], start=(c == 0), stop=(c == CH - 1))
                    mm.then_inc(ph[phase]["ar"], 1)
                    if phase == "f1":
                        for q in range(TT):
                            bank = g_bank(phase, f"s{q}")
                            pe.wait_ge(read[bank], before(phase, bank, f"s{q}", smp))
                            for c in range(CH):
                                mm = pe.matmul(ps[bank][:, :], hT[:, c, q * P:(q + 1) * P], wQK[:, c, :],
                                               start=(c == 0), stop=(c == CH - 1))
                            mm.then_inc(full[bank], 1)
                    for q in range(TT):
                        pe.wait_ge(read[XB[q]], before(phase, XB[q], "y", smp))
                        for c in range(CH):
                            pe.matmul(ps[XB[q]][:, :], hT[:, c, q * P:(q + 1) * P], wbase[:, c, :], start=(c == 0), stop=False)
                    if nxt:
                        first(nxt)
                    bank = g_bank(phase, "w")
                    pe.wait_ge(read["V0"], before(phase, "V0", "ar", smp) + 1)
                    pe.wait_ge(read[bank], before(phase, bank, "w", smp))
                    for q in range(TT):
                        mm = pe.transpose(ps[bank][:, q * P:(q + 1) * P], hw[:, q, :], ident[:, :])
                    mm.then_inc(full[bank], 1)
                    pe.wait_ge(read[bank], before(phase, bank, "w", smp) + 1)
                    for q in range(TT):
                        pe.matmul(ps[XB[q]][:, :], hwT[:, q, :], wB[:, :], start=False, stop=True).then_inc(full[XB[q]], 1)

                first(Sample(-1, 1))
                loop(pe, turn)

            def modulation_rest(layer):
                for n in (3, 4):
                    modulation_columns(layer, n)
                for n in (2, 5):
                    modulation_gate(layer, n)

            pe.wait_ge(s_silu, 3)
            pe.wait_ge(s_const, 5)
            pe.wait_ge(s_constd, 2)
            for n in (0, 1):
                modulation_columns(0, n)
            pe.wait_ge(ld["l0"], 16 * 6)
            pe.wait_ge(s_vfill, 2)
            w0 = {"q": wqk0, "v": wv0, "o": wo0}
            first_sample(A0, w0)
            attention_loop(A0, w0)
            pe.wait_ge(ld["l0f"], 16 * 6)
            for n in (0, 1):
                modulation_columns(1, n)
            feed("f0")
            pe.wait_ge(s_vfill, 4)
            w1 = {"k": wk1, "v": wv1, "q": wq1, "o": wo1}
            pe.wait_ge(ld["l1"], 16 * 3)
            first_sample(A1, w1)
            pe.wait_ge(ld["l1"], 16 * 4)
            attention_loop(A1, w1)
            pe.wait_ge(ld["l1f"], 16 * 5)
            feed("f1")


def kernel(**inputs):
    import numpy as np
    import concourse.bacc as bacc
    from concourse import mybir as mb
    from concourse.bass_utils import run_bass_kernel_spmd

    g = {k: np.asarray(v) for k, v in inputs.items()}
    kv, rep, hd = A1.kv, A1.rep, A1.hd
    wqk = g["L0_attn_Wqk_w"].reshape(64, 2, D).transpose(1, 0, 2).reshape(128, D)
    bqk = g["L0_attn_Wqk_b"].reshape(64, 2).T.reshape(128)
    wq = g["L1_attn_wq"].reshape(D, A1.steps, A1.khs, rep, hd).transpose(0, 1, 2, 4, 3).reshape(D, kv * rep * hd)
    wk = g["L1_attn_wk"].reshape(D, 2, 2, A1.khs, hd).transpose(0, 1, 3, 4, 2).reshape(D, kv * hd)
    data = {
        "x": g["L0_attn_x"],
        "c0": g["L0_c"].T, "c1": g["L1_c"].T, "wmod0": g["L0_wmod"], "wmod1": g["L1_wmod"],
        "wqk0": wqk.T, "bqk0": bqk, "wv0": g["L0_attn_Wv_w"].T, "bv0": g["L0_attn_Wv_b"],
        "wo0": g["L0_attn_Wo_w"].T, "bo0": g["L0_attn_Wo_b"],
        "wbase": g["L0_ffn_base_W"].T, "bbase": g["L0_ffn_base_b"],
        "war": np.concatenate([g["L0_ffn_A"].reshape(E * R, D).T, g["L0_ffn_router_W"].T], axis=1),
        "brout": g["L0_ffn_router_b"],
        "wB0": g["L0_ffn_B"].transpose(0, 2, 1).reshape(E * R, D),
        "emap": g["L0_ffn_expert_map"],
        "wq1": wq, "wk1": wk, "wv1": g["L1_attn_wv"], "wo1": g["L1_attn_wo"],
        "wW1": g["L1_ffn_W"].T, "b1": g["L1_ffn_b"],
        "wQK1": np.concatenate([g["L1_ffn_Wq"].T, g["L1_ffn_Wk"].T], axis=1),
        "wA1": g["L1_ffn_A"].reshape(E * R, D).T,
        "wB1": g["L1_ffn_Bm"].transpose(0, 2, 1).reshape(E * R, D),
    }
    nc = bacc.Bacc("TRN2", target_bir_lowering=False, num_devices=1)
    arrays, t = {}, {}
    for name, a in data.items():
        a = np.ascontiguousarray(a)
        arrays[f"in_{name}"] = a
        t[name] = nc.dram_tensor(f"in_{name}", a.shape, mb.dt.from_np(a.dtype), kind="ExternalInput").ap()
    t["out"] = nc.dram_tensor("out", (NB, N, D), F32, kind="ExternalOutput").ap()
    build(nc, t)
    r = run_bass_kernel_spmd(nc, [arrays], core_ids=[0])
    return r.results[0]["out"]
```

```python
import concourse.bass as bass
from concourse import mybir
from contextlib import ExitStack

F32 = mybir.dt.float32
F32R = mybir.dt.float32r
BF16 = mybir.dt.bfloat16
I32 = mybir.dt.int32
ALU = mybir.AluOpType
ACT = mybir.ActivationFunctionType
AX = mybir.AxisListType

P = 128
D = 512
NB = 4
N = 512
TT = N // P
CH = D // P
EPS = 1e-5
GATE_MIN = 0.25
NEG = -1e30
NMAP = 15
E = 8
R = 16
DK = 32
LORA_SCALE0 = 32.0 / 16.0
MROW = 96
SEED = 1
MIN_R = 256


class Attn:

    def __init__(self, name, hd, kv, rep, steps, causal, scale, ones):
        self.name, self.hd, self.kv, self.rep, self.steps = name, hd, kv, rep, steps
        self.causal, self.scale, self.ones = causal, scale, ones
        self.khs = kv // steps
        self.heads = self.khs * rep
        if rep == 1:
            self.quads = [[(0, k) for k in range(self.khs)]]
        else:
            self.quads = [[(r, k) for r in range(rep)] for k in range(self.khs)]
        self.nq = len(self.quads)
        self.jobs = self.heads * TT
        self.groups = steps * self.nq * TT
        self.vch = kv * hd
        self.och = kv * rep * hd
        self.oc = max(1, self.och // P)
        self.orows = min(P, self.och)
        self.kgroups = kv if rep == 1 else 2
        self.kdma = 16 * 3 * (1 if rep == 1 else self.khs)
        self.qdma = 16 * 3
        self.mdma = 16 * 2
        last = [f"c{c}" for c in range(self.oc)] + [f"y{q}" for q in range(TT)]
        if rep == 1:
            self.after = [["m1", "t0'", "t1'", "o0", "t2'", "t3'", "q0'", "v'"], ["m0'", "o1", "w'"] + last]
            self.lag = 4
        else:
            self.after = [["m1", "q3", "o0", "o1"],
                          ["m2", "t0'", "t1'", "t2'", "t3'", "k'", "o2", "o3", "v'"],
                          ["m3", "q0'", "q1'", "o4", "o5"],
                          ["m0'", "o6", "o7", "w'", "q2'", "c0", "c1", "c2", "c3"] + last[self.oc:]]
            self.lag = 0
        self.ahead = [j[:-1] for jobs in self.after for j in jobs if j[-1] == "'"]
        first = self.ahead.index("m0")
        self.first, self.second = self.ahead[:first], self.ahead[first:]
        self.mod_after = [1 + i * self.jobs // 8 for i in range(6)]
        gap = self.jobs // 8
        self.stats_after = [q * gap for q in range(TT)]
        self.norm_after = [self.jobs - 1 - (TT - 1 - q) * (gap - (rep == 1)) for q in range(TT)]
        self.turn_step = 0 if rep == 1 else 1


A0 = Attn("a0", 8, 8, 1, 2, False, 1.0, 8.0)
A1 = Attn("a1", 16, 8, 4, 4, True, 16.0 ** -0.5, 1.0)

XB = ["M0", "M1", "E0", "E1"]
BANKS = XB + ["V0", "V1", "G0", "G1"]
AFTER_BANKS = ["G0", "G1", "M0", "M1"]
PHASES = ["mod0", "a0", "mod1a", "f0", "mod1b", "a1", "f1"]
TURNS = {"mod0": 1, "mod1a": 1, "mod1b": 1, "a0": NB, "a1": NB, "f0": NB, "f1": NB}


MOD_FIRST = [("row", 0), ("row", 1), ("col", 0), ("col", 1)]
MOD_REST = [("row", 3), ("row", 4), ("col", 3), ("row", 2), ("col", 4), ("row", 5)]
MOD_PLACE = {0: 0, 1: 1, 3: 0, 4: 1, 2: 0, 5: 1}


def mod_phase(layer, n):
    return "mod0" if layer == 0 else "mod1a" if n < 2 else "mod1b"


def score_job(a, kind, n):
    turn = n % a.jobs % 3
    if kind == "e":
        return ("E0", "E1", "G1")[turn], f"e{n}"
    return ("M0", "M1", "G0")[turn], f"x{n}"


def last_jobs(a, kind, n):
    return [score_job(a, kind, m) for m in range(n - 2, n + 1)]


def job_tables():
    uses = {p: {k: [] for k in BANKS + ["high"]} for p in PHASES}
    for layer in (0, 1):
        for kind, n in MOD_FIRST + MOD_REST:
            uses[mod_phase(layer, n)]["E0" if kind == "row" else "E1"].append(f"{kind}{n}")
    for a in (A0, A1):
        count = 0
        for step in range(a.steps):
            following = (step + 1) % a.steps
            prime = "" if following else "'"
            for i in range(a.jobs):
                bank, job = score_job(a, "e", step * a.jobs + i)
                uses[a.name][bank].append(job)
                bank, job = score_job(a, "x", following * a.jobs + i)
                uses[a.name][bank].append(job + prime)
            for j in a.after[step]:
                uses[a.name][AFTER_BANKS[count % 4]].append(j)
                count += 1
                if j[0] in "kqm":
                    uses[a.name]["high"].append(j)
        for i in range(a.steps * a.nq):
            uses[a.name][f"V{i % 2}"].append(i)
    for f in ("f0", "f1"):
        tiles = [f"s{q}" for q in range(TT)] if f == "f1" else []
        for i, j in enumerate(tiles + ["w"] + [f"t{c}'" for c in range(CH)]):
            uses[f][f"G{i % 2}"].append(j)
        for q in range(TT):
            uses[f][XB[q]].append("y")
        uses[f]["V0"].append("ar")
    return uses


USES = job_tables()


class Sample:

    def __init__(self, turn, ahead=0):
        self.turn, self.ahead = turn, ahead

    def count(self, per, more):
        if isinstance(self.turn, int):
            return (self.turn + self.ahead) * per + more
        return self.turn * per + (self.ahead * per + more)


def loop(eng, turn):
    with eng.Fori(0, NB - 1) as b:
        turn(Sample(b), Sample(b, 1))
    turn(Sample(NB - 1), None)


ONCE = Sample(0)


def start(phase, bank):
    return SEED + sum(TURNS[p] * len(USES[p][bank]) for p in PHASES[:PHASES.index(phase)])


def before(phase, bank, job, smp):
    jobs = USES[phase][bank]
    base = 0 if bank == "high" else start(phase, bank)
    ahead = [j for j in jobs if str(j)[-1] == "'"]
    if not ahead:
        return smp.count(len(jobs), base + jobs.index(job))
    if isinstance(smp.turn, int) and smp.turn < 0:
        return base + ahead.index(job + "'")
    if smp.ahead:
        job += "'"
    if isinstance(smp.turn, int):
        jobs_here = [j for j in jobs if j not in ahead]
        return base + len(ahead) + smp.turn * len(jobs) + jobs_here.index(job)
    return smp.turn * len(jobs) + (base + len(ahead) + jobs.index(job))


def turn_start(phase, bank, smp):
    jobs = USES[phase][bank]
    return smp.count(len(jobs), start(phase, bank) + len([j for j in jobs if j[-1] == "'"]))


def g_bank(phase, job):
    for bank in AFTER_BANKS:
        if job in USES[phase][bank] or job + "'" in USES[phase][bank]:
            return bank


def output_bank(phase, q):
    return (g_bank(phase, f"y{q}"), f"y{q}") if phase[0] == "a" else (XB[q], "y")


def build(nc, t):
    with ExitStack() as ctx:
        def sb(name, shape, dt=F32):
            return ctx.enter_context(nc.sbuf_tensor(name, shape, dt))

        def sem(name):
            return ctx.enter_context(nc.semaphore(name))

        x = sb("x", [P, NB * TT, D])
        xn = sb("xn", [P, TT, D])
        on = sb("on", [P, TT, D])
        hT = sb("hT", [P, CH, N])
        QS = sb("QS", [P, 16, N], F32R)
        KS = sb("KS", [P, 8, N], F32R)
        V = sb("V", [P, TT, 8, 32])
        PR = sb("PR", [P, 2, 4, N])
        partR = sb("partR", [P, 2, N], F32R)
        partL = sb("partL", [P, 2, N], F32R)
        kR = sb("kR", [P, N], F32R)
        kL = sb("kL", [P, N], F32R)
        tile2 = sb("tile2", [P, 2, D])
        oT = sb("oT", [P, CH, N])
        gate = sb("gate", [P, D])
        vT = sb("vT", [P, N])

        wqk0 = sb("wqk0", [P, CH, P])
        wv0 = sb("wv0", [P, CH, A0.vch])
        wo0 = sb("wo0", [A0.och, D])
        wbase = sb("wbase", [P, CH, D])
        war = sb("war", [P, CH, E * R + NMAP])
        wB = sb("wB", [E * R, D])
        wq1 = sb("wq1", [P, CH, D])
        wk1 = sb("wk1", [P, CH, P])
        wv1 = sb("wv1", [P, CH, P])
        wo1 = sb("wo1", [P, CH, D])
        wQK, wA1 = wq1, wk1
        bqk = sb("bqk", [P, 1])
        bv = sb("bv", [P, A0.vch])
        bo = sb("bo", [P, D])
        bbase = sb("bbase", [P, D])
        brout = sb("brout", [P, NMAP])
        emap = sb("emap", [P, NMAP], I32)
        emapf = sb("emapf", [P, NMAP])
        onehot = sb("onehot", [P, E, NMAP])

        ident = sb("ident", [P, P])
        identb = sb("identb", [P, P], BF16)
        maskf = sb("maskf", [P, P])
        maskb = sb("maskb", [P, P], BF16)
        padc = sb("padc", [P, 2, 8])
        half = sb("half", [P, TT])
        cT = sb("cT", [P, 2, CH, NB])
        cE = sb("cE", [P, 2, CH, NB])
        cols = sb("cols", [P, 2, 4 * CH, NB])
        st = sb("st", [P, TT, 6])
        mv = sb("mv", [P, TT, 2])
        vareps = sb("vareps", [P, TT])
        rstd = sb("rstd", [P, TT])
        mcol = sb("mcol", [P, 2, TT, 8])
        mh = sb("mh", [8, N], F32R)
        ml = sb("ml", [8, N], F32R)
        rs = sb("rs", [P, 2, TT, 4])
        lg = sb("lg", [P, TT, 16])
        lmax = sb("lmax", [P, TT])
        top = sb("top", [P, TT, 8])
        rest = sb("rest", [P, TT, 16])
        sel = sb("sel", [P, TT, 16])
        lsum = sb("lsum", [P, TT])
        lrec = sb("lrec", [P, TT])
        wsel = sb("wsel", [P, TT, E, NMAP])
        wexp = sb("wexp", [P, TT, E])
        modrow = oT[0:NB, 0:2, :]
        bounded = oT[0:NB, 2:4, :]
        hw = oT[:, 0, :].rearrange("p (t n) -> p t n", t=TT)
        hwT = oT[:, 1, :].rearrange("p (t n) -> p t n", t=TT)
        qs = oT[:, 2, :].rearrange("p (a n) -> p a n", a=2)
        qk = oT[:, 3, :].rearrange("p (a n) -> p a n", a=2)

        gates_dram = nc.dram_tensor("gates_scratch", (2, 2, NB, D), F32).ap()

        ps = {k: ctx.enter_context(nc.psum_tensor(k, [P, 512], F32)) for k in XB + ["G0", "G1"]}
        VV = ctx.enter_context(nc.psum_tensor("VV", [P, 2, 512], F32))
        ps["V0"], ps["V1"] = VV[:, 0, :], VV[:, 1, :]

        full = {k: sem(f"full_{k}") for k in BANKS if k[0] != "V"}
        read = {k: sem(f"read_{k}") for k in BANKS}
        ld = {k: sem(f"ld_{k}") for k in ("c", "x0", "x", "l0", "l0f", "l1", "l1f", "gates", "gate", "out")}
        ld_wmod = [sem(f"ld_wmod{n}") for n in range(6)]
        s_const = sem("s_const")
        s_constd = sem("s_constd")
        w_high = sem("w_high")
        w_low = sem("w_low")
        s_pad = sem("s_pad")
        s_apart = sem("s_apart")
        s_silu = sem("s_silu")
        s_silu_e = sem("s_silu_e")
        s_gate = sem("s_gate")
        s_vfill = sem("s_vfill")
        ph = {}
        for p in ("a0", "f0", "a1", "f1"):
            names = ["bn", "stats", "vareps", "rstd", "xn", "gated", "xadd"]
            if p[0] == "a":
                names += ["high", "mstack", "rs", "pd0", "pd1", "pv0", "pv1"]
                a = A0 if p == "a0" else A1
                names += [f"qstack{n}" for n in range(a.steps)] + [f"kstack{n}" for n in range(a.kgroups)]
            else:
                names += ["step", "lg", "ex", "qs", "ar", "high", "low"]
            ph[p] = {n: sem(f"{p}_{n}") for n in names}
        gate_turn = {"a0": 0, "f0": NB, "a1": 2 * NB, "f1": 3 * NB}

        block = ctx.enter_context(nc.Block())

        hTR, hTL = KS[:, 0:CH, :], KS[:, CH:2 * CH, :]
        wide = {"f0": [wbase], "f1": [wbase, wQK]}
        parts = [(QS[:, 2 * CH * i:2 * CH * i + CH, :], QS[:, 2 * CH * i + CH:2 * CH * (i + 1), :]) for i in range(2)]
        made_parts = {"f0": CH, "f1": 3 * CH}

        wmod_at = [[PR[:, 0, :, :], PR[:, 1, :, :], wq1[:, :, :], wo1[:, :, :], wbase[:, :, :], on[:, :, :]],
                   [wq1[:, :, :], wo1[:, :, :], on[:, :, :], PR[:, 0, :, :], PR[:, 1, :, :], wo1[:, :, :]]]

        def xt(smp, q, k=1):
            return x[:, bass.ds(smp.count(TT, q), k), :]

        def wait_alone(eng, s, value):
            eng.wait_ge(s, value)
            eng.sem_inc(s_apart, 1)

        @block.sync
        def _(sp):
            def chunks(w):
                return w.rearrange("(c p) n -> p c n", p=P)

            def row_to_all(dst, v, s):
                sp.dma_start(dst, v.rearrange("(a n) -> a n", a=1).to_broadcast([P, v.shape[0]])).then_inc(s, 16)

            def load_wmod(layer, n):
                sp.dma_start(wmod_at[layer][n], chunks(t[f"wmod{layer}"])[:, :, n * D:(n + 1) * D]).then_inc(ld_wmod[n], 16)

            def store_gate(layer, which):
                sp.wait_ge(s_gate, (2 * layer + which) * 5 + 5)
                sp.dma_start(gates_dram[layer, which], bounded[:, which, :]).then_inc(ld["gates"], 16)

            def load_gate(layer, which, smp, phase):
                wait_alone(sp, ph[phase]["xadd"], smp.count(TT, SEED))
                sp.dma_start(gate[:, :], gates_dram[layer, which, bass.ds(smp.count(1, 0), 1), :].to_broadcast([P, D]))\
                    .then_inc(ld["gate"], 16)

            def move(dst, src, s):
                sp.dma_start(dst.bitcast(F32), src.bitcast(F32)).then_inc(s, 16)

            def stack_maxima(a, step, smp):
                bank = g_bank(a.name, f"m{step}")
                sp.wait_ge(read[bank], before(a.name, bank, f"m{step}", smp) + 1)
                for row, part in ((MROW, mh), (MROW + a.khs, ml)):
                    move(QS[row:row + a.khs, step * a.rep:(step + 1) * a.rep, :], part[0:a.heads, :], ph[a.name]["mstack"])

            def stack_step0(step):
                for rows, part in ((0, partR), (32, partR), (64, partL)):
                    move(QS[rows:rows + 32, step, :], part[32 * step:32 * step + 32, 0, :], ph["a0"][f"qstack{step}"])
                for h in range(A0.khs * step, A0.khs * step + A0.khs):
                    for rows, part in ((0, partR), (32, partL), (64, partR)):
                        row, src = rows + A0.hd * (h % A0.khs), 64 + A0.hd * h
                        move(KS[row:row + A0.hd, h, :], part[src:src + A0.hd, 0, :], ph["a0"][f"kstack{h}"])

            def projection_split(phase, job, smp):
                bank = g_bank(phase, job)
                sp.wait_ge(read[bank], before(phase, bank, job, smp) + 1)

            def first0(nxt):
                projection_split("a0", "q0", nxt)
                stack_step0(0)
                stack_step0(1)
                store_gate(0, 0)
                store_gate(0, 1)
                stack_maxima(A0, 0, nxt)

            def turn0(smp, nxt):
                stack_maxima(A0, 1, smp)
                load_gate(0, 0, smp, "a0")
                if nxt:
                    projection_split("a0", "q0", nxt)
                    stack_step0(0)
                    stack_maxima(A0, 0, nxt)
                    stack_step0(1)

            def stack_queries(step, smp):
                projection_split("a1", f"q{step}", smp)
                for rows, part in ((0, partR), (32, partR), (64, partL)):
                    move(QS[rows:rows + 32, step * A1.rep:(step + 1) * A1.rep, :], part[:, step % 2, :], ph["a1"][f"qstack{step}"])

            def stack_keys(half):
                for parity in range(A1.khs):
                    first = 4 * half + parity
                    src = 64 * half + 32 * parity
                    for rows, part in ((0, kR), (32, kL), (64, kR)):
                        row = rows + A1.hd * parity
                        move(KS[row:row + A1.hd, first:first + 3:2, :], part[src:src + 32, :], ph["a1"][f"kstack{half}"])

            def first1(nxt):
                projection_split("a1", "k", nxt)
                stack_keys(0)
                stack_queries(0, nxt)
                stack_queries(1, nxt)
                stack_keys(1)
                sp.wait_ge(full["E0"], start("a1", "E0"))
                sp.dma_start(wo1[:, :, :], chunks(t["wo1"])).then_inc(ld["l1"], 16)
                store_gate(1, 0)
                store_gate(1, 1)
                stack_maxima(A1, 0, nxt)
                stack_queries(2, nxt)

            def turn1(smp, nxt):
                stack_maxima(A1, 1, smp)
                stack_queries(3, smp)
                stack_maxima(A1, 2, smp)
                load_gate(1, 0, smp, "a1")
                if nxt:
                    projection_split("a1", "k", nxt)
                    stack_keys(0)
                else:
                    for dst, src in ((wQK, "wQK1"), (wA1, "wA1")):
                        sp.dma_start(dst[:, :, :], chunks(t[src])).then_inc(ld["l1f"], 16)
                stack_maxima(A1, 3, smp)
                if nxt:
                    stack_queries(0, nxt)
                    stack_queries(1, nxt)
                    stack_maxima(A1, 0, nxt)
                    stack_keys(1)
                    stack_queries(2, nxt)

            seeded = [*full.values(), *read.values()]
            for p in ("a0", "f0", "a1", "f1"):
                seeded += [ph[p][n] for n in ph[p] if n in ("xadd", "mstack", "pv0", "pv1") or n[1:6] == "stack"]
            for s_ in seeded:
                sp.sem_inc(s_, SEED)
            for layer in (0, 1):
                sp.dma_start(cT[:, layer, :, :], t[f"c{layer}"].rearrange("(c p) b -> p c b", p=P)).then_inc(ld["c"], 16)
            def load_x(b, s):
                sp.dma_start(x[:, b * TT:(b + 1) * TT, :], t["x"][b].rearrange("(t p) d -> p t d", p=P)).then_inc(ld[s], 16)

            load_x(0, "x0")
            load_wmod(0, 0)
            load_wmod(0, 1)
            sp.dma_start(wqk0[:, :, :], chunks(t["wqk0"])).then_inc(ld["l0"], 16)
            sp.dma_start(bqk[:, :], t["bqk0"].rearrange("(p a) -> p a", a=1)).then_inc(ld["l0"], 16)
            sp.dma_start(wv0[:, :, :], chunks(t["wv0"])).then_inc(ld["l0"], 16)
            sp.dma_start(wo0[:, :], t["wo0"]).then_inc(ld["l0"], 16)
            row_to_all(bv[:, :], t["bv0"], ld["l0"])
            row_to_all(bo[:, :], t["bo0"], ld["l0"])
            for n in range(2, 6):
                load_wmod(0, n)
            for b in range(1, NB):
                load_x(b, "x")
            sp.dma_start(war[:, :, :], chunks(t["war"])).then_inc(ld["l0f"], 16)
            sp.dma_start(wB[:, :], t["wB0"]).then_inc(ld["l0f"], 16)
            row_to_all(bbase[:, :], t["bbase"], ld["l0f"])
            row_to_all(brout[:, :], t["brout"], ld["l0f"])
            row_to_all(emap[:, :], t["emap"], ld["l0f"])
            sp.wait_ge(s_pad, 2)
            first0(Sample(-1, 1))
            sp.dma_start(wbase[:, :, :], chunks(t["wbase"])).then_inc(ld["l0f"], 16)
            for n in (0, 1):
                load_wmod(1, n)
            sp.wait_ge(ld["gates"], 32)
            loop(sp, turn0)
            sp.wait_ge(full["E1"], start("mod1a", "E1"))
            for parity in range(2):
                sp.wait_ge(ph["a0"][f"pv{parity}"], SEED + NB * A0.groups // 2)
            sp.wait_ge(ph["a0"]["xadd"], SEED + NB * TT)
            with sp.Fori(0, 1) as b:
                load_gate(0, 1, Sample(b), "f0")
            for n in (3, 4, 2):
                load_wmod(1, n)
            sp.wait_ge(full["E0"], start("f0", "E0"))
            for dst, src in ((wk1, "wk1"), (wv1, "wv1"), (wq1, "wq1")):
                sp.dma_start(dst[:, :, :], chunks(t[src])).then_inc(ld["l1"], 16)
            load_wmod(1, 5)
            with sp.Fori(0, NB - 1) as b:
                load_gate(0, 1, Sample(b, 1), "f0")
            sp.wait_ge(ph["f0"]["xadd"], SEED + NB * TT)
            sp.dma_start(wbase[:, :, :], chunks(t["wW1"])).then_inc(ld["l1f"], 16)
            sp.dma_start(wB[:, :], t["wB1"]).then_inc(ld["l1f"], 16)
            row_to_all(bo[:, :], t["b1"], ld["l1f"])
            sp.wait_ge(s_pad, 2 + KS.shape[1])
            first1(Sample(-1, 1))
            sp.wait_ge(ld["gates"], 64)
            sp.wait_ge(ph["f0"]["xadd"], SEED + NB * TT)
            loop(sp, turn1)
            sp.wait_ge(ph["a1"]["xadd"], SEED + NB * TT)
            with sp.Fori(0, NB) as b:
                smp = Sample(b)
                load_gate(1, 1, smp, "f1")
                wait_alone(sp, ph["f1"]["xadd"], smp.count(TT, SEED + TT))
                sp.dma_start(t["out"][bass.ds(b, 1), :, :].rearrange("a (t p) d -> p (a t) d", p=P),
                             xt(smp, 0, TT)).then_inc(ld["out"], 16)
            sp.wait_ge(ld["out"], 16 * NB)

        @block.gpsimd
        def _(gp):
            for dst, value in ((ident[:, :], 0.0), (maskf[:, :], 0.0), (padc[:, :, :], 0.0), (half[:, :], -0.5)):
                gp.memset(dst, value).then_inc(s_const, 1)
            gp.wait_ge(s_const, 4)
            gp.affine_select(out=ident[:, :], in_=ident[:, :], compare_op=ALU.not_equal, fill=1.0, base=0,
                             pattern=[[-1, P]], channel_multiplier=1).then_inc(s_const, 1)
            gp.affine_select(out=maskf[:, :], in_=maskf[:, :], compare_op=ALU.is_ge, fill=NEG, base=0,
                             pattern=[[-1, P]], channel_multiplier=1).then_inc(s_const, 1)
            made = 6
            for layer, a in ((0, A0), (1, A1)):
                for row in (MROW, MROW + a.khs):
                    v = padc[:, layer, :].rearrange("p (g k) -> p g k", k=a.khs)
                    gp.affine_select(out=v, in_=v, compare_op=ALU.not_equal, fill=1.0, base=-row,
                                     pattern=[[0, a.steps], [-1, a.khs]], channel_multiplier=1).then_inc(s_const, 1)
                    made += 1
                    gp.wait_ge(s_const, made)

            def reciprocal_deviation(s, smp):
                wait_alone(gp, s["stats"], smp.count(TT, TT))
                gp.tensor_scalar(vareps[:, :], mv[:, :, 1], EPS, None, ALU.add).then_inc(s["vareps"], 1)
                gp.wait_ge(s["vareps"], smp.count(1, 1))
                gp.tensor_tensor(rstd[:, :], vareps[:, :], half[:, :], ALU.pow).then_inc(s["rstd"], 1)

            def residual(phase, smp):
                s = ph[phase]
                for q in range(TT):
                    bank, job = output_bank(phase, q)
                    if phase == "a1":
                        wait_alone(gp, read[bank], before(phase, bank, job, smp) + 1)
                    else:
                        wait_alone(gp, s["gated"], smp.count(TT, q + 1))
                    gp.tensor_tensor(xt(smp, q), xt(smp, q), tile2[:, q % 2, None, :], ALU.add).then_inc(s["xadd"], 1)

            def mask_group(g, smp):
                kt = g % TT
                for bank, job in last_jobs(A1, "e", 4 * g + 3):
                    wait_alone(gp, read[bank], before("a1", bank, job, smp) + 1)
                v = PR[:, g % 2, :, kt * P:(kt + 1) * P]
                gp.affine_select(out=v, in_=v, compare_op=ALU.is_ge, fill=0.0, base=0,
                                 pattern=[[0, 4], [1, P]], channel_multiplier=-1).then_inc(ph["a1"][f"pd{g % 2}"], 1)

            def low_parts(phase, smp):
                for c in range(CH):
                    wait_alone(gp, ph[phase]["high"], smp.count(CH, c + 1))
                    gp.tensor_tensor(hTL[:, c, :], hT[:, c, :], hTR[:, c, :].bitcast(F32), ALU.subtract)\
                        .then_inc(ph[phase]["low"], 1)

            def turn(phase, onward):
                def one(smp, nxt):
                    if nxt:
                        reciprocal_deviation(ph[phase], nxt)
                    elif onward:
                        reciprocal_deviation(ph[onward], Sample(-1, 1))
                    if nxt and phase[0] == "f":
                        low_parts(phase, nxt)
                    residual(phase, smp)
                return one

            def turn1(smp, nxt):
                each = A1.nq * TT
                for g in range(A1.groups):
                    if nxt and g == A1.turn_step * each + each // 2 - 1:
                        reciprocal_deviation(ph["a1"], nxt)
                    if not nxt and g == (A1.steps - 1) * each + 1:
                        reciprocal_deviation(ph["f1"], Sample(-1, 1))
                    mask_group(g, smp)
                residual("a1", smp)

            reciprocal_deviation(ph["a0"], Sample(-1, 1))
            gp.wait_ge(ph["a0"]["rstd"], 1)
            gp.memset(QS[MROW:P, :, :].bitcast(F32), 0.0).then_inc(s_pad, 1)
            gp.wait_ge(s_pad, 1)
            gp.tensor_copy(KS[:, :, :], padc[:, 0, :, None].to_broadcast([P, 8, N])).then_inc(s_pad, 1)
            loop(gp, turn("a0", "f0"))
            low_parts("f0", Sample(-1, 1))
            loop(gp, turn("f0", "a1"))
            loop(gp, turn1)
            low_parts("f1", Sample(-1, 1))
            loop(gp, turn("f1", None))

        @block.scalar
        def _(act):
            def modulated(phase, c, smp):
                layer, kind = int(phase[1]), 2 * (phase[0] == "f")
                bank = g_bank(phase, f"t{c}")
                act.wait_ge(full[bank], before(phase, bank, f"t{c}", smp) + 1)
                b = smp.count(1, 0)
                act.activation(hT[:, c, :], ps[bank][:, :], ACT.Identity,
                               scale=cols[:, layer, (kind + 1) * CH + c, bass.ds(b, 1)],
                               bias=cols[:, layer, kind * CH + c, bass.ds(b, 1)]).then_inc(read[bank], 1)

            def high_part(a, job, smp):
                s = ph[a.name]
                if a.rep == 1:
                    for n in range(a.kgroups):
                        act.wait_ge(s[f"kstack{n}"], smp.count(a.kdma, SEED))
                    for n in range(a.steps):
                        act.wait_ge(s[f"qstack{n}"], smp.count(a.qdma, SEED))
                    dst, bias = partR[:, 0, :], bqk[:, 0:1]
                elif job == "k":
                    for n in range(a.kgroups):
                        act.wait_ge(s[f"kstack{n}"], smp.count(a.kdma, SEED))
                    dst, bias = kR[:, :], 0.0
                else:
                    step = int(job[1])
                    if step < 2:
                        act.wait_ge(s[f"qstack{step + 2}"], smp.count(a.qdma, SEED))
                    else:
                        act.wait_ge(s[f"qstack{step - 2}"], smp.count(a.qdma, SEED + a.qdma))
                    dst, bias = partR[:, step % 2, :], 0.0
                bank = g_bank(a.name, job)
                act.wait_ge(full[bank], before(a.name, bank, job, smp) + 1)
                act.activation(dst, ps[bank][:, :], ACT.Identity, bias=bias).then_inc(s["high"], 1)

            def max_high(a, step, smp):
                bank = g_bank(a.name, f"m{step}")
                act.wait_ge(full[bank], before(a.name, bank, f"m{step}", smp) + 1)
                act.wait_ge(ph[a.name]["mstack"], smp.count(a.steps * a.mdma, step * a.mdma + SEED))
                act.activation(mh[0:a.heads, :], ps[bank][0:a.heads, :], ACT.Copy).then_inc(ph[a.name]["high"], 1)

            def copy_out(a, n, smp):
                act.wait_ge(ph[a.name]["pv1"], smp.count(a.groups // 2, (n + 1) * TT // 2 + SEED))
                if n >= 2:
                    bank = g_bank(a.name, f"o{n - 2}")
                    act.wait_ge(full[bank], before(a.name, bank, f"o{n - 2}", smp) + 1)
                else:
                    act.wait_ge(ph[a.name]["xadd"], smp.count(TT, SEED))
                act.activation(tile2[:, n % 2, :], ps[f"V{n % 2}"], ACT.Copy).then_inc(read[f"V{n % 2}"], 1)

            def exp_step(a, step, smp):
                for i in range(a.jobs):
                    n = step * a.jobs + i
                    g = n // 4
                    q0 = (g % TT) * P if a.causal else 0
                    bank, tile = score_job(a, "e", n)
                    if n % 4 == 0:
                        act.wait_ge(ph[a.name][f"pv{g % 2}"], smp.count(a.groups // 2, g // 2 + SEED))
                    if i > 4 * TT and i % (4 * TT) == 4:
                        copy_out(a, step * a.nq + i // (4 * TT) - 1, smp)
                    act.wait_ge(full[bank], before(a.name, bank, tile, smp) + 1)
                    act.activation(PR[:, g % 2, n % 4, q0:N], ps[bank][:, q0:N], ACT.Exp, scale=a.scale)\
                        .then_inc(read[bank], 1)
                copy_out(a, step * a.nq + a.nq - 1, smp)

            def outputs_turned(a, c, smp):
                bank = g_bank(a.name, f"c{c}")
                act.wait_ge(full[bank], before(a.name, bank, f"c{c}", smp) + 1)
                act.activation(oT[0:a.orows, c, :], ps[bank][0:a.orows, :], ACT.Copy).then_inc(read[bank], 1)

            def job(a, j, smp):
                if j[0] == "t":
                    modulated(a.name, int(j[1]), smp)
                elif j[0] in "kq":
                    high_part(a, j, smp)
                elif j[0] == "m":
                    max_high(a, int(j[1]), smp)
                elif j[0] == "c":
                    outputs_turned(a, int(j[1]), smp)
                elif j[0] == "v":
                    bank = g_bank(a.name, "v")
                    act.wait_ge(full[bank], before(a.name, bank, "v", smp) + 1)
                    act.activation(vT[0:a.vch, :], ps[bank][0:a.vch, :], ACT.Copy).then_inc(read[bank], 1)

            def attention_turn(a, smp, nxt):
                for step in range(a.steps):
                    exp_step(a, step, smp)
                    for j in a.after[step]:
                        if j[-1] != "'":
                            job(a, j, smp)
                        elif nxt:
                            job(a, j[:-1], nxt)

            def attention(a):
                for j in a.ahead:
                    job(a, j, Sample(-1, 1))
                act.wait_ge(ld["gates"], 32 * (int(a.name[1]) + 1))
                loop(act, lambda smp, nxt: attention_turn(a, smp, nxt))

            def feed(phase):
                s = ph[phase]

                def first(nxt):
                    for c in range(CH):
                        modulated(phase, c, nxt)

                act.wait_ge(full["E1"], start("mod1a" if phase == "f0" else "f1", "E1"))
                if phase == "f0":
                    act.wait_ge(ld["l0f"], 16 * 6)
                else:
                    act.wait_ge(ld["l1f"], 16 * 5)
                for w, (high, _) in zip(wide[phase], parts):
                    for c in range(CH):
                        act.activation(high[:, c, :], w[:, c, :], ACT.Copy).then_inc(w_high, 1)

                def turn(smp, nxt):
                    if phase == "f1":
                        for q in range(TT):
                            bank = g_bank("f1", f"s{q}")
                            act.wait_ge(full[bank], before("f1", bank, f"s{q}", smp) + 1)
                            act.wait_ge(read[bank], before("f1", bank, f"s{q}", smp))
                            act.activation(qs[:, q % 2, :], ps[bank][:, 0:E * DK], ACT.Copy).then_inc(s["qs"], 1)
                    logits, scale = (NMAP, 1.0) if phase == "f0" else (E, float(DK) ** -0.5)
                    act.wait_ge(s["lg"], smp.count(1, 1))
                    act.activation(lg[:, :, 0:logits], lg[:, :, 0:logits], ACT.Exp, scale=scale).then_inc(s["ex"], 1)
                    bank = g_bank(phase, "w")
                    act.wait_ge(full[bank], before(phase, bank, "w", smp) + 1)
                    act.activation(oT[:, 1, :], ps[bank][:, :], ACT.Copy).then_inc(read[bank], 1)
                    if nxt:
                        first(nxt)
                    if phase == "f0" and not nxt:
                        for h in range(KS.shape[1]):
                            act.activation(KS[:, h, :], padc[:, 1, h:h + 1].to_broadcast([P, N]), ACT.Copy).then_inc(s_pad, 1)

                first(Sample(-1, 1))
                loop(act, turn)

            act.wait_ge(ld["c"], 32)
            act.activation(cE[:, :, :, :], cT[:, :, :, :], ACT.Exp, scale=-1.0).then_inc(s_silu_e, 1)
            act.wait_ge(ld["l0"], 16 * 6)
            act.wait_ge(read["E1"], SEED + 2)
            attention(A0)
            act.wait_ge(read["E1"], start("a0", "E1"))
            feed("f0")
            act.wait_ge(read["E1"], start("f0", "E1"))
            attention(A1)
            act.wait_ge(read["E1"], start("a1", "E1"))
            feed("f1")

        @block.vector
        def _(dve):
            def modulation_row(layer, n):
                m, place = mod_phase(layer, n), MOD_PLACE[n]
                row = modrow[:, place, :]
                dve.wait_ge(full["E0"], before(m, "E0", f"row{n}", ONCE) + 1)
                dve.tensor_scalar(row, ps["E0"][0:NB, :], 1.0 if n in (1, 4) else 0.0, None, ALU.add).then_inc(read["E0"], 1)
                if n not in (2, 5):
                    return
                g, done = bounded[:, n // 3, :], (2 * layer + n // 3) * 5
                dve.wait_ge(read["E0"], before(m, "E0", f"row{n}", ONCE) + 1)
                dve.tensor_scalar(g, row, -1.0, None, ALU.mult).then_inc(s_gate, 1)
                dve.wait_ge(s_gate, done + 1)
                dve.tensor_tensor(g, g, row, ALU.max).then_inc(s_gate, 1)
                dve.wait_ge(s_gate, done + 2)
                dve.tensor_scalar(g, g, GATE_MIN, None, ALU.max).then_inc(s_gate, 1)
                dve.tensor_scalar(row, row, 0.0, 2.0, ALU.is_ge, ALU.mult).then_inc(s_gate, 1)
                dve.wait_ge(s_gate, done + 4)
                dve.scalar_tensor_tensor(out=g, in0=row, scalar=-1.0, in1=g, op0=ALU.add, op1=ALU.mult).then_inc(s_gate, 1)

            def modulation_column(layer, n):
                m, kind = mod_phase(layer, n), {0: 0, 1: 1, 3: 2, 4: 3}[n]
                dve.wait_ge(full["E1"], before(m, "E1", f"col{n}", ONCE) + 1)
                dve.tensor_copy(cols[:, layer, kind * CH:(kind + 1) * CH, :],
                                ps["E1"][:, 0:CH * NB].rearrange("p (c b) -> p c b", c=CH)).then_inc(read["E1"], 1)

            def modulation(layer, kind, n):
                (modulation_row if kind == "row" else modulation_column)(layer, n)

            def tile_statistics(phase, q, smp):
                dve.bn_stats(st[:, q, :], xt(smp, q)).then_inc(ph[phase]["bn"], 1)

            def sample_statistics(phase, smp):
                wait_alone(dve, ph[phase]["bn"], smp.count(TT, TT))
                for q in range(TT):
                    dve.bn_aggr(mv[:, q, :], st[:, q, :]).then_inc(ph[phase]["stats"], 1)

            def tile_normalised(phase, q, smp):
                dve.wait_ge(ph[phase]["rstd"], smp.count(1, 1))
                dve.tensor_scalar(xn[:, q, None, :], xt(smp, q), mv[:, q, 0:1], rstd[:, q:q + 1],
                                  ALU.subtract, ALU.mult).then_inc(ph[phase]["xn"], 1)

            def normalise(phase, smp):
                for q in range(TT):
                    tile_statistics(phase, q, smp)
                sample_statistics(phase, smp)
                for q in range(TT):
                    tile_normalised(phase, q, smp)

            def low_part(a, job, smp):
                bank = g_bank(a.name, job)
                dve.wait_ge(ph[a.name]["high"], before(a.name, "high", job, smp) + 1)
                if a.rep == 1 and job == "q0":
                    dve.scalar_tensor_tensor(out=partL[:, 0, :], in0=ps[bank][:, :], scalar=bqk[:, 0:1],
                                             in1=partR[:, 0, :].bitcast(F32), op0=ALU.add, op1=ALU.subtract)\
                        .then_inc(read[bank], 1)
                    return
                if job == "k":
                    dst, high = kL[:, :], kR[:, :]
                elif job[0] == "m":
                    dst, high = ml[0:a.heads, :], mh[0:a.heads, :]
                else:
                    dst, high = partL[:, int(job[1]) % 2, :], partR[:, int(job[1]) % 2, :]
                dve.tensor_tensor(dst, ps[bank][0:dst.shape[0], :], high.bitcast(F32), ALU.subtract).then_inc(read[bank], 1)

            def values(a, smp):
                bank = g_bank(a.name, "w")
                dve.wait_ge(full[bank], before(a.name, bank, "w", smp) + 1)
                src = ps[bank][:, 0:TT * a.vch].rearrange("p (t h d) -> p t h d", t=TT, d=a.hd)
                dst = V[:, :, :, 0:a.hd]
                if a is A0:
                    dve.tensor_tensor(dst, src, bv[:, None, :].rearrange("p a (h d) -> p a h d", d=a.hd)
                                      .to_broadcast([P, TT, a.kv, a.hd]), ALU.add).then_inc(read[bank], 1)
                else:
                    dve.tensor_copy(dst, src).then_inc(read[bank], 1)

            def maxima(a, step, smp, nxt=None, between=None):
                for i in range(a.jobs):
                    n = step * a.jobs + i
                    h, qt = i // TT, i % TT
                    bank, tile = score_job(a, "x", n)
                    dve.wait_ge(full[bank], before(a.name, bank, tile, smp) + 1)
                    dve.tensor_reduce(mcol[:, step % 2, qt, h:h + 1], ps[bank][:, 0:(qt + 1) * P if a.causal else N],
                                      AX.X, ALU.max, negate=True).then_inc(read[bank], 1)
                    if between:
                        between(i)
                    if nxt:
                        if i in a.stats_after:
                            tile_statistics(a.name, a.stats_after.index(i), nxt)
                            if i == a.stats_after[-1]:
                                sample_statistics(a.name, nxt)
                        elif i in a.norm_after:
                            tile_normalised(a.name, a.norm_after.index(i), nxt)

            def heads_normalised(a, n, smp):
                s = ph[a.name]
                bank = g_bank(a.name, f"o{n}")
                dve.wait_ge(full[bank], before(a.name, bank, f"o{n}", smp) + 1)
                v = ps[bank][:, :].rearrange("p (t i w) -> p t i w", t=TT, i=4)
                dve.reciprocal(rs[:, n % 2, :, :], v[:, :, :, a.hd]).then_inc(s["rs"], 1)
                dve.wait_ge(s["rs"], smp.count(a.steps * a.nq, n + 1))
                dst = on[:, :, n * 4 * a.hd:(n + 1) * 4 * a.hd].rearrange("p t (i w) -> p t i w", i=4)
                dve.tensor_tensor(dst, v[:, :, :, 0:a.hd], rs[:, n % 2, :, :, None].to_broadcast([P, TT, 4, a.hd]), ALU.mult)\
                    .then_inc(read[bank], 1)

            def output_tile(phase, q, bias, smp):
                s = ph[phase]
                bank, job = output_bank(phase, q)
                if q == 0:
                    wait_alone(dve, ld["gate"], smp.count(16, 16 * (gate_turn[phase] + 1)))
                dve.wait_ge(full[bank], before(phase, bank, job, smp) + 1)
                dve.wait_ge(s["xadd"], smp.count(TT, SEED + max(q - 1, 0)))
                if bias is None:
                    dve.tensor_tensor(tile2[:, q % 2, :], ps[bank][:, :], gate[:, :], ALU.mult).then_inc(read[bank], 1)
                    return
                dve.tensor_tensor(tile2[:, q % 2, :], ps[bank][:, :], bias, ALU.add).then_inc(read[bank], 1)
                dve.wait_ge(read[bank], before(phase, bank, job, smp) + 1)
                dve.tensor_tensor(tile2[:, q % 2, :], tile2[:, q % 2, :], gate[:, :], ALU.mult).then_inc(s["gated"], 1)

            def fill_values(a):
                done = 2 * (a is A1)
                dve.memset(V[:, :, :, :], 0.0).then_inc(s_vfill, 1)
                dve.wait_ge(s_vfill, done + 1)
                dve.memset(V[:, :, :, a.hd], a.ones).then_inc(s_vfill, 1)
                dve.wait_ge(s_vfill, done + 2)

            def attention_job(a, j, bias, smp):
                if j[0] in "kqm":
                    low_part(a, j, smp)
                elif j[0] == "w":
                    values(a, smp)
                elif j[0] == "o":
                    heads_normalised(a, int(j[1]), smp)
                elif j[0] == "y":
                    output_tile(a.name, int(j[1]), bias, smp)

            def first_normalised(phase, prev):
                dve.wait_ge(ph[prev]["xadd"], SEED + TT)
                normalise(phase, Sample(-1, 1))

            def attention_turn(a, bias, smp, nxt, onward):
                for step in range(a.steps):
                    here = nxt if step == a.turn_step else None
                    if step + 1 < a.steps:
                        maxima(a, step + 1, smp, here)
                    elif nxt:
                        maxima(a, 0, nxt, here)
                    else:
                        first_normalised(onward, a.name)
                    for j in a.after[step]:
                        if j[-1] != "'":
                            attention_job(a, j, bias, smp)
                        elif nxt:
                            attention_job(a, j[:-1], bias, nxt)

            def attention_loop(a, bias, onward):
                loop(dve, lambda smp, nxt: attention_turn(a, bias, smp, nxt, onward))

            def expert_weights0(smp):
                s = ph["f0"]
                S = 9

                def after(n):
                    dve.wait_ge(s["step"], smp.count(S, n))

                dve.wait_ge(s["ar"], smp.count(1, 1))
                ar = VV[:, :, 0:2 * (E * R + NMAP)].rearrange("p k (j n) -> p k j n", j=2)
                dve.tensor_tensor(lg[:, :, 0:NMAP].rearrange("p (k j) n -> p k j n", k=2), ar[:, :, :, E * R:],
                                  brout[:, None, None, :].to_broadcast([P, 2, 2, NMAP]), ALU.add).then_inc(s["step"], 1)
                after(1)
                dve.tensor_reduce(lmax[:, :], lg[:, :, 0:NMAP], AX.X, ALU.max).then_inc(s["step"], 1)
                after(2)
                dve.tensor_tensor(lg[:, :, 0:NMAP], lg[:, :, 0:NMAP], lmax[:, :, None].to_broadcast([P, TT, NMAP]),
                                  ALU.subtract).then_inc(s["lg"], 1)
                dve.wait_ge(s["ex"], smp.count(1, 1))
                dve.tensor_reduce(lsum[:, :], lg[:, :, 0:NMAP], AX.X, ALU.add).then_inc(s["step"], 1)
                for q in range(TT):
                    ins = dve.max(top[:, q, :], lg[:, q, 0:NMAP])
                ins.then_inc(s["step"], 1)
                after(4)
                dve.reciprocal(lrec[:, :], lsum[:, :]).then_inc(s["step"], 1)
                for q in range(TT):
                    ins = dve.match_replace(out=rest[:, q, 0:NMAP], in_to_replace=top[:, q, :],
                                            in_values=lg[:, q, 0:NMAP], imm_value=0.0)
                ins.then_inc(s["step"], 1)
                after(6)
                dve.tensor_tensor(sel[:, :, 0:NMAP], lg[:, :, 0:NMAP], rest[:, :, 0:NMAP], ALU.subtract).then_inc(s["step"], 1)
                after(7)
                dve.tensor_tensor(wsel[:, :, :, :], sel[:, :, None, 0:NMAP].to_broadcast([P, TT, E, NMAP]),
                                  onehot[:, None, :, :].to_broadcast([P, TT, E, NMAP]), ALU.mult).then_inc(s["step"], 1)
                after(8)
                dve.tensor_reduce(wexp[:, :, :], wsel[:, :, :, :], AX.X, ALU.add).then_inc(s["step"], 1)
                after(9)
                for q in range(TT):
                    h = ar[:, q // 2, q % 2, 0:E * R].rearrange("p (e r) -> p e r", e=E)
                    ins = dve.scalar_tensor_tensor(out=hw[:, q, :].rearrange("p (e r) -> p e r", e=E), in0=h,
                                                   scalar=lrec[:, q:q + 1],
                                                   in1=wexp[:, q, :, None].to_broadcast([P, E, R]),
                                                   op0=ALU.mult, op1=ALU.mult)
                ins.then_inc(read["V0"], 1)

            def expert_weights1(smp):
                s = ph["f1"]
                S = 8

                def after(n):
                    dve.wait_ge(s["step"], smp.count(S, n))

                for q in range(TT):
                    bank = g_bank("f1", f"s{q}")
                    dve.wait_ge(s["qs"], smp.count(TT, q + 1))
                    dve.tensor_tensor(qk[:, q % 2, :], ps[bank][:, E * DK:2 * E * DK], qs[:, q % 2, :], ALU.mult)\
                        .then_inc(read[bank], 1)
                    dve.wait_ge(read[bank], before("f1", bank, f"s{q}", smp) + 1)
                    dve.tensor_reduce(lg[:, q, 0:E], qk[:, q % 2, :].rearrange("p (e d) -> p e d", e=E), AX.X, ALU.add)\
                        .then_inc(s["step"], 1)
                    after(q + 1)
                dve.tensor_reduce(lmax[:, :], lg[:, :, 0:E], AX.X, ALU.max).then_inc(s["step"], 1)
                after(5)
                dve.tensor_tensor(lg[:, :, 0:E], lg[:, :, 0:E], lmax[:, :, None].to_broadcast([P, TT, E]),
                                  ALU.subtract).then_inc(s["lg"], 1)
                dve.wait_ge(s["ex"], smp.count(1, 1))
                dve.tensor_reduce(lsum[:, :], lg[:, :, 0:E], AX.X, ALU.add).then_inc(s["step"], 1)
                after(6)
                dve.reciprocal(lrec[:, :], lsum[:, :]).then_inc(s["step"], 1)
                after(7)
                dve.tensor_tensor(wexp[:, :, :], lg[:, :, 0:E], lrec[:, :, None].to_broadcast([P, TT, E]), ALU.mult)\
                    .then_inc(s["step"], 1)
                after(8)
                dve.wait_ge(s["ar"], smp.count(1, 1))
                dve.tensor_tensor(hw[:, :, :].rearrange("p t (e r) -> p (t e) r", e=E),
                                  ps["V0"].rearrange("p (u r) -> p u r", r=R),
                                  wexp[:, :, :].rearrange("p t e -> p (t e)")[:, :, None].to_broadcast([P, TT * E, R]),
                                  ALU.mult).then_inc(read["V0"], 1)

            def high_parts(phase, smp):
                for c in range(CH):
                    bank = g_bank(phase, f"t{c}")
                    dve.wait_ge(read[bank], before(phase, bank, f"t{c}", smp) + 1)
                    dve.tensor_copy(hTR[:, c, :], hT[:, c, :]).then_inc(ph[phase]["high"], 1)

            def feed(phase, prev, weights, bias, onward):
                def turn(smp, nxt):
                    if nxt:
                        dve.wait_ge(ph[prev]["xadd"], nxt.count(TT, SEED + TT))
                        for q in range(TT):
                            tile_statistics(phase, q, nxt)
                        sample_statistics(phase, nxt)
                    weights(smp)
                    if nxt:
                        for q in range(TT):
                            tile_normalised(phase, q, nxt)
                        high_parts(phase, nxt)
                    elif onward:
                        first_normalised(onward, phase)
                    for q in range(TT):
                        output_tile(phase, q, bias, smp)

                high_parts(phase, Sample(-1, 1))
                for i, w in enumerate(wide[phase]):
                    high, low = parts[i]
                    for c in range(CH):
                        dve.wait_ge(w_high, made_parts[phase] - CH * len(wide[phase]) + CH * i + c + 1)
                        dve.tensor_tensor(low[:, c, :], w[:, c, :], high[:, c, :].bitcast(F32), ALU.subtract)\
                            .then_inc(w_low, 1)
                loop(dve, turn)

            dve.wait_ge(s_silu_e, 1)
            dve.tensor_scalar(cE[:, :, :, :], cE[:, :, :, :], 1.0, None, ALU.add).then_inc(s_silu, 1)
            dve.wait_ge(s_silu, 1)
            dve.reciprocal(cE[:, :, :, :], cE[:, :, :, :]).then_inc(s_silu, 1)
            dve.wait_ge(s_silu, 2)
            dve.tensor_tensor(cT[:, :, :, :], cT[:, :, :, :], cE[:, :, :, :], ALU.mult).then_inc(s_silu, 1)
            dve.wait_ge(s_const, 6)
            dve.tensor_copy(identb[:, :], ident[:, :]).then_inc(s_constd, 1)
            dve.tensor_copy(maskb[:, :], maskf[:, :]).then_inc(s_constd, 1)

            def first_sample(a, bias):
                smp = Sample(-1, 1)
                for j in a.first:
                    attention_job(a, j, bias, smp)
                maxima(a, 0, smp, between=lambda i: i in a.mod_after
                       and modulation(int(a.name[1]), *MOD_REST[a.mod_after.index(i)]))
                for j in a.second:
                    attention_job(a, j, bias, smp)

            fill_values(A0)
            dve.wait_ge(ld["x0"], 16)
            normalise("a0", Sample(-1, 1))
            for kind, n in MOD_FIRST:
                modulation(0, kind, n)
            dve.wait_ge(ld["l0"], 16 * 6)
            first_sample(A0, bo[:, :])
            dve.wait_ge(ld["x"], 16 * (NB - 1))
            attention_loop(A0, bo[:, :], "f0")
            for kind, n in MOD_FIRST:
                modulation(1, kind, n)
            dve.wait_ge(ld["l0f"], 16 * 6)
            dve.tensor_copy(emapf[:, :], emap[:, :]).then_inc(s_constd, 1)
            dve.wait_ge(s_constd, 3)
            for e in range(E):
                dve.tensor_scalar(onehot[:, e, :], emapf[:, :], float(e), LORA_SCALE0, ALU.is_equal, ALU.mult)\
                    .then_inc(s_constd, 1)
            dve.wait_ge(s_constd, 3 + E)
            feed("f0", "a0", expert_weights0, bbase[:, :], "a1")
            fill_values(A1)
            first_sample(A1, None)
            dve.wait_ge(ph["f0"]["xadd"], SEED + NB * TT)
            attention_loop(A1, None, "f1")
            dve.wait_ge(ld["l1f"], 16 * 5)
            feed("f1", "a1", expert_weights1, bo[:, :], None)

        @block.tensor
        def _(pe):
            def modulation(layer, kind, n):
                m = mod_phase(layer, n)
                if kind == "row":
                    pe.wait_ge(ld_wmod[n], 16 * (layer + 1))
                    pe.wait_ge(read["E0"], before(m, "E0", f"row{n}", ONCE))
                    for c in range(CH):
                        mm = pe.matmul(ps["E0"][0:NB, :], cT[:, layer, c, :], wmod_at[layer][n][:, c, :],
                                       start=(c == 0), stop=(c == CH - 1))
                    mm.then_inc(full["E0"], 1)
                else:
                    pe.wait_ge(read["E0"], before(m, "E0", f"row{n}", ONCE) + 1)
                    pe.wait_ge(read["E1"], before(m, "E1", f"col{n}", ONCE))
                    for c in range(CH):
                        mm = pe.transpose(ps["E1"][:, c * NB:(c + 1) * NB], modrow[:, MOD_PLACE[n], c * P:(c + 1) * P],
                                          ident[0:NB, 0:NB])
                    mm.then_inc(full["E1"], 1)

            def turned(phase, c, smp):
                if c == 0:
                    pe.wait_ge(ph[phase]["xn"], smp.count(TT, TT))
                bank = g_bank(phase, f"t{c}")
                pe.wait_ge(read[bank], before(phase, bank, f"t{c}", smp))
                for q in range(TT):
                    mm = pe.transpose(ps[bank][:, q * P:(q + 1) * P], xn[:, q, c * P:(c + 1) * P], ident[:, :])
                mm.then_inc(full[bank], 1)

            def hT_ready(phase, smp):
                for c in range(CH - 2, CH):
                    bank = g_bank(phase, f"t{c}")
                    pe.wait_ge(read[bank], before(phase, bank, f"t{c}", smp) + 1)

            def project(a, job, w, smp):
                bank = g_bank(a.name, job)
                pe.wait_ge(read[bank], before(a.name, bank, job, smp))
                for c in range(CH):
                    mm = pe.matmul(ps[bank][:, :], w[:, c, :], hT[:, c, :], start=(c == 0), stop=(c == CH - 1))
                mm.then_inc(full[bank], 1)

            def project_values(a, w, smp):
                bank = g_bank(a.name, "v")
                pe.wait_ge(read[bank], before(a.name, bank, "v", smp))
                for c in range(CH):
                    mm = pe.matmul(ps[bank][0:a.vch, :], w[:, c, :], hT[:, c, :], start=(c == 0), stop=(c == CH - 1))
                mm.then_inc(full[bank], 1)

            def values_turned(a, smp):
                bank = g_bank(a.name, "v")
                wait_alone(pe, read[bank], before(a.name, bank, "v", smp) + 1)
                bank = g_bank(a.name, "w")
                wait_alone(pe, read[bank], before(a.name, bank, "w", smp))
                for q in range(TT):
                    mm = pe.transpose(ps[bank][:, q * a.vch:(q + 1) * a.vch], vT[0:a.vch, q * P:(q + 1) * P],
                                      ident[0:a.vch, 0:a.vch])
                mm.then_inc(full[bank], 1)

            def query_major(a, step, i, smp):
                n = step * a.jobs + i
                h, qt = i // TT, i % TT
                kh = step * a.khs + h // a.rep
                slot = step if a.rep == 1 else step * 4 + h % a.rep
                bank, tile = score_job(a, "x", n)
                if i == 0:
                    pe.wait_ge(ph[a.name][f"qstack{step}"], smp.count(a.qdma, SEED + a.qdma))
                if i == 0 or a.rep == 1 and i % TT == 0:
                    group = kh if a.rep == 1 else step // 2
                    pe.wait_ge(ph[a.name][f"kstack{group}"], smp.count(a.kdma, SEED + a.kdma))
                pe.wait_ge(read[bank], before(a.name, bank, tile, smp))
                cols_ = max(MIN_R, (qt + 1) * P) if a.causal else N
                mm = pe.matmul(ps[bank][:, 0:cols_], QS[0:MROW, slot, qt * P:(qt + 1) * P], KS[0:MROW, kh, 0:cols_],
                               start=True, stop=not a.causal)
                if a.causal:
                    mm = pe.matmul(ps[bank][:, qt * P:(qt + 1) * P], identb[:, :], maskb[:, :], start=False, stop=True)
                mm.then_inc(full[bank], 1)

            def maxima_turned(a, step, smp):
                for bank, tile in last_jobs(a, "x", step * a.jobs + a.jobs - 1):
                    pe.wait_ge(read[bank], before(a.name, bank, tile, smp) + 1)
                bank = g_bank(a.name, f"m{step}")
                pe.wait_ge(read[bank], before(a.name, bank, f"m{step}", smp))
                for q in range(TT):
                    mm = pe.transpose(ps[bank][0:a.heads, q * P:(q + 1) * P], mcol[:, step % 2, q, 0:a.heads], ident[:, :])
                mm.then_inc(full[bank], 1)

            def key_major(a, step, i, smp):
                n = step * a.jobs + i
                g = i // 4
                r, k = a.quads[g // TT][i % 4]
                kt = g % TT
                kh = step * a.khs + k
                slot = step if a.rep == 1 else step * 4 + r
                q0 = min(kt * P, N - MIN_R) if a.causal else 0
                bank, tile = score_job(a, "e", n)
                if i == 0:
                    pe.wait_ge(ph[a.name]["mstack"], smp.count(a.steps * a.mdma, (step + 1) * a.mdma + SEED))
                pe.wait_ge(read[bank], before(a.name, bank, tile, smp))
                pe.matmul(ps[bank][:, q0:N], KS[:, kh, kt * P:(kt + 1) * P], QS[:, slot, q0:N],
                          start=True, stop=True).then_inc(full[bank], 1)

            def value_product(a, step, gi, smp):
                g = step * a.nq * TT + gi
                kt = gi % TT
                quad = step * a.nq + gi // TT
                q0 = kt * P if a.causal else 0
                if g == 0:
                    b_ = g_bank(a.name, "w")
                    pe.wait_ge(read[b_], turn_start(a.name, b_, smp))
                for bank, tile in last_jobs(a, "e", 4 * g + 3):
                    pe.wait_ge(read[bank], before(a.name, bank, tile, smp) + 1)
                bank = f"V{quad % 2}"
                if a.causal:
                    pe.wait_ge(ph[a.name][f"pd{g % 2}"], smp.count(a.groups // 2, g // 2 + 1))
                if kt == 0:
                    pe.wait_ge(read[bank], before(a.name, bank, quad, smp))
                for i, (_, k) in enumerate(a.quads[gi // TT]):
                    mm = pe.matmul(ps[bank][32 * i:32 * i + 32, q0:N], V[:, kt, step * a.khs + k, :],
                                   PR[:, g % 2, i, q0:N], start=(kt == 0), stop=(kt == TT - 1))
                mm.then_inc(ph[a.name][f"pv{g % 2}"], 1)

            def heads_turned(a, n, smp):
                bank = g_bank(a.name, f"o{n}")
                pe.wait_ge(read[f"V{n % 2}"], before(a.name, f"V{n % 2}", n, smp) + 1)
                pe.wait_ge(read[bank], before(a.name, bank, f"o{n}", smp))
                for q in range(TT):
                    mm = pe.transpose(ps[bank][:, q * P:(q + 1) * P], tile2[:, n % 2, q * P:(q + 1) * P], ident[:, :])
                mm.then_inc(full[bank], 1)

            def outputs_turned(a, c, smp):
                if c == 0:
                    for n in (a.steps * a.nq - 2, a.steps * a.nq - 1):
                        bank = g_bank(a.name, f"o{n}")
                        wait_alone(pe, read[bank], before(a.name, bank, f"o{n}", smp) + 1)
                bank = g_bank(a.name, f"c{c}")
                wait_alone(pe, read[bank], before(a.name, bank, f"c{c}", smp))
                for q in range(TT):
                    mm = pe.transpose(ps[bank][0:a.orows, q * P:(q + 1) * P], on[:, q, c * P:c * P + a.orows], ident[:, :])
                mm.then_inc(full[bank], 1)

            def output(a, q, w, smp):
                if q == 0 and a is A1:
                    pe.wait_ge(ld["l1"], 16 * 4)
                if q == 0:
                    for c in range(a.oc):
                        bank = g_bank(a.name, f"c{c}")
                        pe.wait_ge(read[bank], before(a.name, bank, f"c{c}", smp) + 1)
                bank = g_bank(a.name, f"y{q}")
                pe.wait_ge(read[bank], before(a.name, bank, f"y{q}", smp))
                for c in range(a.oc):
                    rhs = w[:, :] if a.oc == 1 else w[:, c, :]
                    mm = pe.matmul(ps[bank][:, :], oT[0:a.orows, c, q * P:(q + 1) * P], rhs,
                                   start=(c == 0), stop=(c == a.oc - 1))
                mm.then_inc(full[bank], 1)

            def job(a, j, w, smp):
                kind, n = j[0], int(j[1:] or 0)
                if kind == "t":
                    turned(a.name, n, smp)
                    if n == CH - 1:
                        hT_ready(a.name, smp)
                elif kind == "k":
                    project(a, j, w["k"], smp)
                elif kind == "q":
                    project(a, j, w["q"][:, :, n * P:(n + 1) * P], smp)
                elif kind == "v":
                    project_values(a, w["v"], smp)
                elif kind == "w":
                    values_turned(a, smp)
                elif kind == "m":
                    maxima_turned(a, n, smp)
                elif kind == "o":
                    heads_turned(a, n, smp)
                elif kind == "c":
                    outputs_turned(a, n, smp)
                elif kind == "y":
                    output(a, n, w["o"], smp)

            def first_sample(a, w):
                smp = Sample(-1, 1)
                for j in a.first:
                    job(a, j, w, smp)
                for i in range(a.jobs):
                    query_major(a, 0, i, smp)
                    if i in a.mod_after:
                        modulation(int(a.name[1]), *MOD_REST[a.mod_after.index(i)])
                for j in a.second:
                    job(a, j, w, smp)

            def attention_turn(a, w, smp, nxt):
                for step in range(a.steps):
                    lag = 0
                    if step + 1 < a.steps:
                        after_step, after_smp = step + 1, smp
                    else:
                        after_step, after_smp, lag = 0, nxt, a.lag
                    for i in range(a.jobs + lag):
                        if i < a.jobs:
                            key_major(a, step, i, smp)
                        if after_smp and i >= lag:
                            query_major(a, after_step, i - lag, after_smp)
                        if i % 4 == 3 and 4 < i < a.jobs:
                            value_product(a, step, i // 4 - 1, smp)
                        if lag and i == a.jobs:
                            value_product(a, step, a.jobs // 4 - 1, smp)
                    if not lag:
                        value_product(a, step, a.jobs // 4 - 1, smp)
                    for j in a.after[step]:
                        if j[-1] != "'":
                            job(a, j, w, smp)
                        elif nxt:
                            job(a, j[:-1], w, nxt)

            def attention_loop(a, w):
                loop(pe, lambda smp, nxt: attention_turn(a, w, smp, nxt))

            def feed(phase):
                def first(nxt):
                    for c in range(CH):
                        turned(phase, c, nxt)

                def wide_product(dst, q, i, stop):
                    w_high_, w_low_ = parts[i]
                    tokens = slice(q * P, (q + 1) * P)
                    for c in range(CH):
                        pe.matmul(dst, hTR[:, c, tokens], w_high_[:, c, :], start=(c == 0), stop=False)
                        pe.matmul(dst, hTR[:, c, tokens], w_low_[:, c, :], start=False, stop=False)
                        mm = pe.matmul(dst, hTL[:, c, tokens], w_high_[:, c, :], start=False, stop=(stop and c == CH - 1))
                    return mm

                def turn(smp, nxt):
                    for bank in ("G0", "G1"):
                        pe.wait_ge(read[bank], turn_start(phase, bank, smp))
                    pe.wait_ge(read["V0"], before(phase, "V0", "ar", smp))
                    for q in range(TT):
                        if phase == "f0":
                            dst, w = VV[:, q // 2, (q % 2) * (E * R + NMAP):(q % 2 + 1) * (E * R + NMAP)], war
                        else:
                            dst, w = VV[:, 0, q * E * R:(q + 1) * E * R], wA1
                        for c in range(CH):
                            mm = pe.matmul(dst, hT[:, c, q * P:(q + 1) * P], w[:, c, :], start=(c == 0), stop=(c == CH - 1))
                    mm.then_inc(ph[phase]["ar"], 1)
                    pe.wait_ge(w_high, made_parts[phase])
                    pe.wait_ge(w_low, made_parts[phase])
                    wait_alone(pe, ph[phase]["low"], smp.count(CH, CH))
                    if phase == "f1":
                        for q in range(TT):
                            bank = g_bank(phase, f"s{q}")
                            pe.wait_ge(read[bank], before(phase, bank, f"s{q}", smp))
                            wide_product(ps[bank][:, :], q, 1, True).then_inc(full[bank], 1)
                    for q in range(TT):
                        pe.wait_ge(read[XB[q]], before(phase, XB[q], "y", smp))
                        wide_product(ps[XB[q]][:, :], q, 0, False)
                    bank = g_bank(phase, "w")
                    pe.wait_ge(read["V0"], before(phase, "V0", "ar", smp) + 1)
                    pe.wait_ge(read[bank], before(phase, bank, "w", smp))
                    for q in range(TT):
                        mm = pe.transpose(ps[bank][:, q * P:(q + 1) * P], hw[:, q, :], ident[:, :])
                    mm.then_inc(full[bank], 1)
                    if nxt:
                        first(nxt)
                    wait_alone(pe, read[bank], before(phase, bank, "w", smp) + 1)
                    for q in range(TT):
                        pe.matmul(ps[XB[q]][:, :], hwT[:, q, :], wB[:, :], start=False, stop=True).then_inc(full[XB[q]], 1)

                first(Sample(-1, 1))
                loop(pe, turn)

            pe.wait_ge(s_silu, 3)
            pe.wait_ge(s_const, 5)
            for kind, n in MOD_FIRST:
                modulation(0, kind, n)
            pe.wait_ge(ld["l0"], 16 * 6)
            pe.wait_ge(s_vfill, 2)
            w0 = {"q": wqk0, "v": wv0, "o": wo0}
            first_sample(A0, w0)
            attention_loop(A0, w0)
            pe.wait_ge(ld["l0f"], 16 * 6)
            for kind, n in MOD_FIRST:
                modulation(1, kind, n)
            feed("f0")
            pe.wait_ge(s_vfill, 4)
            w1 = {"k": wk1, "v": wv1, "q": wq1, "o": wo1}
            pe.wait_ge(ld["l1"], 16 * 3)
            first_sample(A1, w1)
            attention_loop(A1, w1)
            pe.wait_ge(ld["l1f"], 16 * 5)
            feed("f1")


def kernel(**inputs):
    import numpy as np
    import concourse.bacc as bacc
    from concourse import mybir as mb
    from concourse.bass_utils import run_bass_kernel_spmd

    g = {k: np.asarray(v) for k, v in inputs.items()}
    kv, rep, hd = A1.kv, A1.rep, A1.hd
    wqk = g["L0_attn_Wqk_w"].reshape(64, 2, D).transpose(1, 0, 2).reshape(128, D)
    bqk = g["L0_attn_Wqk_b"].reshape(64, 2).T.reshape(128)
    wq = g["L1_attn_wq"].reshape(D, A1.steps, A1.khs, rep, hd).transpose(0, 1, 2, 4, 3).reshape(D, kv * rep * hd)
    wk = g["L1_attn_wk"].reshape(D, 2, 2, A1.khs, hd).transpose(0, 1, 3, 4, 2).reshape(D, kv * hd)
    data = {
        "x": g["L0_attn_x"],
        "c0": g["L0_c"].T, "c1": g["L1_c"].T, "wmod0": g["L0_wmod"], "wmod1": g["L1_wmod"],
        "wqk0": wqk.T, "bqk0": bqk, "wv0": g["L0_attn_Wv_w"].T, "bv0": g["L0_attn_Wv_b"],
        "wo0": g["L0_attn_Wo_w"].T, "bo0": g["L0_attn_Wo_b"],
        "wbase": g["L0_ffn_base_W"].T, "bbase": g["L0_ffn_base_b"],
        "war": np.concatenate([g["L0_ffn_A"].reshape(E * R, D).T, g["L0_ffn_router_W"].T], axis=1),
        "brout": g["L0_ffn_router_b"],
        "wB0": g["L0_ffn_B"].transpose(0, 2, 1).reshape(E * R, D),
        "emap": g["L0_ffn_expert_map"],
        "wq1": wq, "wk1": wk, "wv1": g["L1_attn_wv"], "wo1": g["L1_attn_wo"],
        "wW1": g["L1_ffn_W"].T, "b1": g["L1_ffn_b"],
        "wQK1": np.concatenate([g["L1_ffn_Wq"].T, g["L1_ffn_Wk"].T], axis=1),
        "wA1": g["L1_ffn_A"].reshape(E * R, D).T,
        "wB1": g["L1_ffn_Bm"].transpose(0, 2, 1).reshape(E * R, D),
    }
    nc = bacc.Bacc("TRN2", target_bir_lowering=False, num_devices=1)
    arrays, t = {}, {}
    for name, a in data.items():
        a = np.ascontiguousarray(a)
        arrays[f"in_{name}"] = a
        t[name] = nc.dram_tensor(f"in_{name}", a.shape, mb.dt.from_np(a.dtype), kind="ExternalInput").ap()
    t["out"] = nc.dram_tensor("out", (NB, N, D), F32, kind="ExternalOutput").ap()
    build(nc, t)
    r = run_bass_kernel_spmd(nc, [arrays], core_ids=[0])
    return r.results[0]["out"]
```
